# Optimizing a Trainium2 kernel written in Bass

```python
import numpy as np
import jax
import jax.numpy as jnp

def _softmax(x, axis=-1):
    return jax.nn.softmax(x, axis=axis)

def _gelu(x):
    return jax.nn.gelu(x, approximate=True)

def _silu(x):
    return jax.nn.silu(x)

def _sigmoid(x):
    return jax.nn.sigmoid(x)

def _layernorm(x, axis=-1, eps=1e-05):
    m = jnp.mean(x, axis=axis, keepdims=True)
    v = jnp.var(x, axis=axis, keepdims=True)
    return (x - m) / jnp.sqrt(v + eps)

def _scatter_add(tgt, idx, src, axis=0):
    return tgt.at[idx].add(src)

def _segment_sum(src, seg, n):
    return jax.ops.segment_sum(src, seg, n)
kernel_name = 'mk_gnn_preln_d4_gnn_r32_f223b6'

def setup_inputs(seed: int=0):
    np.random.seed(seed)
    _w = jnp.asarray

    def _rec_inputs():
        import jax
        import jax.numpy as jnp
        _gk = jax.random.key(seed)
        x = -0.0005121 + 1.001 * jax.random.normal(jax.random.fold_in(_gk, 1), (50000, 64), jnp.float32)
        src = jax.random.randint(jax.random.fold_in(_gk, 2), (50000,), 0, 50000, jnp.int32)
        dst = jax.random.randint(jax.random.fold_in(_gk, 3), (50000,), 0, 50000, jnp.int32)
        _o = jnp.argsort(dst, stable=True)
        src = src[_o]
        dst = dst[_o]
        edge_attr_10 = jax.random.uniform(jax.random.fold_in(_gk, 12), (50000, 10), jnp.float32, 0.0, 1)
        edge_attr_32 = 0.000196303 + 1.00016 * jax.random.normal(jax.random.fold_in(_gk, 13), (50000, 32), jnp.float32)
        edge_type_16 = jax.random.randint(jax.random.fold_in(_gk, 15), (50000,), 0, 16, jnp.int32)
        return (x, src, dst, edge_attr_10, edge_attr_32, edge_type_16)
    x, src, dst, edge_attr_10, edge_attr_32, edge_type_16 = _rec_inputs()

    def _L0_gnn_setup():
        import jax, jax.numpy as jnp
        import numpy as np
        N = 50000
        E = 25000
        D_IN = 64
        D_OUT = 64
        EDGE_DIM = 32
        BN_EPS = 1e-05
        GIN_EPS = 0.0
        key = jax.random.key(seed)
        ks = jax.random.split(key, 10)
        x = jax.random.normal(ks[0], (N, D_IN), dtype=jnp.float32)
        edge_index = jax.random.randint(ks[1], (2, E), 0, N, dtype=jnp.int64)
        edge_attr = jax.random.normal(ks[2], (E, EDGE_DIM), dtype=jnp.float32)
        W_edge = jax.random.normal(ks[3], (EDGE_DIM, D_IN), dtype=jnp.float32) / np.sqrt(EDGE_DIM)
        b_edge = jnp.zeros((D_IN,), dtype=jnp.float32)
        W1 = jax.random.normal(ks[4], (D_IN, D_OUT), dtype=jnp.float32) / np.sqrt(D_IN)
        b1 = jnp.zeros((D_OUT,), dtype=jnp.float32)
        gamma = jnp.ones((D_OUT,), dtype=jnp.float32)
        beta = jnp.zeros((D_OUT,), dtype=jnp.float32)
        W2 = jax.random.normal(ks[5], (D_OUT, D_OUT), dtype=jnp.float32) / np.sqrt(D_OUT)
        b2 = jnp.zeros((D_OUT,), dtype=jnp.float32)
        return {'x': x, 'edge_index': edge_index, 'edge_attr': edge_attr, 'W_edge': W_edge, 'b_edge': b_edge, 'W1': W1, 'b1': b1, 'gamma': gamma, 'beta': beta, 'W2': W2, 'b2': b2}
    _L0_gnn_all = _L0_gnn_setup()
    _L0_gnn_in = {k: v for k, v in _L0_gnn_all.items() if k in ('W_edge', 'b_edge', 'W1', 'b1', 'gamma', 'beta', 'W2', 'b2')}
    del _L0_gnn_all

    def _L1_gnn_setup():
        import jax, jax.numpy as jnp
        import numpy as np
        N_NODES = 50000
        N_EDGES = 25000
        IN_FEATS = 64
        DIST_DIM = 10
        key = jax.random.key(seed)
        ks = jax.random.split(key, 8)
        feature = jax.random.normal(ks[0], (N_NODES, IN_FEATS), dtype=jnp.float32)
        dist = jax.random.uniform(ks[1], (N_EDGES, DIST_DIM), dtype=jnp.float32)
        src = jax.random.randint(ks[2], (N_EDGES,), 0, N_NODES, dtype=jnp.int64)
        dst = jax.random.randint(ks[3], (N_EDGES,), 0, N_NODES, dtype=jnp.int64)
        fan_in = 2 * IN_FEATS + DIST_DIM
        scale = 1.0 / np.sqrt(fan_in)
        Wf = jax.random.normal(ks[4], (fan_in, IN_FEATS), dtype=jnp.float32) * scale
        bf = jax.random.normal(ks[5], (IN_FEATS,), dtype=jnp.float32) * scale
        Ws = jax.random.normal(ks[6], (fan_in, IN_FEATS), dtype=jnp.float32) * scale
        bs = jax.random.normal(ks[7], (IN_FEATS,), dtype=jnp.float32) * scale
        return {'feature': feature, 'dist': dist, 'src': src, 'dst': dst, 'Wf': Wf, 'bf': bf, 'Ws': Ws, 'bs': bs}
    _L1_gnn_all = _L1_gnn_setup()
    _L1_gnn_in = {k: v for k, v in _L1_gnn_all.items() if k in ('Wf', 'bf', 'Ws', 'bs')}
    del _L1_gnn_all

    def _L2_gnn_setup():
        import jax, jax.numpy as jnp
        import numpy as np
        N_NODES = 50000
        N_EDGES = 25000
        D_IN = 64
        D_OUT = 64
        NUM_RELS = 16
        key = jax.random.key(seed)
        k1, k2, k3, k4, k5 = jax.random.split(key, 5)
        feat = jax.random.normal(k1, (N_NODES, D_IN), dtype=jnp.float32)
        weight = jax.random.normal(k2, (NUM_RELS, D_IN, D_OUT), dtype=jnp.float32) * 0.05
        src = jax.random.randint(k3, (N_EDGES,), 0, N_NODES, dtype=jnp.int32)
        dst = jax.random.randint(k4, (N_EDGES,), 0, N_NODES, dtype=jnp.int32)
        etypes = jax.random.randint(k5, (N_EDGES,), 0, NUM_RELS, dtype=jnp.int32)
        return {'feat': feat, 'weight': weight, 'src': src, 'dst': dst, 'etypes': etypes}
    _L2_gnn_all = _L2_gnn_setup()
    _L2_gnn_in = {k: v for k, v in _L2_gnn_all.items() if k in ('weight',)}
    del _L2_gnn_all

    def _L3_gnn_setup():
        import jax, jax.numpy as jnp
        import numpy as np
        N = 3125
        E = 50000
        C = 64
        L = 3

        def _gcn_layer(x, W, b, src, dst, dinv):
            h = x @ W
            coef = dinv[src] * dinv[dst]
            agg = jax.ops.segment_sum(h[src] * coef[:, None], dst, num_segments=x.shape[0])
            return agg + h * (dinv * dinv)[:, None] + b
        key = jax.random.key(seed)
        k1, k2, k3 = jax.random.split(key, 3)
        x = jax.random.normal(k1, (N, C), dtype=jnp.float32)
        Ws = jax.random.normal(k2, (L, C, 2 * C), dtype=jnp.float32) / np.sqrt(C)
        bs = jnp.zeros((L, 2 * C), dtype=jnp.float32)
        edge_index = jax.random.randint(k3, (2, E), 0, N, dtype=jnp.int64)
        return {'x': x, 'Ws': Ws, 'bs': bs, 'edge_index': edge_index}
    _L3_gnn_all = _L3_gnn_setup()
    _L3_gnn_in = {k: v for k, v in _L3_gnn_all.items() if k in ('Ws', 'bs')}
    del _L3_gnn_all
    return {'x': x, 'src': src, 'dst': dst, 'edge_attr_10': edge_attr_10, 'edge_attr_32': edge_attr_32, 'edge_type_16': edge_type_16, 'L0_gnn_W_edge': _L0_gnn_in['W_edge'], 'L0_gnn_b_edge': _L0_gnn_in['b_edge'], 'L0_gnn_W1': _L0_gnn_in['W1'], 'L0_gnn_b1': _L0_gnn_in['b1'], 'L0_gnn_gamma': _L0_gnn_in['gamma'], 'L0_gnn_beta': _L0_gnn_in['beta'], 'L0_gnn_W2': _L0_gnn_in['W2'], 'L0_gnn_b2': _L0_gnn_in['b2'], 'L1_gnn_Wf': _L1_gnn_in['Wf'], 'L1_gnn_bf': _L1_gnn_in['bf'], 'L1_gnn_Ws': _L1_gnn_in['Ws'], 'L1_gnn_bs': _L1_gnn_in['bs'], 'L2_gnn_weight': _L2_gnn_in['weight'], 'L3_gnn_Ws': _L3_gnn_in['Ws'], 'L3_gnn_bs': _L3_gnn_in['bs']}

def reference(x, src, dst, edge_attr_10, edge_attr_32, edge_type_16, L0_gnn_W_edge, L0_gnn_b_edge, L0_gnn_W1, L0_gnn_b1, L0_gnn_gamma, L0_gnn_beta, L0_gnn_W2, L0_gnn_b2, L1_gnn_Wf, L1_gnn_bf, L1_gnn_Ws, L1_gnn_bs, L2_gnn_weight, L3_gnn_Ws, L3_gnn_bs):
    import jax
    import jax.numpy as jnp

    def _L0_gnn_ref(x, edge_index, edge_attr, W_edge, b_edge, W1, b1, gamma, beta, W2, b2):
        import jax, jax.numpy as jnp
        import numpy as np
        N = 50000
        E = 25000
        D_IN = 64
        D_OUT = 64
        EDGE_DIM = 32
        BN_EPS = 1e-05
        GIN_EPS = 0.0
        src = edge_index[0]
        dst = edge_index[1]
        msg = jax.nn.relu(x[src] + edge_attr @ W_edge + b_edge)
        agg = jax.ops.segment_sum(msg, dst, num_segments=N)
        h = (1.0 + GIN_EPS) * x + agg
        h1 = h @ W1 + b1
        mean = jnp.mean(h1, axis=0)
        var = jnp.var(h1, axis=0)
        h1 = (h1 - mean) * jax.lax.rsqrt(var + BN_EPS) * gamma + beta
        h1 = jax.nn.relu(h1)
        out = h1 @ W2 + b2
        return out + x

    def _L1_gnn_ref(feature, dist, src, dst, Wf, bf, Ws, bs):
        import jax, jax.numpy as jnp
        import numpy as np
        N_NODES = 50000
        N_EDGES = 25000
        IN_FEATS = 64
        DIST_DIM = 10
        msg = jnp.concatenate([feature[src], feature[dst], dist], axis=-1)
        gated = jax.nn.sigmoid(msg @ Wf + bf) * jax.nn.softplus(msg @ Ws + bs)
        m_sum = jax.ops.segment_sum(gated, dst, num_segments=feature.shape[0])
        return feature + m_sum

    def _L2_gnn_ref(feat, weight, src, dst, etypes):
        import jax, jax.numpy as jnp
        import numpy as np
        N_NODES = 50000
        N_EDGES = 25000
        D_IN = 64
        D_OUT = 64
        NUM_RELS = 16
        num_rels = weight.shape[0]
        h_src = feat[src]
        msg = jnp.zeros((h_src.shape[0], weight.shape[2]), dtype=feat.dtype)
        for r in range(num_rels):
            mask = etypes == r
            msg = msg + h_src * mask[:, None].astype(feat.dtype) @ weight[r]
        out = jax.ops.segment_sum(msg, dst, num_segments=feat.shape[0])
        return out

    def _L3_gnn_ref(x, Ws, bs, edge_index):
        import jax, jax.numpy as jnp
        import numpy as np
        N = 3125
        E = 50000
        C = 64
        L = 3

        def _gcn_layer(x, W, b, src, dst, dinv):
            h = x @ W
            coef = dinv[src] * dinv[dst]
            agg = jax.ops.segment_sum(h[src] * coef[:, None], dst, num_segments=x.shape[0])
            return agg + h * (dinv * dinv)[:, None] + b
        src, dst = (edge_index[0], edge_index[1])
        n = x.shape[0]
        deg = jnp.zeros((n,), x.dtype).at[dst].add(jnp.asarray(1.0, x.dtype)) + 1.0
        dinv = jax.lax.rsqrt(deg)
        for l in range(Ws.shape[0]):
            residual = x
            h = _gcn_layer(x, Ws[l], bs[l], src, dst, dinv)
            a, g = jnp.split(h, 2, axis=-1)
            x = a * jax.nn.sigmoid(g) + residual
        return x
    edge_index = jnp.stack([src, dst])
    h = jnp.maximum(_layernorm(x, axis=-1), 0.0)
    x = x + _L0_gnn_ref(h, edge_index, edge_attr_32, L0_gnn_W_edge, L0_gnn_b_edge, L0_gnn_W1, L0_gnn_b1, L0_gnn_gamma, L0_gnn_beta, L0_gnn_W2, L0_gnn_b2)
    h = jnp.maximum(_layernorm(x, axis=-1), 0.0)
    x = x + _L1_gnn_ref(h, edge_attr_10, src, dst, L1_gnn_Wf, L1_gnn_bf, L1_gnn_Ws, L1_gnn_bs)
    h = jnp.maximum(_layernorm(x, axis=-1), 0.0)
    x = x + _L2_gnn_ref(h, L2_gnn_weight, src, dst, edge_type_16)
    h = jnp.maximum(_layernorm(x, axis=-1), 0.0)
    x = x + _L3_gnn_ref(h, L3_gnn_Ws, L3_gnn_bs, edge_index)
    return x

_drawn_inputs = setup_inputs


def setup_inputs(seed=0):
    import zlib

    import numpy as np

    out = dict(_drawn_inputs(seed))
    spreads = {'L0_gnn_b_edge': (0.0, 0.323),
     'L0_gnn_b1': (0.0, 0.8),
     'L0_gnn_gamma': (1.0, 0.2),
     'L0_gnn_beta': (0.0, 0.1),
     'L0_gnn_b2': (0.0, 0.1),
     'L3_gnn_bs': (0.0, 0.277)}
    factors = {'edge_attr_10': 6.126, 'L1_gnn_bf': 5.838, 'L1_gnn_bs': 4.588}
    for name, (base, spread) in spreads.items():
        noise = np.random.default_rng([zlib.crc32(name.encode()), seed]).standard_normal(out[name].shape)
        drawn = base * np.exp(spread * noise) if base else spread * noise
        out[name] = jnp.asarray(drawn.astype(out[name].dtype))
    for name, factor in factors.items():
        out[name] = (out[name] * factor).astype(out[name].dtype)
    return out
```

```python
from contextlib import ExitStack

import concourse.bass as bass
from concourse import mybir

F32 = mybir.dt.float32
I32 = mybir.dt.int32
ALU = mybir.AluOpType
ACT = mybir.ActivationFunctionType
AX = mybir.AxisListType

P = 128
D = 64
N = 50000
E = 50000
SB = 7
STEPS = 28
T = SB * 2 * STEPS
NP = T * P
FULL = N // P
REST = N - FULL * P
BANK = 4
W = 2 * P
GB = 14
GSTEPS = T // (2 * GB)
GC = GB * D
LN_EPS = 1e-5
BN_EPS = 1e-5
RELS = 16
EA = 32
EB = 10
LAYERS = 3
WHY = "the table is clamped to the node blocks where it is made"


class Links:

    def __init__(self, eng, sem, per_step):
        self.eng, self.sem, self.per_step, self.at = eng, sem, per_step, 0

    def step(self, i):
        self.i, self.at = i, 0

    def link(self, ins):
        self.at += 1
        ins.then_inc(self.sem, 1)
        self.eng.wait_ge(self.sem, self.i * self.per_step + self.at)

    def done(self):
        assert self.at == self.per_step, (self.at, self.per_step)


def peel_first(eng, n, body):
    body(0, True)
    with eng.Fori(1, n) as i:
        body(i, False)


def tiles_of(dram, first, count):
    return dram[bass.ds(first * P, count * P), :].rearrange("(k p) f -> p k f", p=P)


def load_regs(nc, eng_type, ap, top):
    _, values = nc.values_load_multi_w_load_instructions(
        ap, engines=[eng_type], min_val=0, max_val=top, skip_runtime_bounds_check_because=WHY)
    return values


def build(nc, x, src, dst, ea10, ea32, et, W_edge, b_edge, W1, b1, gamma, beta, W2, b2,
          Wf, bf, Ws, bs, W_rel, W_gcn, b_gcn, out):
    with ExitStack() as whole:
        def scratch(name, shape, dt=F32):
            return nc.dram_tensor(name, shape, dt, kind="Internal").ap()

        h_tab = scratch("h_tab", (NP, D))
        z_tab = scratch("z_tab", (NP, D))
        xh_tab = scratch("xh_tab", (NP, D))
        ea10_s = scratch("ea10_s", (NP, EB))
        ea32_s = scratch("ea32_s", (NP, EA))
        et_s = scratch("et_s", (1, NP), I32)

        def keep(name, shape, dt=F32):
            return whole.enter_context(nc.sbuf_tensor(name, shape, dt))

        agg = keep("agg", [P, T * D])
        src_idx = keep("src_idx", [P, T], I32)
        dst_idx = keep("dst_idx", [P, T], I32)
        dst_rel = keep("dst_rel", [P, T])
        win = keep("win", [1, 2 * STEPS * 8], I32)
        win_b = keep("win_b", [1, 2 * STEPS * 8], I32)
        iota_w = keep("iota_w", [P, W])
        ident = keep("ident", [P, P])
        ones = keep("ones", [P, P])
        deg = keep("deg", [P, T])
        dinv = keep("dinv", [P, T])
        eps_col = keep("eps_col", [P, 1])

        prologue(nc, src, dst, et, ea10, ea32, ea10_s, ea32_s, et_s, src_idx, dst_idx, dst_rel, win,
                 win_b, iota_w, ident, ones, deg, eps_col)
        first_norm(nc, x, agg, h_tab, xh_tab, eps_col)
        gin_edges(nc, h_tab, ea32_s, W_edge, b_edge, agg, src_idx, dst_rel, win, iota_w, ident)
        gin_nodes(nc, agg, xh_tab, h_tab, W1, b1, gamma, beta, W2, b2, ident, ones, eps_col)
        gated_edges(nc, h_tab, ea10_s, Wf, bf, Ws, bs, agg, deg, src_idx, dst_idx, dst_rel, win, win_b,
                    iota_w, ident, ones)
        norm_nodes(nc, agg, h_tab, eps_col)
        rel_edges(nc, h_tab, et_s, W_rel, agg, src_idx, dst_rel, win, iota_w, ident)
        gcn_start(nc, agg, deg, dinv, h_tab, z_tab, xh_tab, eps_col)
        for layer in range(LAYERS):
            gcn_edges(nc, layer, h_tab, agg, src_idx, dst_rel, win, iota_w)
            gcn_nodes(nc, layer, agg, dinv, h_tab, z_tab, xh_tab, W_gcn, b_gcn, ident, ones, out)


def prologue(nc, src, dst, et, ea10, ea32, ea10_s, ea32_s, et_s, src_idx, dst_idx, dst_rel, win,
             win_b, iota_w, ident, ones, deg, eps_col):
    C = -(-T // P)
    lasts = T - (C - 1) * P
    with ExitStack() as ctx:
        ctx.enter_context(nc.cleanup_on_exit())
        def sb(name, shape, dt=F32):
            return ctx.enter_context(nc.sbuf_tensor(name, shape, dt))

        def sem(name):
            return nc.alloc_semaphore(name)

        srow = sb("p_srow", [P, C, P], I32)
        drow = sb("p_drow", [P, C, P], I32)
        srowf = sb("p_srowf", [P, C, P])
        drowf = sb("p_drowf", [P, C, P])
        drelf = sb("p_drelf", [P, C, P])
        lo_i = sb("p_lo_i", [P, C, 2], I32)
        lo_f = sb("p_lo_f", [P, C, 2])
        cols = sb("p_cols", [P, C, 3])
        base = sb("p_base", [P, C])
        rows = sb("p_rows", [1, 3, C * P])
        zero = sb("p_zero", [P, EA * 2])
        zero_i = sb("p_zero_i", [1, NP - E], I32)
        ps = [ctx.enter_context(nc.psum_tensor(f"p_ps{k}", [P, C, P], F32)) for k in range(3)]
        ps_r = [ctx.enter_context(nc.psum_tensor(f"p_psr{k}", [P, C, P], F32)) for k in range(3)]
        padded, loaded, consts, made, turned, copied, chain, zeroed, pooled = (
            sem("p_" + s) for s in ("padded", "loaded", "consts", "made", "turned", "copied", "chain",
                                    "zeroed", "pooled"))
        block = ctx.enter_context(nc.Block())
        pad_rows = NP - E

        @block.sync
        def _(sp):
            sp.dma_start(ea32_s[0:E, :].rearrange("(a b) f -> a (b f)", a=400),
                         ea32.rearrange("(a b) f -> a (b f)", a=400)).then_inc(copied, 16)
            sp.dma_start(ea10_s[0:E, :].rearrange("(a b) f -> a (b f)", a=400),
                         ea10.rearrange("(a b) f -> a (b f)", a=400)).then_inc(copied, 16)
            sp.dma_start(et_s[0:1, 0:E].rearrange("o (a b) -> (o a) b", a=400),
                         et.rearrange("(a b) -> a b", a=400)).then_inc(copied, 16)
            sp.wait_ge(zeroed, 2)
            sp.dma_start(ea32_s[E:NP, :].rearrange("(a b) f -> a (b f)", b=2),
                         zero[0:pad_rows // 2, 0:2 * EA]).then_inc(copied, 16)
            sp.dma_start(ea10_s[E:NP, :].rearrange("(a b) f -> a (b f)", b=2),
                         zero[0:pad_rows // 2, 0:2 * EB]).then_inc(copied, 16)
            sp.dma_start(et_s[0:1, E:NP], zero_i[:, :]).then_inc(copied, 16)
            sp.wait_ge(copied, 16 * 6)

        @block.scalar
        def _(act):
            act.wait_ge(padded, 2)
            for row, dram in ((srow, src), (drow, dst)):
                full = (C - 1) * P
                act.dma_start(row[:, 0:C - 1, :],
                              dram[0:full * P].rearrange("(c t p) -> t c p", t=P, p=P)).then_inc(loaded, 16)
                act.dma_start(row[0:FULL - full, C - 1, :],
                              dram[full * P:FULL * P].rearrange("(t p) -> t p", p=P)).then_inc(loaded, 16)
                act.dma_start(row[FULL - full:FULL - full + 1, C - 1, 0:REST],
                              dram[FULL * P:E].rearrange("(o p) -> o p", o=1)).then_inc(loaded, 16)

        @block.gpsimd
        def _(pool):
            nc.gpsimd.memset(ident[:, :], 0.0).then_inc(pooled, 1)
            nc.gpsimd.iota(iota_w[:, :], [[1, W]], base=0, channel_multiplier=0,
                           allow_small_or_imprecise_dtypes=True).then_inc(pooled, 1)
            pool.wait_ge(pooled, 2)
            nc.gpsimd.affine_select(out=ident[:, :], in_=ident[:, :], compare_op=ALU.not_equal, fill=1.0,
                                    base=0, pattern=[[-1, P]], channel_multiplier=1).then_inc(consts, 1)
            nc.gpsimd.memset(ones[:, :], 1.0)
            nc.gpsimd.memset(deg[:, :], 0.0)
            nc.gpsimd.memset(eps_col[:, :], LN_EPS).then_inc(pooled, 1)
            pool.wait_ge(pooled, 3)

        @block.vector
        def _(dve):
            c = Links(dve, chain, 0)
            c.step(0)
            nc.vector.memset(srow[:, :, :], 0).then_inc(padded, 1)
            nc.vector.memset(drow[:, :, :], -1).then_inc(padded, 1)
            nc.vector.memset(zero[:, :], 0.0).then_inc(zeroed, 1)
            nc.vector.memset(zero_i[:, :], 0).then_inc(zeroed, 1)
            dve.wait_ge(loaded, 16 * 6)
            nc.vector.tensor_copy(srowf[:, :, :], srow[:, :, :]).then_inc(made, 1)
            c.link(nc.vector.tensor_copy(drowf[:, :, :], drow[:, :, :]))
            c.link(nc.vector.tensor_copy(lo_i[:, :, 0], drow[:, :, 0]))
            c.link(nc.vector.tensor_reduce(lo_i[:, :, 1], drowf[:, :, :], AX.X, ALU.max))
            c.link(nc.vector.tensor_scalar(lo_i[:, :, :], lo_i[:, :, :], 7, None, ALU.arith_shift_right))
            c.link(nc.vector.tensor_copy(lo_f[:, :, :], lo_i[:, :, :]))
            c.link(nc.vector.tensor_scalar(cols[:, :, 2], lo_f[:, :, 0], 0.0, None, ALU.max))
            c.link(nc.vector.tensor_scalar(cols[:, :, 0], cols[:, :, 2], float(D), None, ALU.mult))
            c.link(nc.vector.tensor_scalar(base[:, :], cols[:, :, 2], float(P), None, ALU.mult))
            c.link(nc.vector.tensor_tensor(cols[:, :, 1], lo_f[:, :, 1], cols[:, :, 2], ALU.subtract))
            c.link(nc.vector.tensor_scalar(cols[:, :, 1], cols[:, :, 1], -1.0, 0.0, ALU.add, ALU.max))
            for k in range(C):
                last = nc.vector.tensor_scalar(drelf[:, k, :], drowf[:, k, :], base[:, k:k + 1], None,
                                               ALU.subtract)
            last.then_inc(made, 1)
            dve.wait_ge(turned, 1)
            nc.vector.tensor_copy(src_idx[:, :], ps[0][:, :, :].rearrange("p c t -> p (c t)")[:, 0:T])
            nc.vector.tensor_scalar(dst_idx[:, :], ps[1][:, :, :].rearrange("p c t -> p (c t)")[:, 0:T],
                                    0.0, None, ALU.max)
            nc.vector.tensor_copy(dst_rel[:, :], ps[2][:, :, :].rearrange("p c t -> p (c t)")[:, 0:T])
            for k in range(3):
                last = nc.vector.tensor_copy(rows[:, k, :], ps_r[k][0:1, :, :].rearrange("p c t -> p (c t)"))
            c.link(last)
            halves = [rows[:, k, 0:T].rearrange("p (n j) -> p n j", j=SB) for k in range(3)]
            w8 = win[:, :].rearrange("p (n j) -> p n j", j=8)
            wb8 = win_b[:, :].rearrange("p (n j) -> p n j", j=8)
            nc.vector.tensor_copy(w8[:, :, 0:SB], halves[0])
            c.link(nc.vector.tensor_reduce(w8[:, :, SB], halves[1], AX.X, ALU.max))
            nc.vector.tensor_copy(wb8[:, :, 0:SB], halves[2])
            c.link(nc.vector.tensor_copy(wb8[:, :, SB], w8[:, :, SB]))

        @block.tensor
        def _(pe):
            pe.wait_ge(consts, 1)
            pe.wait_ge(made, 2)
            pe.wait_ge(chain, 10)
            for k in range(C):
                for to, frm in zip(ps, (srowf, drowf, drelf)):
                    nc.tensor.transpose(to[:, k, :], frm[:, k, :], ident[:, :])
                for q in range(3):
                    last = nc.tensor.transpose(ps_r[q][0:1, k, :], cols[:, k, q:q + 1], ident[:, :])
            last.then_inc(turned, 1)


def gather_pass(nc, pool, tag, tables, idx_small, ring, wait_used, landed, idx_ready):
    halves = pool.alloc_register(f"{tag}_halves")
    pool.reg_mov(halves, 1)

    def body(i, first):
        for h in range(2):
            if not first:
                wait_used(i, h)
            for s, (_, index, _) in enumerate(tables):
                last = nc.gpsimd.tensor_copy(idx_small[:, s, h, :],
                                             index[:, bass.ds((2 * i + h) * SB, SB)])
            last.then_inc(idx_ready, 1)
            pool.wait_ge(idx_ready, pool.snap(halves))
            pool.reg_add(halves, halves, 1)
            for j in range(SB):
                for s, (dram, _, slot) in enumerate(tables):
                    pool.indirect_dma_start(
                        out=ring(h, j, slot), out_offset=None, in_=dram[:, :],
                        in_offset=bass.IndirectOffsetOnAxis(ap=idx_small[:, s, h, j:j + 1], axis=0),
                    ).then_inc(landed[h], 16)
    peel_first(pool, STEPS, body)


class Sums:

    def __init__(self, nc, ctx, tag, agg, dst_rel, win, iota_w, deg=None, win_b=None, ones=None):
        def sem(name):
            return nc.alloc_semaphore(f"{tag}_{name}")
        self.nc, self.tag, self.agg, self.dst_rel, self.win, self.iota_w = nc, tag, agg, dst_rel, win, iota_w
        self.deg, self.win_b, self.ones = deg, win_b, ones
        self.S = ctx.enter_context(nc.sbuf_tensor(f"{tag}_S", [P, SB, W], F32))
        self.Sx = ctx.enter_context(nc.sbuf_tensor(f"{tag}_Sx", [P, P], F32))
        self.relx = ctx.enter_context(nc.sbuf_tensor(f"{tag}_relx", [P, SB], F32))
        self.ps = ctx.enter_context(nc.psum_tensor(f"{tag}_ps_sum", [P, 8, 2, D], F32))
        self.ps_x = ctx.enter_context(nc.psum_tensor(f"{tag}_ps_x", [P, 512], F32))
        self.count = {}
        self.member_ready = sem("member_ready")
        self.summed = sem("summed")
        self.added = sem("added")
        self.x_ready = sem("x_ready")
        self.x_summed = sem("x_summed")
        self.x_chain = sem("x_chain")
        self.tick = ctx.enter_context(nc.sbuf_tensor(f"{tag}_tick", [1, 1], F32))
        self.counted = sem("counted")

    def start(self, eng, name):
        self.count[name] = eng.alloc_register(f"{self.tag}_{name}")
        eng.reg_mov(self.count[name], 1)

    def wait_next(self, eng, sem, name):
        r = self.count[name]
        eng.wait_ge(sem, eng.snap(r))
        eng.reg_add(r, r, 1)

    def within(self, dve, at, top):
        r = self.count["place"]
        dve.reg_alu(r, at, top, op=ALU.min)
        return dve.snap(r, min_val=0, max_val=top)

    def vector_members(self, dve, i, h):
        n = 2 * i + h
        for j in range(SB):
            self.nc.vector.tensor_scalar(self.S[:, j, :], self.iota_w[:, :],
                                         self.dst_rel[:, bass.ds(n * SB + j, 1)], None,
                                         ALU.is_equal).then_inc(self.member_ready, 1)

    def tensor_sum(self, pe, i, h, msg):
        nc, n = self.nc, 2 * i + h
        for j in range(SB):
            pe.wait_ge(self.member_ready, n * SB + j + 1)
            for w in range(2):
                last = nc.tensor.matmul(self.ps[:, j, w, :], lhsT=self.S[:, j, w * P:(w + 1) * P],
                                        rhs=msg(j), start=True, stop=True)
            if self.deg is not None:
                for w in range(2):
                    at = 128 + 2 * j + w
                    last = nc.tensor.matmul(self.ps_x[:, at:at + 1], lhsT=self.S[:, j, w * P:(w + 1) * P],
                                            rhs=self.ones[:, 0:1], start=True, stop=True)
            last.then_inc(self.summed, 1)
        (more,) = load_regs(nc, mybir.EngineType.PE, self.win[0:1, bass.ds(n * 8 + SB, 1)], T)
        with pe.If(more > 0):
            with pe.Fori(0, more) as _:
                for j in range(SB):
                    self.wait_next(pe, self.x_ready, "pe")
                    last = nc.tensor.matmul(self.ps_x[:, 0:D], lhsT=self.Sx[:, :], rhs=msg(j),
                                            start=True, stop=True)
                    if self.deg is not None:
                        last = nc.tensor.matmul(self.ps_x[:, 64:65], lhsT=self.Sx[:, :],
                                                rhs=self.ones[:, 0:1], start=True, stop=True)
                    last.then_inc(self.x_summed, 1)

    def vector_add(self, dve, i, h, signals=()):
        nc, n = self.nc, 2 * i + h
        DVE = mybir.EngineType.DVE
        regs = load_regs(nc, DVE, self.win[0:1, bass.ds(n * 8, 8)], (T - 2) * D)
        if self.deg is not None:
            blocks = load_regs(nc, DVE, self.win_b[0:1, bass.ds(n * 8, 8)], T - 2)
        for j in range(SB):
            if j in (0, BANK):
                dve.wait_ge(self.summed, n * SB + min(j + BANK, SB))
            if not (isinstance(n, int) and n * SB + j == 0):
                dve.wait_ge(self.added, n * SB + j)
            part = self.agg[:, bass.ds(regs[j], 2 * D)]
            nc.vector.tensor_tensor(part, self.ps[:, j, :, :].rearrange("p w f -> p (w f)"), part,
                                    ALU.add).then_inc(self.added, 1)
        if self.deg is not None:
            for j in range(SB):
                if not (isinstance(n, int) and n * SB + j == 0):
                    dve.wait_ge(self.counted, n * SB + j)
                part = self.deg[:, bass.ds(blocks[j], 2)]
                nc.vector.tensor_tensor(part, self.ps_x[:, 128 + 2 * j:130 + 2 * j], part,
                                        ALU.add).then_inc(self.counted, 1)
        more = regs[SB]
        with dve.If(more > 0):
            dve.wait_ge(self.added, n * SB + SB)
            if self.deg is not None:
                dve.wait_ge(self.counted, n * SB + SB)

            def link(ins):
                ins.then_inc(self.x_chain, 1)
                self.wait_next(dve, self.x_chain, "link")
            link(nc.vector.tensor_scalar(self.relx[:, :], self.dst_rel[:, bass.ds(n * SB, SB)], -float(P),
                                         None, ALU.add))
            with dve.Fori(0, more) as w:
                link(nc.vector.tensor_scalar(self.relx[:, :], self.relx[:, :], -float(P), None, ALU.add))
                for j in range(SB):
                    nc.vector.tensor_scalar(self.Sx[:, :], self.iota_w[:, 0:P], self.relx[:, j:j + 1], None,
                                            ALU.is_equal).then_inc(self.x_ready, 1)
                    self.wait_next(dve, self.x_summed, "dve")
                    part = self.agg[:, bass.ds(self.within(dve, regs[j] + w * D + 2 * D, (T - 1) * D), D)]
                    link(nc.vector.tensor_tensor(part, self.ps_x[:, 0:D], part, ALU.add))
                    if self.deg is not None:
                        part = self.deg[:, bass.ds(self.within(dve, blocks[j] + w + 2, T - 1), 1)]
                        link(nc.vector.tensor_tensor(part, self.ps_x[:, 64:65], part, ALU.add))
        for done in signals:
            nc.vector.memset(self.tick[:, :], 0.0).then_inc(done, 1)




def norm_stats(nc, c, x_in, st, small, eps_col, std_ready, roots, n):
    for k in range(GB):
        last = nc.vector.bn_stats(st[:, k, :], x_in(k))
    c.link(last)
    mean2, m2, rstd, shift, dif = (small[:, s, :] for s in range(5))
    nc.vector.tensor_tensor(mean2, st[:, :, 1], st[:, :, 4], ALU.add)
    nc.vector.tensor_tensor(dif, st[:, :, 1], st[:, :, 4], ALU.subtract)
    c.link(nc.vector.tensor_tensor(m2, st[:, :, 2], st[:, :, 5], ALU.add))
    c.link(nc.vector.tensor_tensor(dif, dif, dif, ALU.mult))
    nc.vector.scalar_tensor_tensor(out=m2, in0=dif, scalar=D / 4.0, in1=m2, op0=ALU.mult,
                                   op1=ALU.add).then_inc(std_ready, 1)
    c.eng.wait_ge(roots, n + 1)
    c.link(nc.vector.reciprocal(rstd, rstd))
    return nc.vector.scalar_tensor_tensor(out=shift, in0=mean2, scalar=-0.5, in1=rstd, op0=ALU.mult,
                                          op1=ALU.mult)


def norm_apply(nc, act, x_in, small, eps_col, to, std_ready, roots, shifts, n):
    act.wait_ge(std_ready, n + 1)
    nc.scalar.activation(small[:, 2, :], small[:, 1, :], ACT.Sqrt, bias=eps_col[:, 0:1],
                         scale=1.0 / D).then_inc(roots, 1)
    act.wait_ge(shifts, n + 1)
    for k in range(GB):
        last = nc.scalar.activation(to(k), x_in(k), ACT.Relu, bias=small[:, 3, k:k + 1],
                                    scale=small[:, 2, k:k + 1])
    return last


class Pass:

    def __init__(self, nc, ctx, tag):
        self.nc, self.ctx, self.tag = nc, ctx, tag

    def sb(self, name, shape, dt=F32):
        return self.ctx.enter_context(self.nc.sbuf_tensor(f"{self.tag}_{name}", shape, dt))

    def ps(self, name, shape):
        return self.ctx.enter_context(self.nc.psum_tensor(f"{self.tag}_{name}", shape, F32))

    def sem(self, name):
        return self.nc.alloc_semaphore(f"{self.tag}_{name}")

    def sems(self, names):
        return [self.sem(n) for n in names.split()]


def group(agg, n):
    return agg[:, bass.ds(n * GC, GC)]


def rows_of(buf):
    return buf.rearrange("p (k f) -> p k f", f=D)


def store_group(sp, tab, n, buf):
    return sp.dma_start(tiles_of(tab, n * GB, GB), rows_of(buf))


def first_norm(nc, x, agg, h_tab, xh_tab, eps_col):
    with ExitStack() as ctx:
        ctx.enter_context(nc.cleanup_on_exit())
        p = Pass(nc, ctx, "n0")
        xb = p.sb("x", [P, 2, GC])
        xh = p.sb("xh", [P, 2, GC])
        st = p.sb("st", [P, GB, 6])
        small = p.sb("small", [P, 5, GB])
        std_ready, roots, shifts, chain, h_ready, xh_ready = p.sems("std_ready roots shifts chain h_ready xh_ready")
        x_in, xh_out, h_out = ([p.sem(f"{s}{h}") for h in range(2)] for s in ("x_in", "xh_out", "h_out"))
        block = ctx.enter_context(nc.Block())
        full_groups = FULL // GB
        left = FULL - full_groups * GB
        assert full_groups == 2 * GSTEPS - 1

        @block.sync
        def _(sp):
            def load(i, h, first):
                n = 2 * i + h
                if not first:
                    sp.wait_ge(xh_ready, n - 1)
                if isinstance(n, int) and n == full_groups:
                    part = rows_of(xb[:, h, :])
                    sp.dma_start(part[:, 0:left, :], tiles_of(x, n * GB, left)).then_inc(x_in[h], 16)
                    sp.dma_start(part[0:REST, left, :], x[FULL * P:N, :]).then_inc(x_in[h], 16)
                else:
                    sp.dma_start(rows_of(xb[:, h, :]), tiles_of(x, n * GB, GB)).then_inc(x_in[h], 16)

            def store(i, h):
                n = 2 * i + h
                sp.wait_ge(h_ready, n + 1)
                store_group(sp, h_tab, n, group(agg, n)).then_inc(h_out[h], 16)
                sp.wait_ge(xh_ready, n + 1)
                store_group(sp, xh_tab, n, xh[:, h, :]).then_inc(xh_out[h], 16)

            load(0, 0, True)
            load(0, 1, True)
            with sp.Fori(0, GSTEPS - 2) as i:
                for h in range(2):
                    store(i, h)
                    load(i + 1, h, False)
            for i in range(GSTEPS - 2, GSTEPS):
                for h in range(2):
                    store(i, h)
                    if i + 1 < GSTEPS:
                        load(i + 1, h, False)
            for h in range(2):
                sp.wait_ge(h_out[h], 16 * GSTEPS)
                sp.wait_ge(xh_out[h], 16 * GSTEPS)

        def x_landed(eng, i, h):
            eng.wait_ge(x_in[h], 16 * (i + 1) + (16 if isinstance(i, int) and i == GSTEPS - 1 and h else 0))

        def peel_last(eng, body):
            body(0, True)
            with eng.Fori(1, GSTEPS - 1) as i:
                body(i, False)
            body(GSTEPS - 1, False)

        @block.vector
        def _(dve):
            c = Links(dve, chain, 8)

            def body(i, first):
                c.step(i)
                for h in range(2):
                    n = 2 * i + h
                    x_landed(dve, i, h)
                    if not first or h:
                        dve.wait_ge(h_ready, n)
                    norm_stats(nc, c, lambda k: xb[:, h, k * D:(k + 1) * D], st, small, eps_col,
                               std_ready, roots, n).then_inc(shifts, 1)
                c.done()
            peel_last(dve, body)

        @block.scalar
        def _(act):
            def body(i, first):
                for h in range(2):
                    n = 2 * i + h
                    to = group(agg, n)
                    norm_apply(nc, act, lambda k: xb[:, h, k * D:(k + 1) * D], small, eps_col,
                               lambda k: agg[:, bass.ds(n * GC + k * D, D)], std_ready, roots, shifts,
                               n).then_inc(h_ready, 1)
            peel_last(act, body)

        @block.gpsimd
        def _(pool):
            def body(i, first):
                for h in range(2):
                    n = 2 * i + h
                    pool.wait_ge(h_ready, n + 1)
                    if not first:
                        pool.wait_ge(xh_out[h], 16 * i)
                    nc.gpsimd.tensor_tensor(xh[:, h, :], xb[:, h, :], group(agg, n), ALU.add)\
                        .then_inc(xh_ready, 1)
            peel_last(pool, body)


def gcn_edges(nc, layer, h_tab, agg, src_idx, dst_rel, win, iota_w):
    with ExitStack() as ctx:
        ctx.enter_context(nc.cleanup_on_exit())
        p = Pass(nc, ctx, f"ge{layer}")
        ring = p.sb("ring", [P, 2, SB, D])
        idx_small = p.sb("idx", [P, 1, 2, SB], I32)
        rows_used, landed = ([p.sem(f"{s}{h}") for h in range(2)] for s in ("rows_used", "landed"))
        idx_ready = p.sem("idx_ready")
        sums = Sums(nc, ctx, p.tag, agg, dst_rel, win, iota_w)
        block = ctx.enter_context(nc.Block())

        @block.gpsimd
        def _(pool):
            gather_pass(nc, pool, p.tag, [(h_tab, src_idx, 0)], idx_small, lambda h, j, s: ring[:, h, j, :],
                        lambda i, h: pool.wait_ge(rows_used[h], i), landed, idx_ready)

        @block.vector
        def _(dve):
            sums.start(dve, "dve")
            sums.start(dve, "link")
            sums.start(dve, "place")

            def body(i, first):
                for h in range(2):
                    sums.vector_members(dve, i, h)
                    sums.vector_add(dve, i, h, [rows_used[h]])
            peel_first(dve, STEPS, body)

        @block.tensor
        def _(pe):
            sums.start(pe, "pe")

            def body(i, first):
                for h in range(2):
                    pe.wait_ge(landed[h], 16 * SB * (i + 1))
                    sums.tensor_sum(pe, i, h, lambda j: ring[:, h, j, :])
            peel_first(pe, STEPS, body)


def gin_edges(nc, h_tab, ea32_s, W_edge, b_edge, agg, src_idx, dst_rel, win, iota_w, ident):
    K1 = EA + 1
    PACK = 3
    packs = [(q * PACK, min(PACK, SB - q * PACK)) for q in range(-(-SB // PACK))]
    with ExitStack() as ctx:
        ctx.enter_context(nc.cleanup_on_exit())
        p = Pass(nc, ctx, "e0")
        ring = p.sb("ring", [P, 2, SB, D])
        idx_small = p.sb("idx", [P, 1, 2, SB], I32)
        ea = p.sb("ea", [P, 2, SB, K1])
        eaT = p.sb("eaT", [P, len(packs), P])
        w = p.sb("w", [P, PACK, D])
        msg = p.sb("msg", [P, SB, D])
        raw = p.sb("raw", [P, SB, D])
        ps_t = p.ps("ps_t", [P, 4, P])
        ps_e = p.ps("ps_e", [P, 8, D])
        rows_used, landed, ea_in = ([p.sem(f"{s}{h}") for h in range(2)] for s in ("rows_used", "landed", "ea_in"))
        idx_ready, turned, copied, mixed, raw_ready, msg_ready, cleared, w_in, zeroed = p.sems(
            "idx_ready turned copied mixed raw_ready msg_ready cleared w_in zeroed")
        sums = Sums(nc, ctx, p.tag, agg, dst_rel, win, iota_w)
        block = ctx.enter_context(nc.Block())

        @block.gpsimd
        def _(pool):
            nc.gpsimd.memset(w[:, :, :], 0.0).then_inc(zeroed, 1)
            nc.gpsimd.memset(ea[:, :, :, EA:K1], 1.0).then_inc(cleared, 1)
            gather_pass(nc, pool, p.tag, [(h_tab, src_idx, 0)], idx_small, lambda h, j, s: ring[:, h, j, :],
                        lambda i, h: pool.wait_ge(rows_used[h], i), landed, idx_ready)

        @block.sync
        def _(sp):
            sp.wait_ge(zeroed, 1)
            for q in range(PACK):
                sp.dma_start(w[q * K1:q * K1 + EA, q, :], W_edge[:, :]).then_inc(w_in, 16)
                sp.dma_start(w[q * K1 + EA:(q + 1) * K1, q, :],
                             b_edge.rearrange("(o f) -> o f", o=1)).then_inc(w_in, 16)

            def body(i, first):
                for h in range(2):
                    n = 2 * i + h
                    if not first:
                        sp.wait_ge(turned, n - 1)
                    sp.dma_start(ea[:, h, :, 0:EA], tiles_of(ea32_s, n * SB, SB)).then_inc(ea_in[h], 16)
            peel_first(sp, STEPS, body)

        @block.scalar
        def _(act):
            def body(i, first):
                for h in range(2):
                    n = 2 * i + h
                    act.wait_ge(turned, n + 1)
                    if not first or h:
                        act.wait_ge(mixed, n)
                    for q, (_, many) in enumerate(packs):
                        last = nc.scalar.activation(eaT[0:many * K1, q, :], ps_t[0:many * K1, q, :], ACT.Copy)
                    last.then_inc(copied, 1)
            peel_first(act, STEPS, body)

        @block.tensor
        def _(pe):
            sums.start(pe, "pe")
            pe.wait_ge(w_in, 16 * 2 * PACK)
            pe.wait_ge(cleared, 1)

            def body(i, first):
                for h in range(2):
                    n = 2 * i + h
                    pe.wait_ge(ea_in[h], 16 * (i + 1))
                    for q, (t0, many) in enumerate(packs):
                        last = nc.tensor.transpose(
                            ps_t[0:many * K1, q, :],
                            ea[:, h, t0:t0 + many, :].rearrange("p k f -> p (k f)"), ident[:, :])
                    last.then_inc(turned, 1)
                    pe.wait_ge(copied, n + 1)
                    if not first or h:
                        pe.wait_ge(raw_ready, n)
                    for j in range(SB):
                        q = j // PACK
                        k = packs[q][1] * K1
                        last = nc.tensor.matmul(ps_e[:, j, :], lhsT=eaT[0:k, q, :], rhs=w[0:k, j % PACK, :],
                                                start=True, stop=True)
                    last.then_inc(mixed, 1)
                    pe.wait_ge(msg_ready, n + 1)
                    sums.tensor_sum(pe, i, h, lambda j: msg[:, j, :])
            peel_first(pe, STEPS, body)

        @block.vector
        def _(dve):
            for name in ("dve", "link", "place"):
                sums.start(dve, name)

            def body(i, first):
                for h in range(2):
                    n = 2 * i + h
                    dve.wait_ge(landed[h], 16 * SB * (i + 1))
                    dve.wait_ge(mixed, n + 1)
                    nc.vector.tensor_tensor(raw[:, :, :], ps_e[:, 0:SB, :], ring[:, h, :, :],
                                            ALU.add).then_inc(raw_ready, 1)
                    dve.wait_ge(raw_ready, n + 1)
                    nc.vector.tensor_scalar(msg[:, :, :], raw[:, :, :], 0.0, None,
                                            ALU.max).then_inc(msg_ready, 1)
                    sums.vector_members(dve, i, h)
                    sums.vector_add(dve, i, h, [rows_used[h]])
            peel_first(dve, STEPS, body)


def gin_nodes(nc, agg, xh_tab, h_tab, W1, b1, gamma, beta, W2, b2, ident, ones, eps_col):
    pads = NP - N
    C0 = (FULL // 2) * P
    assert FULL % 2 == 0 and T - FULL == 2
    with ExitStack() as both:
        p = Pass(nc, both, "m")
        wbd = [p.sb(f"wbd{k}", [P, P]) for k in range(2)]
        cols = p.sb("cols", [P, 3])
        b2row = p.sb("b2row", [1, P])
        scale, shift = p.sb("scale", [P, 1]), p.sb("shift", [P, 1])
        with ExitStack() as ctx:
            ctx.enter_context(nc.cleanup_on_exit())
            p = Pass(nc, ctx, "m1")
            stage = p.sb("stage", [P, 2, GC])
            aT = p.sb("aT", [P, GC])
            stats = p.sb("stats", [P, 4 * GSTEPS, 6])
            mv = p.sb("mv", [P, 2])
            fold = p.sb("fold", [P, P])
            tmp = p.sb("tmp", [P, 8])
            ps_t = p.ps("ps_t", [P, 8, P])
            ps_1 = p.ps("ps_1", [P, 1024])
            ps_f = p.ps("ps_f", [P, 2])
            zeroed, w_in, staged, turned, copied, mixed, biased, chain, folded, rooted, padz = p.sems(
                "zeroed w_in staged turned copied mixed biased chain folded rooted padz")
            block = ctx.enter_context(nc.Block())

            @block.sync
            def _(sp):
                sp.wait_ge(zeroed, 2)
                for a in range(2):
                    half = slice(a * D, (a + 1) * D)
                    for wb, wd in zip(wbd, (W1, W2)):
                        sp.dma_start(wb[half, half], wd[:, :]).then_inc(w_in, 16)
                    for k, vec in enumerate((b1, gamma, beta)):
                        sp.dma_start(cols[half, k:k + 1], vec.rearrange("(f o) -> f o", o=1)).then_inc(w_in, 16)
                    sp.dma_start(b2row[:, half], b2.rearrange("(o f) -> o f", o=1)).then_inc(w_in, 16)
                sp.wait_ge(w_in, 16 * 12)

            @block.gpsimd
            def _(pool):
                nc.gpsimd.memset(wbd[0][:, :], 0.0).then_inc(zeroed, 1)
                nc.gpsimd.memset(wbd[1][:, :], 0.0).then_inc(zeroed, 1)

                def body(i, first):
                    for h in range(2):
                        n = 2 * i + h
                        if not first:
                            pool.wait_ge(turned, n - 1)
                        nc.gpsimd.tensor_copy(stage[:, h, :], group(agg, n)).then_inc(staged, 1)
                peel_first(pool, GSTEPS, body)

            @block.tensor
            def _(pe):
                pe.wait_ge(w_in, 16 * 12)

                def body(i, first):
                    for h in range(2):
                        n = 2 * i + h
                        pe.wait_ge(staged, n + 1)
                        for q in range(GB // 2):
                            last = nc.tensor.transpose(ps_t[:, q, :], stage[:, h, q * P:(q + 1) * P],
                                                       ident[:, :])
                        last.then_inc(turned, 1)
                        pe.wait_ge(copied, n + 1)
                        if not first or h:
                            pe.wait_ge(biased, n)
                        nc.tensor.matmul(ps_1[:, 0:512], lhsT=wbd[0][:, :], rhs=aT[:, 0:512], start=True,
                                         stop=True)
                        nc.tensor.matmul(ps_1[:, 512:GC], lhsT=wbd[0][:, :], rhs=aT[:, 512:GC], start=True,
                                         stop=True).then_inc(mixed, 1)
                peel_first(pe, GSTEPS, body)
                for k in range(2):
                    pe.wait_ge(folded, k + 1)
                    nc.tensor.matmul(ps_f[:, k:k + 1], lhsT=fold[:, :], rhs=tmp[:, k:k + 1], start=True,
                                     stop=True).then_inc(mixed, 1)

            @block.scalar
            def _(act):
                act.wait_ge(w_in, 16 * 12)

                def body(i, first):
                    for h in range(2):
                        n = 2 * i + h
                        act.wait_ge(turned, n + 1)
                        if not first or h:
                            act.wait_ge(mixed, n)
                        nc.scalar.activation(aT[:, 0:512], ps_t[:, 0:4, :].rearrange("p q n -> p (q n)"), ACT.Copy)
                        nc.scalar.activation(aT[:, 512:GC], ps_t[:, 4:7, :].rearrange("p q n -> p (q n)"),
                                             ACT.Copy).then_inc(copied, 1)
                        act.wait_ge(mixed, n + 1)
                        to = group(agg, n)
                        nc.scalar.activation(to, ps_1[:, 0:GC], ACT.Identity,
                                             bias=cols[:, 0:1]).then_inc(biased, 1)
                peel_first(act, GSTEPS, body)
                act.wait_ge(folded, 3)
                nc.scalar.activation(tmp[:, 4:5], tmp[:, 3:4], ACT.Sqrt, bias=eps_col[:, 0:1]).then_inc(rooted, 1)

            @block.vector
            def _(dve):
                def body(i, first):
                    for h in range(2):
                        n = 2 * i + h
                        dve.wait_ge(biased, n + 1)
                        if isinstance(n, int) and n == 2 * GSTEPS - 1:
                            nc.vector.memset(agg[:, C0 + REST:C0 + P], 0.0).then_inc(padz, 1)
                            nc.vector.memset(agg[D:P, C0:C0 + REST], 0.0).then_inc(padz, 1)
                            dve.wait_ge(padz, 2)
                        for s in range(2):
                            nc.vector.bn_stats(stats[:, bass.ds(2 * n + s, 1), :].rearrange("p a s -> p (a s)"),
                                               agg[:, bass.ds(n * GC + s * (GC // 2), GC // 2)])
                body(0, True)
                with dve.Fori(1, GSTEPS - 1) as i:
                    body(i, False)
                body(GSTEPS - 1, False)
                c = Links(dve, chain, 0)
                c.step(0)
                for a in range(2):
                    last = nc.vector.tensor_tensor(fold[:, a * D:(a + 1) * D], ident[:, 0:D], ident[:, D:P],
                                                   ALU.add)
                c.link(last)
                c.link(nc.vector.bn_aggr(mv[:, :], stats[:, :, :].rearrange("p a s -> p (a s)")))
                nc.vector.tensor_copy(tmp[:, 0:1], mv[:, 0:1]).then_inc(folded, 1)
                dve.wait_ge(mixed, 2 * GSTEPS + 1)
                c.link(nc.vector.tensor_scalar(tmp[:, 2:3], ps_f[:, 0:1], 0.5, None, ALU.mult))
                c.link(nc.vector.tensor_tensor(tmp[:, 5:6], mv[:, 0:1], tmp[:, 2:3], ALU.subtract))
                c.link(nc.vector.tensor_tensor(tmp[:, 6:7], tmp[:, 5:6], tmp[:, 5:6], ALU.mult))
                nc.vector.tensor_tensor(tmp[:, 1:2], tmp[:, 6:7], mv[:, 1:2], ALU.add).then_inc(folded, 1)
                dve.wait_ge(mixed, 2 * GSTEPS + 2)
                c.link(nc.vector.tensor_scalar(tmp[:, 7:8], tmp[:, 2:3], NP / N, None, ALU.mult))
                c.link(nc.vector.tensor_tensor(tmp[:, 5:6], tmp[:, 7:8], tmp[:, 7:8], ALU.mult))
                c.link(nc.vector.tensor_scalar(tmp[:, 6:7], ps_f[:, 1:2], 0.5 * NP / N, None, ALU.mult))
                nc.vector.scalar_tensor_tensor(out=tmp[:, 3:4], in0=tmp[:, 5:6], scalar=-pads / NP,
                                               in1=tmp[:, 6:7], op0=ALU.mult, op1=ALU.add).then_inc(folded, 1)
                dve.wait_ge(rooted, 1)
                c.link(nc.vector.reciprocal(tmp[:, 4:5], tmp[:, 4:5]))
                c.link(nc.vector.tensor_tensor(scale[:, :], tmp[:, 4:5], cols[:, 1:2], ALU.mult))
                c.link(nc.vector.tensor_tensor(tmp[:, 5:6], tmp[:, 7:8], scale[:, :], ALU.mult))
                c.link(nc.vector.tensor_tensor(shift[:, :], cols[:, 2:3], tmp[:, 5:6], ALU.subtract))

        with ExitStack() as ctx:
            ctx.enter_context(nc.cleanup_on_exit())
            p = Pass(nc, ctx, "m2")
            y = p.sb("y", [P, 2, GC])
            xh = p.sb("xh", [P, 2, GC])
            x1 = p.sb("x1", [P, 2, GC])
            hb = p.sb("hb", [P, 2, GC])
            st = p.sb("st", [P, GB, 6])
            small = p.sb("small", [P, 5, GB])
            ps_2 = p.ps("ps_2", [P, 8, P])
            std_ready, roots, shifts, chain, y_ready, mixed, x1_ready, h_ready, summed = p.sems(
                "std_ready roots shifts chain y_ready mixed x1_ready h_ready summed")
            xh_in, h_out = ([p.sem(f"{s}{h}") for h in range(2)] for s in ("xh_in", "h_out"))
            block = ctx.enter_context(nc.Block())

            @block.sync
            def _(sp):
                load_store(sp, GSTEPS,
                           lambda i, h: sp.dma_start(rows_of(xh[:, h, :]), tiles_of(xh_tab, (2 * i + h) * GB, GB))
                           .then_inc(xh_in[h], 16),
                           lambda i, h: (sp.wait_ge(h_ready, 2 * i + h + 1),
                                         store_group(sp, h_tab, 2 * i + h, hb[:, h, :]).then_inc(h_out[h], 16)))
                for h in range(2):
                    sp.wait_ge(h_out[h], 16 * GSTEPS)

            @block.scalar
            def _(act):
                def activate(n, h):
                    nc.scalar.activation(y[:, h, :], group(agg, n), ACT.Relu, bias=shift[:, 0:1],
                                         scale=scale[:, 0:1]).then_inc(y_ready, 1)

                def body(i, first, last=False):
                    for h in range(2):
                        n = 2 * i + h
                        if not (last and h):
                            if not first or h:
                                act.wait_ge(mixed, n)
                            activate(n + 1, 1 - h)
                        if not first:
                            act.wait_ge(h_out[h], 16 * i)
                            act.wait_ge(summed, n - 1)
                        norm_apply(nc, act, lambda k: x1[:, h, k * D:(k + 1) * D], small, eps_col,
                                   lambda k: hb[:, h, k * D:(k + 1) * D], std_ready, roots, shifts,
                                   n).then_inc(h_ready, 1)
                activate(0, 0)
                body(0, True)
                with act.Fori(1, GSTEPS - 1) as i:
                    body(i, False)
                body(GSTEPS - 1, False, True)

            @block.tensor
            def _(pe):
                def body(i, first):
                    for h in range(2):
                        n = 2 * i + h
                        pe.wait_ge(y_ready, n + 1)
                        if not first or h:
                            pe.wait_ge(x1_ready, n)
                        for q in range(GB // 2):
                            nc.tensor.matmul(ps_2[:, q, :], lhsT=y[:, h, q * P:(q + 1) * P], rhs=wbd[1][:, :],
                                             start=True, stop=False)
                            last = nc.tensor.matmul(ps_2[:, q, :], lhsT=ones[0:1, :], rhs=b2row[:, :],
                                                    start=False, stop=True)
                        last.then_inc(mixed, 1)
                peel_first(pe, GSTEPS, body)

            @block.vector
            def _(dve):
                c = Links(dve, chain, 8)

                def body(i, first):
                    c.step(i)
                    for h in range(2):
                        n = 2 * i + h
                        dve.wait_ge(mixed, n + 1)
                        dve.wait_ge(xh_in[h], 16 * (i + 1))
                        if not first:
                            dve.wait_ge(summed, n - 1)
                        nc.vector.tensor_tensor(x1[:, h, :], ps_2[:, 0:7, :].rearrange("p q n -> p (q n)"),
                                                xh[:, h, :], ALU.add).then_inc(x1_ready, 1)
                        dve.wait_ge(x1_ready, n + 1)
                        if not first or h:
                            dve.wait_ge(h_ready, n)
                        norm_stats(nc, c, lambda k: x1[:, h, k * D:(k + 1) * D], st, small, eps_col,
                                   std_ready, roots, n).then_inc(shifts, 1)
                peel_first(dve, GSTEPS, body)

            @block.gpsimd
            def _(pool):
                def body(i, first):
                    for h in range(2):
                        n = 2 * i + h
                        pool.wait_ge(h_ready, n + 1)
                        nc.gpsimd.tensor_tensor(group(agg, n), x1[:, h, :], hb[:, h, :], ALU.add)\
                            .then_inc(summed, 1)
                peel_first(pool, GSTEPS, body)


def load_store(sp, steps, load, store, before_load=None):
    load(0, 0)
    load(0, 1)
    with sp.Fori(0, steps - 1) as i:
        for h in range(2):
            store(i, h)
            load(i + 1, h)
    for h in range(2):
        store(steps - 1, h)


def gated_edges(nc, h_tab, ea10_s, Wf, bf, Ws, bs, agg, deg, src_idx, dst_idx, dst_rel, win, win_b,
                iota_w, ident, ones):
    K1 = EB + 1
    K = SB * K1
    with ExitStack() as ctx:
        ctx.enter_context(nc.cleanup_on_exit())
        p = Pass(nc, ctx, "e1")
        ring = p.sb("ring", [P, 2, SB, 2 * D])
        idx_small = p.sb("idx", [P, 2, 2, SB], I32)
        ea = p.sb("ea", [P, 2, SB, K1])
        eaT = p.sb("eaT", [K, P])
        hT = p.sb("hT", [P, SB, P])
        wcat = p.sb("wcat", [P, P])
        wea = p.sb("wea", [K, SB, P])
        small_e = p.sb("small_e", [P, SB, P])
        log_e = p.sb("log_e", [P, SB, P])
        soft = p.sb("soft", [P, SB, P])
        gate = p.sb("gate", [P, SB, D])
        msg = p.sb("msg", [P, SB, D])
        ps_ea = p.ps("ps_ea", [P, P])
        ps_t = p.ps("ps_t", [P, 8, P])
        ps_m = p.ps("ps_m", [P, 8, P])
        landed, ea_in = ([p.sem(f"{s}{h}") for h in range(2)] for s in ("landed", "ea_in"))
        idx_ready, turned, copied, mixed, act_chain, logs_ready, soft_ready, gated, msg_ready, cleared, w_in, zeroed, negated = p.sems(
            "idx_ready turned copied mixed act_chain logs_ready soft_ready gated msg_ready cleared w_in zeroed negated")
        sums = Sums(nc, ctx, p.tag, agg, dst_rel, win, iota_w, deg, win_b, ones)
        block = ctx.enter_context(nc.Block())

        @block.gpsimd
        def _(pool):
            nc.gpsimd.memset(wea[:, :, :], 0.0).then_inc(zeroed, 1)
            nc.gpsimd.memset(ea[:, :, :, EB:K1], 1.0).then_inc(cleared, 1)
            gather_pass(nc, pool, p.tag, [(h_tab, src_idx, 0), (h_tab, dst_idx, 1)], idx_small,
                        lambda h, j, s: ring[:, h, j, s * D:(s + 1) * D],
                        lambda i, h: pool.wait_ge(turned, 2 * i + h - 1), landed, idx_ready)

        @block.sync
        def _(sp):
            sp.wait_ge(zeroed, 1)
            for a, (wd, bd) in enumerate(((Wf, bf), (Ws, bs))):
                half = slice(a * D, (a + 1) * D)
                sp.dma_start(wcat[:, half], wd[0:P, :]).then_inc(w_in, 16)
                for j in range(SB):
                    sp.dma_start(wea[j * K1:j * K1 + EB, j, half], wd[P:P + EB, :]).then_inc(w_in, 16)
                    sp.dma_start(wea[j * K1 + EB:(j + 1) * K1, j, half],
                                 bd.rearrange("(o f) -> o f", o=1)).then_inc(w_in, 16)

            def body(i, first):
                for h in range(2):
                    n = 2 * i + h
                    if not first:
                        sp.wait_ge(turned, n - 1)
                    sp.dma_start(ea[:, h, :, 0:EB], tiles_of(ea10_s, n * SB, SB)).then_inc(ea_in[h], 16)
            peel_first(sp, STEPS, body)

        @block.tensor
        def _(pe):
            sums.start(pe, "pe")
            pe.wait_ge(negated, 2)
            pe.wait_ge(cleared, 1)

            def body(i, first):
                for h in range(2):
                    n = 2 * i + h
                    pe.wait_ge(ea_in[h], 16 * (i + 1))
                    pe.wait_ge(landed[h], 16 * 2 * SB * (i + 1))
                    nc.tensor.transpose(ps_ea[0:K, :], ea[:, h, :, :].rearrange("p k f -> p (k f)"), ident[:, :])
                    for j in range(SB):
                        last = nc.tensor.transpose(ps_t[:, j, :], ring[:, h, j, :], ident[:, :])
                    last.then_inc(turned, 1)
                    pe.wait_ge(copied, n + 1)
                    if not first or h:
                        pe.wait_ge(msg_ready, n)
                    for j in range(SB):
                        nc.tensor.matmul(ps_m[:, j, :], lhsT=hT[:, j, :], rhs=wcat[:, :], start=True, stop=False)
                        last = nc.tensor.matmul(ps_m[:, j, :], lhsT=eaT[:, :], rhs=wea[:, j, :], start=False,
                                                stop=True)
                    last.then_inc(mixed, 1)
                    pe.wait_ge(msg_ready, n + 1)
                    sums.tensor_sum(pe, i, h, lambda j: msg[:, j, :])
            peel_first(pe, STEPS, body)

        @block.scalar
        def _(act):
            c = Links(act, act_chain, 4)
            act.wait_ge(w_in, 16 * 2 * (1 + 2 * SB))
            nc.scalar.activation(wcat[:, 0:D], wcat[:, 0:D], ACT.Copy, scale=-1.0).then_inc(negated, 1)
            nc.scalar.activation(wea[:, :, 0:D], wea[:, :, 0:D], ACT.Copy, scale=-1.0).then_inc(negated, 1)

            def body(i, first):
                c.step(i)
                for h in range(2):
                    n = 2 * i + h
                    act.wait_ge(turned, n + 1)
                    if not first or h:
                        act.wait_ge(mixed, n)
                    nc.scalar.activation(eaT[:, :], ps_ea[0:K, :], ACT.Copy)
                    nc.scalar.activation(hT[:, 0:BANK, :], ps_t[:, 0:BANK, :], ACT.Copy)
                    nc.scalar.activation(hT[:, BANK:SB, :], ps_t[:, BANK:SB, :], ACT.Copy).then_inc(copied, 1)
                    act.wait_ge(mixed, n + 1)
                    c.link(nc.scalar.activation(small_e[:, :, :], ps_m[:, 0:SB, :], ACT.Abs))
                    c.link(nc.scalar.activation(small_e[:, :, :], small_e[:, :, :], ACT.Exp, scale=-1.0))
                    nc.scalar.activation(log_e[:, :, :], small_e[:, :, :], ACT.Ln,
                                         bias=ones[:, 0:1]).then_inc(logs_ready, 1)
                    act.wait_ge(soft_ready, n + 1)
                    if not first or h:
                        act.wait_ge(msg_ready, n)
                    nc.scalar.activation(gate[:, :, :], soft[:, :, 0:D], ACT.Exp, scale=-1.0).then_inc(gated, 1)
                c.done()
            peel_first(act, STEPS, body)

        @block.vector
        def _(dve):
            for name in ("dve", "link", "place"):
                sums.start(dve, name)

            def body(i, first):
                for h in range(2):
                    n = 2 * i + h
                    dve.wait_ge(logs_ready, n + 1)
                    nc.vector.scalar_tensor_tensor(out=soft[:, :, :], in0=ps_m[:, 0:SB, :], scalar=0.0,
                                                   in1=log_e[:, :, :], op0=ALU.max, op1=ALU.add)\
                        .then_inc(soft_ready, 1)
                    sums.vector_members(dve, i, h)
                    dve.wait_ge(gated, n + 1)
                    nc.vector.tensor_tensor(msg[:, :, :], gate[:, :, :], soft[:, :, D:P],
                                            ALU.mult).then_inc(msg_ready, 1)
                    sums.vector_add(dve, i, h)
            peel_first(dve, STEPS, body)


def norm_nodes(nc, agg, h_tab, eps_col):
    with ExitStack() as ctx:
        ctx.enter_context(nc.cleanup_on_exit())
        p = Pass(nc, ctx, "n2")
        hb = p.sb("hb", [P, 2, GC])
        st = p.sb("st", [P, GB, 6])
        small = p.sb("small", [P, 5, GB])
        std_ready, roots, shifts, chain, h_ready = p.sems("std_ready roots shifts chain h_ready")
        h_out = [p.sem(f"h_out{h}") for h in range(2)]
        block = ctx.enter_context(nc.Block())

        @block.sync
        def _(sp):
            with sp.Fori(0, GSTEPS) as i:
                for h in range(2):
                    sp.wait_ge(h_ready, 2 * i + h + 1)
                    store_group(sp, h_tab, 2 * i + h, hb[:, h, :]).then_inc(h_out[h], 16)
            for h in range(2):
                sp.wait_ge(h_out[h], 16 * GSTEPS)

        @block.vector
        def _(dve):
            c = Links(dve, chain, 8)

            def body(i, first):
                c.step(i)
                for h in range(2):
                    n = 2 * i + h
                    if not first or h:
                        dve.wait_ge(h_ready, n)
                    norm_stats(nc, c, lambda k: agg[:, bass.ds(n * GC + k * D, D)], st, small, eps_col,
                               std_ready, roots, n).then_inc(shifts, 1)
                c.done()
            peel_first(dve, GSTEPS, body)

        @block.scalar
        def _(act):
            def body(i, first):
                for h in range(2):
                    n = 2 * i + h
                    if not first:
                        act.wait_ge(h_out[h], 16 * i)
                    norm_apply(nc, act, lambda k: agg[:, bass.ds(n * GC + k * D, D)], small, eps_col,
                               lambda k: hb[:, h, k * D:(k + 1) * D], std_ready, roots, shifts,
                               n).then_inc(h_ready, 1)
            peel_first(act, GSTEPS, body)


def rel_edges(nc, h_tab, et_s, W_rel, agg, src_idx, dst_rel, win, iota_w, ident):
    PAIRS = RELS // 2
    parts = ((0, BANK), (BANK, SB))
    with ExitStack() as ctx:
        ctx.enter_context(nc.cleanup_on_exit())
        p = Pass(nc, ctx, "e2")
        ring = p.sb("ring", [P, 2, SB, 2 * D])
        idx_small = p.sb("idx", [P, 1, 2, SB], I32)
        types = p.sb("types", [P, 2, SB * P], I32)
        hT = p.sb("hT", [P, SB * P])
        kept = p.sb("kept", [P, PAIRS, SB * P])
        w = p.sb("w", [P, PAIRS, D])
        rel = p.sb("rel", [P, PAIRS])
        msg = p.sb("msg", [P, SB, D])
        ps_t = p.ps("ps_t", [P, 8, P])
        ps_m = p.ps("ps_m", [P, 8, D])
        landed, t_in = ([p.sem(f"{s}{h}") for h in range(2)] for s in ("landed", "t_in"))
        idx_ready, turned, copied, kept_ready, mixed, msg_ready, half_done, w_in, rel_ready, doubled = p.sems(
            "idx_ready turned copied kept_ready mixed msg_ready half_done w_in rel_ready doubled")
        sums = Sums(nc, ctx, p.tag, agg, dst_rel, win, iota_w)
        block = ctx.enter_context(nc.Block())

        @block.gpsimd
        def _(pool):
            for a in range(2):
                nc.gpsimd.iota(rel[a * D:(a + 1) * D, :], [[2, PAIRS]], base=a, channel_multiplier=0,
                               allow_small_or_imprecise_dtypes=True).then_inc(rel_ready, 1)
                pool.wait_ge(rel_ready, a + 1)
            gather_pass(nc, pool, p.tag, [(h_tab, src_idx, 0)], idx_small, lambda h, j, s: ring[:, h, j, 0:D],
                        lambda i, h: pool.wait_ge(turned, 2 * i + h - 1), landed, idx_ready)

        @block.sync
        def _(sp):
            by_half = W_rel.rearrange("(k a) i o -> a i k o", a=2)
            for a in range(2):
                sp.dma_start(w[a * D:(a + 1) * D, :, :], by_half[a]).then_inc(w_in, 16)

            def body(i, first):
                for h in range(2):
                    n = 2 * i + h
                    if not first:
                        sp.wait_ge(kept_ready, 2 * (n - 1))
                    sp.dma_start(types[:, h, :],
                                 et_s[0:1, bass.ds(n * SB * P, SB * P)].to_broadcast([P, SB * P]))\
                        .then_inc(t_in[h], 16)
            peel_first(sp, STEPS, body)

        @block.tensor
        def _(pe):
            sums.start(pe, "pe")
            pe.wait_ge(w_in, 32)

            def body(i, first):
                for h in range(2):
                    n = 2 * i + h
                    pe.wait_ge(landed[h], 16 * SB * (i + 1))
                    pe.wait_ge(doubled, n + 1)
                    for j in range(SB):
                        last = nc.tensor.transpose(ps_t[:, j, :], ring[:, h, j, :], ident[:, :])
                    last.then_inc(turned, 1)
                    for q, (t0, t1) in enumerate(parts):
                        pe.wait_ge(kept_ready, 2 * n + q + 1)
                        for j in range(t0, t1):
                            for k in range(PAIRS):
                                last = nc.tensor.matmul(ps_m[:, j, :], lhsT=kept[:, k, j * P:(j + 1) * P],
                                                        rhs=w[:, k, :], start=(k == 0), stop=(k == PAIRS - 1))
                    last.then_inc(mixed, 1)
                    pe.wait_ge(msg_ready, n + 1)
                    sums.tensor_sum(pe, i, h, lambda j: msg[:, j, :])
            peel_first(pe, STEPS, body)

        @block.scalar
        def _(act):
            def body(i, first):
                for h in range(2):
                    n = 2 * i + h
                    act.wait_ge(landed[h], 16 * SB * (i + 1))
                    nc.scalar.activation(ring[:, h, :, D:2 * D], ring[:, h, :, 0:D], ACT.Copy).then_inc(doubled, 1)
                    act.wait_ge(turned, n + 1)
                    if not first or h:
                        act.wait_ge(kept_ready, 2 * n)
                    nc.scalar.activation(hT[:, 0:BANK * P], ps_t[:, 0:BANK, :].rearrange("p q n -> p (q n)"),
                                         ACT.Copy)
                    nc.scalar.activation(hT[:, BANK * P:SB * P],
                                         ps_t[:, BANK:SB, :].rearrange("p q n -> p (q n)"),
                                         ACT.Copy).then_inc(copied, 1)
                    act.wait_ge(mixed, n + 1)
                    if not first or h:
                        act.wait_ge(half_done, n)
                    nc.scalar.activation(msg[:, :, :], ps_m[:, 0:SB, :], ACT.Copy).then_inc(msg_ready, 1)
            peel_first(act, STEPS, body)

        @block.vector
        def _(dve):
            for name in ("dve", "link", "place"):
                sums.start(dve, name)
            dve.wait_ge(rel_ready, 2)

            def body(i, first):
                for h in range(2):
                    n = 2 * i + h
                    dve.wait_ge(t_in[h], 16 * (i + 1))
                    dve.wait_ge(copied, n + 1)
                    for t0, t1 in parts:
                        at = slice(t0 * P, t1 * P)
                        for k in range(PAIRS):
                            last = nc.vector.scalar_tensor_tensor(
                                out=kept[:, k, at], in0=types[:, h, at], scalar=rel[:, k:k + 1],
                                in1=hT[:, at], op0=ALU.is_equal, op1=ALU.mult)
                        last.then_inc(kept_ready, 1)
                    sums.vector_members(dve, i, h)
                    sums.vector_add(dve, i, h, [half_done])
            peel_first(dve, STEPS, body)


def gcn_start(nc, agg, deg, dinv, h_tab, z_tab, xh_tab, eps_col):
    with ExitStack() as ctx:
        ctx.enter_context(nc.cleanup_on_exit())
        p = Pass(nc, ctx, "n3")
        hb = p.sb("hb", [P, 2, GC])
        st = p.sb("st", [P, GB, 6])
        small = p.sb("small", [P, 5, GB])
        std_ready, roots, shifts, chain, h_ready, scaled, dinv_ready, deg_root = p.sems(
            "std_ready roots shifts chain h_ready scaled dinv_ready deg_root")
        x_out, z_out, u_out = ([p.sem(f"{s}{h}") for h in range(2)] for s in ("x_out", "z_out", "u_out"))
        block = ctx.enter_context(nc.Block())

        @block.sync
        def _(sp):
            with sp.Fori(0, GSTEPS) as i:
                for h in range(2):
                    n = 2 * i + h
                    store_group(sp, xh_tab, n, group(agg, n)).then_inc(x_out[h], 16)
                for h in range(2):
                    n = 2 * i + h
                    sp.wait_ge(h_ready, n + 1)
                    store_group(sp, z_tab, n, hb[:, h, :]).then_inc(z_out[h], 16)
                    sp.wait_ge(scaled, n + 1)
                    store_group(sp, h_tab, n, group(agg, n)).then_inc(u_out[h], 16)
            for h in range(2):
                for s in (x_out, z_out, u_out):
                    sp.wait_ge(s[h], 16 * GSTEPS)

        @block.vector
        def _(dve):
            c = Links(dve, chain, 8)
            dve.wait_ge(deg_root, 1)
            nc.vector.reciprocal(dinv[:, :], dinv[:, :]).then_inc(dinv_ready, 1)

            def body(i, first):
                c.step(i)
                for h in range(2):
                    n = 2 * i + h
                    if not first or h:
                        dve.wait_ge(h_ready, n)
                    norm_stats(nc, c, lambda k: agg[:, bass.ds(n * GC + k * D, D)], st, small, eps_col,
                               std_ready, roots, n).then_inc(shifts, 1)
                c.done()
            peel_first(dve, GSTEPS, body)

        @block.scalar
        def _(act):
            nc.scalar.activation(dinv[:, :], deg[:, :], ACT.Sqrt, bias=1.0).then_inc(deg_root, 1)

            def body(i, first):
                for h in range(2):
                    n = 2 * i + h
                    if not first:
                        act.wait_ge(z_out[h], 16 * i)
                        act.wait_ge(scaled, n - 1)
                    norm_apply(nc, act, lambda k: agg[:, bass.ds(n * GC + k * D, D)], small, eps_col,
                               lambda k: hb[:, h, k * D:(k + 1) * D], std_ready, roots, shifts,
                               n).then_inc(h_ready, 1)
            peel_first(act, GSTEPS, body)

        @block.gpsimd
        def _(pool):
            pool.wait_ge(dinv_ready, 1)

            def body(i, first):
                for h in range(2):
                    n = 2 * i + h
                    pool.wait_ge(h_ready, n + 1)
                    pool.wait_ge(x_out[h], 16 * (i + 1))
                    nc.gpsimd.tensor_tensor(rows_of(group(agg, n)), rows_of(hb[:, h, :]), per_row(dinv, n),
                                            ALU.mult).then_inc(scaled, 1)
            peel_first(pool, GSTEPS, body)


def per_row(dinv, n):
    return dinv[:, bass.ds(n * GB, GB)].unsqueeze(2).to_broadcast([P, GB, D])


def gcn_nodes(nc, layer, agg, dinv, h_tab, z_tab, xh_tab, W_gcn, b_gcn, ident, ones, out):
    end = layer == LAYERS - 1
    with ExitStack() as ctx:
        ctx.enter_context(nc.cleanup_on_exit())
        p = Pass(nc, ctx, f"gn{layer}")
        v = p.sb("v", [P, GC])
        vT = p.sb("vT", [P, GB // 2, P])
        w = p.sb("w", [P, 2, P])
        brow = p.sb("brow", [1, 2, P])
        ex = p.sb("ex", [P, GB, D])
        ax = p.sb("ax", [P, GB, D])
        zi = p.sb("zi", [P, 2, GC])
        zo = p.sb("zo", [P, 2, GC])
        xi = p.sb("xi", [P, 2, GC])
        ps_t = p.ps("ps_t", [P, 8, P])
        ps_g = p.ps("ps_g", [P, 16, P])
        zeroed, w_in, v_ready, turned, copied, mixed, gate_ready, chain, z_ready, scaled = p.sems(
            "zeroed w_in v_ready turned copied mixed gate_ready chain z_ready scaled")
        z_in, x_in, z_out, u_out = ([p.sem(f"{s}{h}") for h in range(2)] for s in ("z_in", "x_in", "z_out", "u_out"))
        block = ctx.enter_context(nc.Block())

        @block.sync
        def _(sp):
            sp.wait_ge(zeroed, 1)
            for a in range(2):
                sp.dma_start(w[a * D:(a + 1) * D, a, :], W_gcn[layer]).then_inc(w_in, 16)
                sp.dma_start(brow[:, a, :], b_gcn[layer:layer + 1, :]).then_inc(w_in, 16)

            def load(i, h):
                n = 2 * i + h
                sp.dma_start(rows_of(zi[:, h, :]), tiles_of(z_tab, n * GB, GB)).then_inc(z_in[h], 16)
                if end:
                    sp.dma_start(rows_of(xi[:, h, :]), tiles_of(xh_tab, n * GB, GB)).then_inc(x_in[h], 16)

            def store(i, h):
                n = 2 * i + h
                sp.wait_ge(scaled, n + 1)
                if not end:
                    store_group(sp, z_tab, n, zo[:, h, :]).then_inc(z_out[h], 16)
                    store_group(sp, h_tab, n, group(agg, n)).then_inc(u_out[h], 16)
                elif isinstance(n, int) and n == 2 * GSTEPS - 1:
                    left = FULL - n * GB
                    rows = rows_of(zo[:, h, :])
                    sp.dma_start(tiles_of(out, n * GB, left), rows[:, 0:left, :]).then_inc(z_out[h], 16)
                    sp.dma_start(out[FULL * P:N, :], rows[0:REST, left, :]).then_inc(u_out[h], 16)
                else:
                    store_group(sp, out, n, zo[:, h, :]).then_inc(z_out[h], 16)
            load_store(sp, GSTEPS, load, store)
            for h in range(2):
                sp.wait_ge(z_out[h], 16 * GSTEPS)
                if not end:
                    sp.wait_ge(u_out[h], 16 * GSTEPS)
            if end:
                sp.wait_ge(u_out[1], 16)

        @block.vector
        def _(dve):
            c = Links(dve, chain, 2)

            def scale(n):
                nc.vector.tensor_tensor(rows_of(v[:, :]), rows_of(group(agg, n)), per_row(dinv, n),
                                        ALU.mult).then_inc(v_ready, 1)

            def body(i, first, last=False):
                c.step(i)
                for h in range(2):
                    n = 2 * i + h
                    if not (last and h):
                        dve.wait_ge(turned, n + 1)
                        scale(n + 1)
                    dve.wait_ge(gate_ready, n + 1)
                    c.link(nc.vector.tensor_tensor(ax[:, :, :], ps_g[:, 0:GB, 0:D], ex[:, :, :], ALU.mult))
                    dve.wait_ge(z_in[h], 16 * (i + 1))
                    if not first:
                        dve.wait_ge(z_out[h], 16 * i)
                        dve.wait_ge(scaled, n - 1)
                    nc.vector.tensor_tensor(rows_of(zo[:, h, :]), ax[:, :, :], rows_of(zi[:, h, :]),
                                            ALU.add).then_inc(z_ready, 1)
                c.done()
            scale(0)
            body(0, True)
            with dve.Fori(1, GSTEPS - 1) as i:
                body(i, False)
            body(GSTEPS - 1, False, True)

        @block.tensor
        def _(pe):
            pe.wait_ge(w_in, 64)

            def body(i, first):
                for h in range(2):
                    n = 2 * i + h
                    pe.wait_ge(v_ready, n + 1)
                    if not first or h:
                        pe.wait_ge(copied, n)
                    for q in range(GB // 2):
                        last = nc.tensor.transpose(ps_t[:, q, :], v[:, q * P:(q + 1) * P], ident[:, :])
                    last.then_inc(turned, 1)
                    pe.wait_ge(copied, n + 1)
                    if not first or h:
                        pe.wait_ge(z_ready, n)
                    for q in range(GB // 2):
                        to = ps_g[:, 2 * q:2 * q + 2, :]
                        nc.tensor.matmul(to, lhsT=vT[:, q, :], rhs=w[:, :, :], start=True, stop=False)
                        last = nc.tensor.matmul(to, lhsT=ones[0:1, :], rhs=brow[:, :, :], start=False, stop=True)
                    last.then_inc(mixed, 1)
            peel_first(pe, GSTEPS, body)

        @block.scalar
        def _(act):
            def body(i, first):
                for h in range(2):
                    n = 2 * i + h
                    act.wait_ge(turned, n + 1)
                    if not first or h:
                        act.wait_ge(mixed, n)
                    nc.scalar.activation(vT[:, 0:BANK, :], ps_t[:, 0:BANK, :], ACT.Copy)
                    nc.scalar.activation(vT[:, BANK:GB // 2, :], ps_t[:, BANK:GB // 2, :],
                                         ACT.Copy).then_inc(copied, 1)
                    act.wait_ge(mixed, n + 1)
                    if not first or h:
                        act.wait_ge(z_ready, n)
                    nc.scalar.activation(ex[:, :, :], ps_g[:, 0:GB, D:P], ACT.Sigmoid).then_inc(gate_ready, 1)
            peel_first(act, GSTEPS, body)

        @block.gpsimd
        def _(pool):
            nc.gpsimd.memset(w[:, :, :], 0.0).then_inc(zeroed, 1)

            def body(i, first):
                for h in range(2):
                    n = 2 * i + h
                    pool.wait_ge(z_ready, n + 1)
                    if end:
                        pool.wait_ge(x_in[h], 16 * (i + 1))
                        nc.gpsimd.tensor_tensor(zo[:, h, :], zo[:, h, :], xi[:, h, :], ALU.add)\
                            .then_inc(scaled, 1)
                    else:
                        nc.gpsimd.tensor_tensor(rows_of(group(agg, n)), rows_of(zo[:, h, :]), per_row(dinv, n),
                                                ALU.mult).then_inc(scaled, 1)
            peel_first(pool, GSTEPS, body)


_INS = ["x", "src", "dst", "edge_attr_10", "edge_attr_32", "edge_type_16", "L0_gnn_W_edge", "L0_gnn_b_edge",
        "L0_gnn_W1", "L0_gnn_b1", "L0_gnn_gamma", "L0_gnn_beta", "L0_gnn_W2", "L0_gnn_b2", "L1_gnn_Wf",
        "L1_gnn_bf", "L1_gnn_Ws", "L1_gnn_bs", "L2_gnn_weight", "L3_gnn_Ws", "L3_gnn_bs"]


def kernel(**inputs):
    import numpy as _np
    import concourse.bacc as _bacc
    from concourse import mybir as _mybir
    from concourse.bass_utils import run_bass_kernel_spmd as _run

    nc = _bacc.Bacc("TRN2", target_bir_lowering=False, num_devices=1)
    arrays, args = {}, []
    for name in _INS:
        a = _np.ascontiguousarray(inputs[name])
        arrays[f"in_{name}"] = a
        args.append(nc.dram_tensor(f"in_{name}", a.shape, _mybir.dt.from_np(a.dtype),
                                   kind="ExternalInput").ap())
    out = nc.dram_tensor("out", (N, D), F32, kind="ExternalOutput").ap()
    build(nc, *args, out)
    r = _run(nc, [arrays], core_ids=[0])
    return r.results[0]["out"]
```

```python
from contextlib import ExitStack

import concourse.bass as bass
from concourse import mybir

F32 = mybir.dt.float32
BF16 = mybir.dt.bfloat16
I32 = mybir.dt.int32
ALU = mybir.AluOpType
ACT = mybir.ActivationFunctionType
AX = mybir.AxisListType

P = 128
D = 64
N = 50000
E = 50000
SB = 7
STEPS = 28
T = SB * 2 * STEPS
NP = T * P
FULL = N // P
REST = N - FULL * P
BANK = 4
W = 2 * P
GB = 14
GSTEPS = T // (2 * GB)
GC = GB * D
LN_EPS = 1e-5
BN_EPS = 1e-5
RELS = 16
EA = 32
EB = 10
LAYERS = 3
WHY = "the table is clamped to the node blocks where it is made"


class Links:

    def __init__(self, eng, sem, per_step):
        self.eng, self.sem, self.per_step, self.at = eng, sem, per_step, 0

    def step(self, i):
        self.i, self.at = i, 0

    def link(self, ins):
        self.at += 1
        ins.then_inc(self.sem, 1)
        self.eng.wait_ge(self.sem, self.i * self.per_step + self.at)

    def done(self):
        assert self.at == self.per_step, (self.at, self.per_step)


def peel_first(eng, n, body):
    body(0, True)
    with eng.Fori(1, n) as i:
        body(i, False)


def staged(eng, stages, steps=STEPS, halves=2):
    lead = len(stages) - 1

    def turn(i, h):
        for s, stage in enumerate(stages):
            ahead = h + lead - s
            at = i + ahead // halves
            if not (isinstance(at, int) and at >= steps):
                stage(at, ahead % halves)
    for m in range(lead):
        for s in range(m + 1):
            stages[s]((m - s) // halves, (m - s) % halves)
    for h in range(halves):
        turn(0, h)
    with eng.Fori(1, steps - 1) as i:
        for h in range(halves):
            turn(i, h)
    for h in range(halves):
        turn(steps - 1, h)


def behind(n, k):
    return not (isinstance(n, int) and n < k)


def tiles_of(dram, first, count):
    return dram[bass.ds(first * P, count * P), :].rearrange("(k p) f -> p k f", p=P)


def load_regs(nc, eng_type, ap, top):
    _, values = nc.values_load_multi_w_load_instructions(
        ap, engines=[eng_type], min_val=0, max_val=top, skip_runtime_bounds_check_because=WHY)
    return values


def build(nc, x, src, dst, ea10, ea32, et, W_edge, b_edge, W1, b1, gamma, beta, W2, b2,
          Wf, bf, Ws, bs, W_rel, W_gcn, b_gcn, out):
    with ExitStack() as whole:
        def scratch(name, shape, dt=F32):
            return nc.dram_tensor(name, shape, dt, kind="Internal").ap()

        h_tab = scratch("h_tab", (NP, D))
        z_tab = scratch("z_tab", (NP, D))
        xh_tab = scratch("xh_tab", (NP, D))
        ea10_s = scratch("ea10_s", (NP, EB))
        ea32_s = scratch("ea32_s", (NP, EA))
        pair_s = scratch("pair_s", (1, NP), I32)

        def keep(name, shape, dt=F32):
            return whole.enter_context(nc.sbuf_tensor(name, shape, dt))

        agg = keep("agg", [P, T * D])
        src_idx = keep("src_idx", [P, T], I32)
        dst_idx = keep("dst_idx", [P, T], I32)
        dst_rel = keep("dst_rel", [P, T])
        win = keep("win", [1, 2 * STEPS * 8], I32)
        win_b = keep("win_b", [1, 2 * STEPS * 8], I32)
        win_m = keep("win_m", [1, 2 * STEPS * 8], I32)
        iota_w = keep("iota_w", [P, W])
        iota_b = keep("iota_b", [P, W], BF16)
        odd = keep("odd", [P, T])
        even = keep("even", [P, T])
        ident = keep("ident", [P, P])
        ones = keep("ones", [P, P])
        ones_b = keep("ones_b", [P, 1], BF16)
        deg = keep("deg", [P, T])
        dinv = keep("dinv", [P, T])
        eps_col = keep("eps_col", [P, 1])

        prologue(nc, src, dst, et, ea10, ea32, ea10_s, ea32_s, pair_s, src_idx, dst_idx, dst_rel, win,
                 win_m, win_b, iota_w, iota_b, ident, ones, ones_b, odd, even, deg, eps_col)
        first_norm(nc, x, agg, h_tab, xh_tab, eps_col)
        gin_edges(nc, h_tab, ea32_s, W_edge, b_edge, agg, src_idx, dst_rel, win, win_m, iota_b, ident)
        gin_nodes(nc, agg, xh_tab, h_tab, W1, b1, gamma, beta, W2, b2, ident, ones, eps_col)
        gated_edges(nc, h_tab, ea10_s, Wf, bf, Ws, bs, agg, deg, src_idx, dst_idx, dst_rel, win, win_m, win_b,
                    iota_b, ident, ones, ones_b)
        norm_nodes(nc, agg, h_tab, eps_col)
        rel_edges(nc, h_tab, pair_s, W_rel, agg, src_idx, dst_rel, win, win_m, iota_b, ident, odd, even)
        gcn_start(nc, agg, deg, dinv, h_tab, z_tab, xh_tab, eps_col)
        with nc.Fori(0, LAYERS - 1) as layer:
            gcn_edges(nc, h_tab, agg, src_idx, dst_rel, win, win_m, iota_w)
            gcn_nodes(nc, layer, agg, dinv, h_tab, z_tab, xh_tab, W_gcn, b_gcn, ident, ones, out)
        gcn_edges(nc, h_tab, agg, src_idx, dst_rel, win, win_m, iota_w, end=True)
        gcn_nodes(nc, LAYERS - 1, agg, dinv, h_tab, z_tab, xh_tab, W_gcn, b_gcn, ident, ones, out, end=True)


def prologue(nc, src, dst, et, ea10, ea32, ea10_s, ea32_s, pair_s, src_idx, dst_idx, dst_rel, win,
             win_m, win_b, iota_w, iota_b, ident, ones, ones_b, odd, even, deg, eps_col):
    C = -(-T // P)
    lasts = T - (C - 1) * P
    with ExitStack() as ctx:
        ctx.enter_context(nc.cleanup_on_exit())
        def sb(name, shape, dt=F32):
            return ctx.enter_context(nc.sbuf_tensor(name, shape, dt))

        def sem(name):
            return nc.alloc_semaphore(name)

        srow = sb("p_srow", [P, C, P], I32)
        drow = sb("p_drow", [P, C, P], I32)
        trow = sb("p_trow", [P, C, P], I32)
        pairs = sb("p_pairs", [P, C, P], I32)
        trowf = sb("p_trowf", [P, C, P])
        srowf = sb("p_srowf", [P, C, P])
        drowf = sb("p_drowf", [P, C, P])
        drelf = sb("p_drelf", [P, C, P])
        lo_i = sb("p_lo_i", [P, C, 2], I32)
        lo_f = sb("p_lo_f", [P, C, 2])
        cols = sb("p_cols", [P, C, 3])
        base = sb("p_base", [P, C])
        rows = sb("p_rows", [1, 3, C * P])
        zero = sb("p_zero", [P, EA * 2])
        ps = [ctx.enter_context(nc.psum_tensor(f"p_ps{k}", [P, C, P], F32)) for k in range(4)]
        ps_r = [ctx.enter_context(nc.psum_tensor(f"p_psr{k}", [P, C, P], F32)) for k in range(3)]
        padded, loaded, consts, made, turned, copied, chain, zeroed, pooled, paired = (
            sem("p_" + s) for s in ("padded", "loaded", "consts", "made", "turned", "copied", "chain",
                                    "zeroed", "pooled", "paired"))
        block = ctx.enter_context(nc.Block())
        pad_rows = NP - E

        @block.sync
        def _(sp):
            sp.dma_start(ea32_s[0:E, :].rearrange("(a b) f -> a (b f)", a=400),
                         ea32.rearrange("(a b) f -> a (b f)", a=400)).then_inc(copied, 16)
            sp.dma_start(ea10_s[0:E, :].rearrange("(a b) f -> a (b f)", a=400),
                         ea10.rearrange("(a b) f -> a (b f)", a=400)).then_inc(copied, 16)
            sp.wait_ge(zeroed, 1)
            sp.dma_start(ea32_s[E:NP, :].rearrange("(a b) f -> a (b f)", b=2),
                         zero[0:pad_rows // 2, 0:2 * EA]).then_inc(copied, 16)
            sp.dma_start(ea10_s[E:NP, :].rearrange("(a b) f -> a (b f)", b=2),
                         zero[0:pad_rows // 2, 0:2 * EB]).then_inc(copied, 16)
            sp.wait_ge(paired, 1)
            for k in range(C):
                many = min(P, T - k * P)
                sp.dma_start(pair_s[0:1, k * P * P:(k * P + many) * P].rearrange("o (t p) -> (o t) p", p=P),
                             pairs[0:many, k, :]).then_inc(copied, 16)
            sp.wait_ge(copied, 16 * (4 + C))

        @block.scalar
        def _(act):
            act.wait_ge(padded, 3)
            for row, dram in ((srow, src), (drow, dst), (trow, et)):
                full = (C - 1) * P
                act.dma_start(row[:, 0:C - 1, :],
                              dram[0:full * P].rearrange("(c t p) -> t c p", t=P, p=P)).then_inc(loaded, 16)
                act.dma_start(row[0:FULL - full, C - 1, :],
                              dram[full * P:FULL * P].rearrange("(t p) -> t p", p=P)).then_inc(loaded, 16)
                act.dma_start(row[FULL - full:FULL - full + 1, C - 1, 0:REST],
                              dram[FULL * P:E].rearrange("(o p) -> o p", o=1)).then_inc(loaded, 16)

        @block.gpsimd
        def _(pool):
            nc.gpsimd.memset(ident[:, :], 0.0).then_inc(pooled, 1)
            nc.gpsimd.iota(iota_w[:, :], [[1, W]], base=0, channel_multiplier=0,
                           allow_small_or_imprecise_dtypes=True).then_inc(pooled, 1)
            pool.wait_ge(pooled, 2)
            nc.gpsimd.affine_select(out=ident[:, :], in_=ident[:, :], compare_op=ALU.not_equal, fill=1.0,
                                    base=0, pattern=[[-1, P]], channel_multiplier=1).then_inc(consts, 1)
            nc.gpsimd.memset(ones[:, :], 1.0)
            nc.gpsimd.memset(deg[:, :], 0.0)
            nc.gpsimd.memset(eps_col[:, :], LN_EPS).then_inc(pooled, 1)
            pool.wait_ge(pooled, 3)

        @block.vector
        def _(dve):
            c = Links(dve, chain, 0)
            c.step(0)
            nc.vector.memset(srow[:, :, :], 0).then_inc(padded, 1)
            nc.vector.memset(drow[:, :, :], -1).then_inc(padded, 1)
            nc.vector.memset(trow[:, :, :], 0).then_inc(padded, 1)
            nc.vector.memset(zero[:, :], 0.0).then_inc(zeroed, 1)
            dve.wait_ge(loaded, 16 * 9)
            dve.wait_ge(pooled, 2)
            nc.vector.tensor_scalar(pairs[:, :, :], trow[:, :, :], 1, None,
                                    ALU.arith_shift_right).then_inc(paired, 1)
            c.link(nc.vector.tensor_scalar(trow[:, :, :], trow[:, :, :], 1, None, ALU.bitwise_and))
            nc.vector.tensor_copy(trowf[:, :, :], trow[:, :, :]).then_inc(made, 1)
            nc.vector.tensor_copy(iota_b[:, :], iota_w[:, :])
            nc.vector.memset(ones_b[:, :], 1.0)
            nc.vector.tensor_copy(srowf[:, :, :], srow[:, :, :]).then_inc(made, 1)
            c.link(nc.vector.tensor_copy(drowf[:, :, :], drow[:, :, :]))
            c.link(nc.vector.tensor_scalar(drelf[:, :, :], drowf[:, :, :], 0.0, float(NP), ALU.is_lt, ALU.mult))
            c.link(nc.vector.tensor_tensor(drelf[:, :, :], drelf[:, :, :], drowf[:, :, :], ALU.add))
            c.link(nc.vector.tensor_reduce(lo_i[:, :, 0], drelf[:, :, :], AX.X, ALU.min))
            c.link(nc.vector.tensor_reduce(lo_i[:, :, 1], drowf[:, :, :], AX.X, ALU.max))
            c.link(nc.vector.tensor_scalar(lo_i[:, :, :], lo_i[:, :, :], 7, None, ALU.arith_shift_right))
            c.link(nc.vector.tensor_copy(lo_f[:, :, :], lo_i[:, :, :]))
            c.link(nc.vector.tensor_scalar(cols[:, :, 2], lo_f[:, :, 0], 0.0, float(T - 2), ALU.max, ALU.min))
            c.link(nc.vector.tensor_scalar(cols[:, :, 0], cols[:, :, 2], float(D), None, ALU.mult))
            c.link(nc.vector.tensor_scalar(base[:, :], cols[:, :, 2], float(P), None, ALU.mult))
            c.link(nc.vector.tensor_tensor(cols[:, :, 1], lo_f[:, :, 1], cols[:, :, 2], ALU.subtract))
            c.link(nc.vector.tensor_scalar(cols[:, :, 1], cols[:, :, 1], -1.0, 0.0, ALU.add, ALU.max))
            for k in range(C):
                last = nc.vector.tensor_scalar(drelf[:, k, :], drowf[:, k, :], base[:, k:k + 1], None,
                                               ALU.subtract)
            last.then_inc(made, 1)
            dve.wait_ge(turned, 1)
            nc.vector.tensor_copy(src_idx[:, :], ps[0][:, :, :].rearrange("p c t -> p (c t)")[:, 0:T])
            nc.vector.tensor_scalar(dst_idx[:, :], ps[1][:, :, :].rearrange("p c t -> p (c t)")[:, 0:T],
                                    0.0, None, ALU.max)
            nc.vector.tensor_copy(dst_rel[:, :], ps[2][:, :, :].rearrange("p c t -> p (c t)")[:, 0:T])
            by_tile = ps[3][:, :, :].rearrange("p c t -> p (c t)")[:, 0:T]
            nc.vector.tensor_copy(odd[:, :], by_tile)
            nc.vector.tensor_scalar(even[:, :], by_tile, -1.0, 1.0, ALU.mult, ALU.add)
            for k in range(3):
                last = nc.vector.tensor_copy(rows[:, k, :], ps_r[k][0:1, :, :].rearrange("p c t -> p (c t)"))
            c.link(last)
            halves = [rows[:, k, 0:T].rearrange("p (n j) -> p n j", j=SB) for k in range(3)]
            w8 = win[:, :].rearrange("p (n j) -> p n j", j=8)
            wb8 = win_b[:, :].rearrange("p (n j) -> p n j", j=8)
            wm8 = win_m[:, :].rearrange("p (n j) -> p n j", j=8)
            nc.vector.tensor_copy(wm8[:, :, 0:SB], halves[1])
            nc.vector.tensor_copy(w8[:, :, 0:SB], halves[0])
            c.link(nc.vector.tensor_reduce(w8[:, :, SB], halves[1], AX.X, ALU.max))
            nc.vector.tensor_copy(wb8[:, :, 0:SB], halves[2])
            c.link(nc.vector.tensor_copy(wb8[:, :, SB], w8[:, :, SB]))

        @block.tensor
        def _(pe):
            pe.wait_ge(consts, 1)
            pe.wait_ge(made, 3)
            pe.wait_ge(chain, 13)
            for k in range(C):
                for to, frm in zip(ps, (srowf, drowf, drelf, trowf)):
                    nc.tensor.transpose(to[:, k, :], frm[:, k, :], ident[:, :])
                for q in range(3):
                    last = nc.tensor.transpose(ps_r[q][0:1, k, :], cols[:, k, q:q + 1], ident[:, :])
            last.then_inc(turned, 1)


def gather_pass(nc, pool, tag, tables, idx_small, ring, wait_used, landed, idx_ready, steps=STEPS, halves=2):
    count = pool.alloc_register(f"{tag}_halves")
    pool.reg_mov(count, 1)

    def body(i, first):
        for h in range(halves):
            n = halves * i + h
            if not first:
                wait_used(i, h)
            for s, (_, index, _) in enumerate(tables):
                last = nc.gpsimd.tensor_copy(idx_small[:, s, h, :], index[:, bass.ds(n * SB, SB)])
            last.then_inc(idx_ready, 1)
            pool.wait_ge(idx_ready, pool.snap(count))
            pool.reg_add(count, count, 1)
            for j in range(SB):
                for s, (dram, _, slot) in enumerate(tables):
                    pool.indirect_dma_start(
                        out=ring(h, j, slot), out_offset=None, in_=dram[:, :],
                        in_offset=bass.IndirectOffsetOnAxis(ap=idx_small[:, s, h, j:j + 1], axis=0),
                    ).then_inc(landed[h], 16)
    peel_first(pool, steps, body)


class Sums:

    def __init__(self, nc, ctx, tag, agg, dst_rel, win, win_m, iota, parts, deg=None, win_b=None, ones=None):
        def sem(name):
            return nc.alloc_semaphore(f"{tag}_{name}")

        def sb(name, shape, dt=F32):
            return ctx.enter_context(nc.sbuf_tensor(f"{tag}_{name}", shape, dt))
        self.nc, self.tag, self.agg, self.dst_rel, self.iota = nc, tag, agg, dst_rel, iota
        self.win, self.win_m = win, win_m
        self.deg, self.win_b, self.ones = deg, win_b, ones
        dt = BF16 if parts else F32
        self.S = sb("S", [P, 2, SB, W], dt)
        self.Sx = sb("Sx", [P, P], dt)
        self.relx = sb("relx", [P, SB])
        if parts:
            self.msg = sb("msg", [P, 2, SB, D])
            self.rest = sb("rest", [P, SB, D])
            self.parts = sb("parts", [P, 2, 3, SB, D], BF16)
            self.msg_ready, self.high, self.split, self.parts_ready = (
                sem(x) for x in ("msg_ready", "high", "split", "parts_ready"))
        self.ps = ctx.enter_context(nc.psum_tensor(f"{tag}_ps_sum", [P, 8, 2, D], F32))
        self.ps_x = ctx.enter_context(nc.psum_tensor(f"{tag}_ps_x", [P, 512], F32))
        self.count = {}
        self.member_ready, self.summed, self.added, self.x_ready, self.x_summed, self.x_chain, self.counted, \
            self.deg_summed, self.half_done = (
                sem(x) for x in ("member_ready", "summed", "added", "x_ready", "x_summed", "x_chain",
                                 "counted", "deg_summed", "half_done"))
        self.tick = sb("tick", [1, 1])

    def start(self, eng, name):
        self.count[name] = eng.alloc_register(f"{self.tag}_{name}")
        eng.reg_mov(self.count[name], 1)

    def wait_next(self, eng, sem, name):
        r = self.count[name]
        eng.wait_ge(sem, eng.snap(r))
        eng.reg_add(r, r, 1)

    def within(self, dve, at, top):
        r = self.count["place"]
        dve.reg_alu(r, at, top, op=ALU.min)
        return dve.snap(r, min_val=0, max_val=top)

    def vector_members(self, dve, n, h):
        for j in range(SB):
            self.nc.vector.tensor_scalar(self.S[:, h % 2, j, :], self.iota[:, :],
                                         self.dst_rel[:, bass.ds(n * SB + j, 1)], None,
                                         ALU.is_equal).then_inc(self.member_ready, 1)

    def scalar_high(self, act, n, h):
        act.wait_ge(self.msg_ready, n + 1)
        if behind(n, 2):
            act.wait_ge(self.half_done, n - 1)
        self.nc.scalar.activation(self.parts[:, h, 0, :, :], self.msg[:, h, :, :], ACT.Copy)\
            .then_inc(self.high, 1)

    def vector_split(self, dve, n, h):
        high, mid, low = (self.parts[:, h, q, :, :] for q in range(3))
        dve.wait_ge(self.high, n + 1)
        self.nc.vector.tensor_tensor(self.rest[:, :, :], self.msg[:, h, :, :], high, ALU.subtract)\
            .then_inc(self.split, 1)
        dve.wait_ge(self.split, 2 * n + 1)
        self.nc.vector.tensor_copy(mid, self.rest[:, :, :]).then_inc(self.split, 1)
        dve.wait_ge(self.split, 2 * n + 2)
        self.nc.vector.tensor_tensor(low, self.rest[:, :, :], mid, ALU.subtract).then_inc(self.parts_ready, 1)

    def tensor_sum(self, pe, n, h, msgs):
        nc = self.nc
        S = self.S[:, h % 2, :, :]
        for j in range(SB):
            pe.wait_ge(self.member_ready, n * SB + j + 1)
            if j in (0, BANK) and behind(n, 1):
                pe.wait_ge(self.added, (n - 1) * SB + min(j + BANK, SB))
            rhs = msgs(j)
            for w in range(2):
                for q, part in enumerate(rhs):
                    last = nc.tensor.matmul(self.ps[:, j, w, :], lhsT=S[:, j, w * P:(w + 1) * P],
                                            rhs=part, start=q == 0, stop=q == len(rhs) - 1)
            last.then_inc(self.summed, 1)
        if self.deg is not None:
            if behind(n, 1):
                pe.wait_ge(self.half_done, n)
            for j in range(SB):
                for w in range(2):
                    at = 128 + 2 * j + w
                    last = nc.tensor.matmul(self.ps_x[:, at:at + 1], lhsT=S[:, j, w * P:(w + 1) * P],
                                            rhs=self.ones[:, 0:1], start=True, stop=True)
            last.then_inc(self.deg_summed, 1)
        (more,) = load_regs(nc, mybir.EngineType.PE, self.win[0:1, bass.ds(n * 8 + SB, 1)], T)
        with pe.If(more > 0):
            further = load_regs(nc, mybir.EngineType.PE, self.win_m[0:1, bass.ds(n * 8, SB)], T)
            for j in range(SB):
                with pe.If(further[j] > 0):
                    with pe.Fori(0, further[j]) as _:
                        self.wait_next(pe, self.x_ready, "pe")
                        rhs = msgs(j)
                        for q, part in enumerate(rhs):
                            last = nc.tensor.matmul(self.ps_x[:, 0:D], lhsT=self.Sx[:, :], rhs=part,
                                                    start=q == 0, stop=q == len(rhs) - 1)
                        if self.deg is not None:
                            last = nc.tensor.matmul(self.ps_x[:, 64:65], lhsT=self.Sx[:, :],
                                                    rhs=self.ones[:, 0:1], start=True, stop=True)
                        last.then_inc(self.x_summed, 1)

    def tensor_sum_parts(self, pe, n, h):
        pe.wait_ge(self.parts_ready, n + 1)
        self.tensor_sum(pe, n, h, lambda j: [self.parts[:, h, q, j, :] for q in range(3)])

    def vector_add(self, dve, n):
        nc = self.nc
        DVE = mybir.EngineType.DVE
        regs = load_regs(nc, DVE, self.win[0:1, bass.ds(n * 8, 8)], (T - 2) * D)
        if self.deg is not None:
            blocks = load_regs(nc, DVE, self.win_b[0:1, bass.ds(n * 8, 8)], T - 2)
        for j in range(SB):
            if j in (0, BANK):
                dve.wait_ge(self.summed, n * SB + min(j + BANK, SB))
            if not (isinstance(n, int) and n * SB + j == 0):
                dve.wait_ge(self.added, n * SB + j)
            part = self.agg[:, bass.ds(regs[j], 2 * D)]
            nc.vector.tensor_tensor(part, self.ps[:, j, :, :].rearrange("p w f -> p (w f)"), part,
                                    ALU.add).then_inc(self.added, 1)
        if self.deg is not None:
            dve.wait_ge(self.deg_summed, n + 1)
            for j in range(SB):
                if not (isinstance(n, int) and n * SB + j == 0):
                    dve.wait_ge(self.counted, n * SB + j)
                part = self.deg[:, bass.ds(blocks[j], 2)]
                nc.vector.tensor_tensor(part, self.ps_x[:, 128 + 2 * j:130 + 2 * j], part,
                                        ALU.add).then_inc(self.counted, 1)
        more = regs[SB]
        with dve.If(more > 0):
            dve.wait_ge(self.added, n * SB + SB)
            if self.deg is not None:
                dve.wait_ge(self.counted, n * SB + SB)

            def link(ins):
                ins.then_inc(self.x_chain, 1)
                self.wait_next(dve, self.x_chain, "link")
            link(nc.vector.tensor_scalar(self.relx[:, :], self.dst_rel[:, bass.ds(n * SB, SB)], -float(P),
                                         None, ALU.add))
            further = load_regs(nc, DVE, self.win_m[0:1, bass.ds(n * 8, SB)], T)
            for j in range(SB):
                with dve.If(further[j] > 0):
                    with dve.Fori(0, further[j]) as w:
                        rel = self.relx[:, j:j + 1]
                        link(nc.vector.tensor_scalar(rel, rel, -float(P), None, ALU.add))
                        nc.vector.tensor_scalar(self.Sx[:, :], self.iota[:, 0:P], rel, None,
                                                ALU.is_equal).then_inc(self.x_ready, 1)
                        self.wait_next(dve, self.x_summed, "dve")
                        part = self.agg[:, bass.ds(self.within(dve, regs[j] + w * D + 2 * D, (T - 1) * D), D)]
                        link(nc.vector.tensor_tensor(part, self.ps_x[:, 0:D], part, ALU.add))
                        if self.deg is not None:
                            part = self.deg[:, bass.ds(self.within(dve, blocks[j] + w + 2, T - 1), 1)]
                            link(nc.vector.tensor_tensor(part, self.ps_x[:, 64:65], part, ALU.add))
        nc.vector.memset(self.tick[:, :], 0.0).then_inc(self.half_done, 1)


def norm_stats(nc, c, x_in, st, small, eps_col, std_ready, roots, n):
    for k in range(GB):
        last = nc.vector.bn_stats(st[:, k, :], x_in(k))
    c.link(last)
    mean2, m2, rstd, shift, dif = (small[:, s, :] for s in range(5))
    nc.vector.tensor_tensor(mean2, st[:, :, 1], st[:, :, 4], ALU.add)
    nc.vector.tensor_tensor(dif, st[:, :, 1], st[:, :, 4], ALU.subtract)
    c.link(nc.vector.tensor_tensor(m2, st[:, :, 2], st[:, :, 5], ALU.add))
    c.link(nc.vector.tensor_tensor(dif, dif, dif, ALU.mult))
    nc.vector.scalar_tensor_tensor(out=m2, in0=dif, scalar=D / 4.0, in1=m2, op0=ALU.mult,
                                   op1=ALU.add).then_inc(std_ready, 1)
    c.eng.wait_ge(roots, n + 1)
    c.link(nc.vector.reciprocal(rstd, rstd))
    return nc.vector.scalar_tensor_tensor(out=shift, in0=mean2, scalar=-0.5, in1=rstd, op0=ALU.mult,
                                          op1=ALU.mult)


def norm_apply(nc, act, x_in, small, eps_col, to, std_ready, roots, shifts, n):
    act.wait_ge(std_ready, n + 1)
    nc.scalar.activation(small[:, 2, :], small[:, 1, :], ACT.Sqrt, bias=eps_col[:, 0:1],
                         scale=1.0 / D).then_inc(roots, 1)
    act.wait_ge(shifts, n + 1)
    for k in range(GB):
        last = nc.scalar.activation(to(k), x_in(k), ACT.Relu, bias=small[:, 3, k:k + 1],
                                    scale=small[:, 2, k:k + 1])
    return last


class Pass:

    def __init__(self, nc, ctx, tag):
        self.nc, self.ctx, self.tag = nc, ctx, tag

    def sb(self, name, shape, dt=F32):
        return self.ctx.enter_context(self.nc.sbuf_tensor(f"{self.tag}_{name}", shape, dt))

    def ps(self, name, shape):
        return self.ctx.enter_context(self.nc.psum_tensor(f"{self.tag}_{name}", shape, F32))

    def sem(self, name):
        return self.nc.alloc_semaphore(f"{self.tag}_{name}")

    def sems(self, names):
        return [self.sem(n) for n in names.split()]


def group(agg, n):
    return agg[:, bass.ds(n * GC, GC)]


def rows_of(buf):
    return buf.rearrange("p (k f) -> p k f", f=D)


def store_group(sp, tab, n, buf):
    return sp.dma_start(tiles_of(tab, n * GB, GB), rows_of(buf))


def first_norm(nc, x, agg, h_tab, xh_tab, eps_col):
    with ExitStack() as ctx:
        ctx.enter_context(nc.cleanup_on_exit())
        p = Pass(nc, ctx, "n0")
        xb = p.sb("x", [P, 2, GC])
        xh = p.sb("xh", [P, 2, GC])
        st = p.sb("st", [P, GB, 6])
        small = p.sb("small", [P, 5, GB])
        std_ready, roots, shifts, chain, h_ready, xh_ready = p.sems("std_ready roots shifts chain h_ready xh_ready")
        x_in, xh_out, h_out = ([p.sem(f"{s}{h}") for h in range(2)] for s in ("x_in", "xh_out", "h_out"))
        block = ctx.enter_context(nc.Block())
        full_groups = FULL // GB
        left = FULL - full_groups * GB
        assert full_groups == 2 * GSTEPS - 1

        @block.sync
        def _(sp):
            def load(i, h, first):
                n = 2 * i + h
                if not first:
                    sp.wait_ge(xh_ready, n - 1)
                if isinstance(n, int) and n == full_groups:
                    part = rows_of(xb[:, h, :])
                    sp.dma_start(part[:, 0:left, :], tiles_of(x, n * GB, left)).then_inc(x_in[h], 16)
                    sp.dma_start(part[0:REST, left, :], x[FULL * P:N, :]).then_inc(x_in[h], 16)
                else:
                    sp.dma_start(rows_of(xb[:, h, :]), tiles_of(x, n * GB, GB)).then_inc(x_in[h], 16)

            def store(i, h):
                n = 2 * i + h
                sp.wait_ge(h_ready, n + 1)
                store_group(sp, h_tab, n, group(agg, n)).then_inc(h_out[h], 16)
                sp.wait_ge(xh_ready, n + 1)
                store_group(sp, xh_tab, n, xh[:, h, :]).then_inc(xh_out[h], 16)

            load(0, 0, True)
            load(0, 1, True)
            with sp.Fori(0, GSTEPS - 2) as i:
                for h in range(2):
                    store(i, h)
                    load(i + 1, h, False)
            for i in range(GSTEPS - 2, GSTEPS):
                for h in range(2):
                    store(i, h)
                    if i + 1 < GSTEPS:
                        load(i + 1, h, False)
            for h in range(2):
                sp.wait_ge(h_out[h], 16 * GSTEPS)
                sp.wait_ge(xh_out[h], 16 * GSTEPS)

        def x_landed(eng, i, h):
            eng.wait_ge(x_in[h], 16 * (i + 1) + (16 if isinstance(i, int) and i == GSTEPS - 1 and h else 0))

        def peel_last(eng, body):
            body(0, True)
            with eng.Fori(1, GSTEPS - 1) as i:
                body(i, False)
            body(GSTEPS - 1, False)

        @block.vector
        def _(dve):
            c = Links(dve, chain, 8)

            def body(i, first):
                c.step(i)
                for h in range(2):
                    n = 2 * i + h
                    x_landed(dve, i, h)
                    if not first or h:
                        dve.wait_ge(h_ready, n)
                    norm_stats(nc, c, lambda k: xb[:, h, k * D:(k + 1) * D], st, small, eps_col,
                               std_ready, roots, n).then_inc(shifts, 1)
                c.done()
            peel_last(dve, body)

        @block.scalar
        def _(act):
            def body(i, first):
                for h in range(2):
                    n = 2 * i + h
                    to = group(agg, n)
                    norm_apply(nc, act, lambda k: xb[:, h, k * D:(k + 1) * D], small, eps_col,
                               lambda k: agg[:, bass.ds(n * GC + k * D, D)], std_ready, roots, shifts,
                               n).then_inc(h_ready, 1)
            peel_last(act, body)

        @block.gpsimd
        def _(pool):
            def body(i, first):
                for h in range(2):
                    n = 2 * i + h
                    pool.wait_ge(h_ready, n + 1)
                    if not first:
                        pool.wait_ge(xh_out[h], 16 * i)
                    nc.gpsimd.tensor_tensor(xh[:, h, :], xb[:, h, :], group(agg, n), ALU.add)\
                        .then_inc(xh_ready, 1)
            peel_last(pool, body)


def gcn_edges(nc, h_tab, agg, src_idx, dst_rel, win, win_m, iota_w, end=False):
    HALVES = 4
    steps = 2 * STEPS // HALVES
    with ExitStack() as ctx:
        ctx.enter_context(nc.cleanup_on_exit())
        p = Pass(nc, ctx, "e4" if end else "e3")
        ring = p.sb("ring", [P, HALVES, SB, D])
        idx_small = p.sb("idx", [P, 1, HALVES, SB], I32)
        landed = [p.sem(f"landed{h}") for h in range(HALVES)]
        idx_ready = p.sem("idx_ready")
        sums = Sums(nc, ctx, p.tag, agg, dst_rel, win, win_m, iota_w, parts=False)
        block = ctx.enter_context(nc.Block())

        @block.gpsimd
        def _(pool):
            gather_pass(nc, pool, p.tag, [(h_tab, src_idx, 0)], idx_small, lambda h, j, s: ring[:, h, j, :],
                        lambda i, h: pool.wait_ge(sums.half_done, HALVES * (i - 1) + h + 1), landed, idx_ready,
                        steps, HALVES)

        @block.vector
        def _(dve):
            for name in ("dve", "link", "place"):
                sums.start(dve, name)
            staged(dve, [lambda i, h: sums.vector_members(dve, HALVES * i + h, h),
                         lambda i, h: sums.vector_add(dve, HALVES * i + h)], steps, HALVES)

        @block.tensor
        def _(pe):
            sums.start(pe, "pe")

            def add_up(i, h):
                pe.wait_ge(landed[h], 16 * SB * (i + 1))
                sums.tensor_sum(pe, HALVES * i + h, h, lambda j: [ring[:, h, j, :]])
            staged(pe, [add_up], steps, HALVES)


def gin_edges(nc, h_tab, ea32_s, W_edge, b_edge, agg, src_idx, dst_rel, win, win_m, iota_b, ident):
    K1 = EA + 1
    PACK = 3
    packs = [(q * PACK, min(PACK, SB - q * PACK)) for q in range(-(-SB // PACK))]
    with ExitStack() as ctx:
        ctx.enter_context(nc.cleanup_on_exit())
        p = Pass(nc, ctx, "e0")
        ring = p.sb("ring", [P, 2, SB, D])
        idx_small = p.sb("idx", [P, 1, 2, SB], I32)
        ea = p.sb("ea", [P, 2, SB, K1])
        eaT = p.sb("eaT", [P, 2, len(packs), P])
        w = p.sb("w", [P, PACK, D])
        raw = p.sb("raw", [P, 2, SB, D])
        ps_t = p.ps("ps_t", [P, 4, P])
        ps_e = p.ps("ps_e", [P, 8, D])
        landed, ea_in = ([p.sem(f"{s}{h}") for h in range(2)] for s in ("landed", "ea_in"))
        idx_ready, turned, copied, mixed, raw_ready, cleared, w_in, zeroed = p.sems(
            "idx_ready turned copied mixed raw_ready cleared w_in zeroed")
        sums = Sums(nc, ctx, p.tag, agg, dst_rel, win, win_m, iota_b, parts=True)
        block = ctx.enter_context(nc.Block())

        @block.gpsimd
        def _(pool):
            nc.gpsimd.memset(w[:, :, :], 0.0).then_inc(zeroed, 1)
            nc.gpsimd.memset(ea[:, :, :, EA:K1], 1.0).then_inc(cleared, 1)
            gather_pass(nc, pool, p.tag, [(h_tab, src_idx, 0)], idx_small, lambda h, j, s: ring[:, h, j, :],
                        lambda i, h: pool.wait_ge(raw_ready, 2 * i + h - 1), landed, idx_ready)

        @block.sync
        def _(sp):
            sp.wait_ge(zeroed, 1)
            for q in range(PACK):
                sp.dma_start(w[q * K1:q * K1 + EA, q, :], W_edge[:, :]).then_inc(w_in, 16)
                sp.dma_start(w[q * K1 + EA:(q + 1) * K1, q, :],
                             b_edge.rearrange("(o f) -> o f", o=1)).then_inc(w_in, 16)

            def body(i, first):
                for h in range(2):
                    n = 2 * i + h
                    if not first:
                        sp.wait_ge(turned, n - 1)
                    sp.dma_start(ea[:, h, :, 0:EA], tiles_of(ea32_s, n * SB, SB)).then_inc(ea_in[h], 16)
            peel_first(sp, STEPS, body)

        @block.scalar
        def _(act):
            def copy(i, h):
                n = 2 * i + h
                act.wait_ge(turned, n + 1)
                if behind(n, 2):
                    act.wait_ge(mixed, n - 1)
                for q, (_, many) in enumerate(packs):
                    last = nc.scalar.activation(eaT[0:many * K1, h, q, :], ps_t[0:many * K1, q, :], ACT.Copy)
                last.then_inc(copied, 1)

            def relu(i, h):
                n = 2 * i + h
                act.wait_ge(raw_ready, n + 1)
                nc.scalar.activation(sums.msg[:, h, :, :], raw[:, h, :, :], ACT.Relu).then_inc(sums.msg_ready, 1)
                sums.scalar_high(act, n, h)
            staged(act, [copy, relu])

        @block.tensor
        def _(pe):
            sums.start(pe, "pe")
            pe.wait_ge(w_in, 16 * 2 * PACK)
            pe.wait_ge(cleared, 1)

            def turn(i, h):
                n = 2 * i + h
                pe.wait_ge(ea_in[h], 16 * (i + 1))
                if behind(n, 1):
                    pe.wait_ge(copied, n)
                for q, (t0, many) in enumerate(packs):
                    last = nc.tensor.transpose(
                        ps_t[0:many * K1, q, :],
                        ea[:, h, t0:t0 + many, :].rearrange("p k f -> p (k f)"), ident[:, :])
                last.then_inc(turned, 1)

            def mix(i, h):
                n = 2 * i + h
                pe.wait_ge(copied, n + 1)
                if behind(n, 1):
                    pe.wait_ge(raw_ready, n)
                for j in range(SB):
                    q = j // PACK
                    k = packs[q][1] * K1
                    last = nc.tensor.matmul(ps_e[:, j, :], lhsT=eaT[0:k, h, q, :], rhs=w[0:k, j % PACK, :],
                                            start=True, stop=True)
                last.then_inc(mixed, 1)
            staged(pe, [turn, mix, lambda i, h: sums.tensor_sum_parts(pe, 2 * i + h, h)])

        @block.vector
        def _(dve):
            for name in ("dve", "link", "place"):
                sums.start(dve, name)

            def message(i, h):
                n = 2 * i + h
                dve.wait_ge(landed[h], 16 * SB * (i + 1))
                dve.wait_ge(mixed, n + 1)
                nc.vector.tensor_tensor(raw[:, h, :, :], ps_e[:, 0:SB, :], ring[:, h, :, :],
                                        ALU.add).then_inc(raw_ready, 1)
                sums.vector_members(dve, n, h)
                sums.vector_split(dve, n, h)
            staged(dve, [message, lambda i, h: sums.vector_add(dve, 2 * i + h)])


def gin_nodes(nc, agg, xh_tab, h_tab, W1, b1, gamma, beta, W2, b2, ident, ones, eps_col):
    pads = NP - N
    C0 = (FULL // 2) * P
    assert FULL % 2 == 0 and T - FULL == 2
    with ExitStack() as both:
        p = Pass(nc, both, "m")
        wbd = [p.sb(f"wbd{k}", [P, P]) for k in range(2)]
        cols = p.sb("cols", [P, 3])
        b2row = p.sb("b2row", [1, P])
        scale, shift = p.sb("scale", [P, 1]), p.sb("shift", [P, 1])
        with ExitStack() as ctx:
            ctx.enter_context(nc.cleanup_on_exit())
            p = Pass(nc, ctx, "m1")
            stage = p.sb("stage", [P, 2, GC])
            aT = p.sb("aT", [P, GC])
            stats = p.sb("stats", [P, 4 * GSTEPS, 6])
            mv = p.sb("mv", [P, 2])
            fold = p.sb("fold", [P, P])
            tmp = p.sb("tmp", [P, 8])
            ps_t = p.ps("ps_t", [P, 8, P])
            ps_1 = p.ps("ps_1", [P, 1024])
            ps_f = p.ps("ps_f", [P, 2])
            zeroed, w_in, staged, turned, copied, mixed, biased, chain, folded, rooted, padz = p.sems(
                "zeroed w_in staged turned copied mixed biased chain folded rooted padz")
            block = ctx.enter_context(nc.Block())

            @block.sync
            def _(sp):
                sp.wait_ge(zeroed, 2)
                for a in range(2):
                    half = slice(a * D, (a + 1) * D)
                    for wb, wd in zip(wbd, (W1, W2)):
                        sp.dma_start(wb[half, half], wd[:, :]).then_inc(w_in, 16)
                    for k, vec in enumerate((b1, gamma, beta)):
                        sp.dma_start(cols[half, k:k + 1], vec.rearrange("(f o) -> f o", o=1)).then_inc(w_in, 16)
                    sp.dma_start(b2row[:, half], b2.rearrange("(o f) -> o f", o=1)).then_inc(w_in, 16)
                sp.wait_ge(w_in, 16 * 12)

            @block.gpsimd
            def _(pool):
                nc.gpsimd.memset(wbd[0][:, :], 0.0).then_inc(zeroed, 1)
                nc.gpsimd.memset(wbd[1][:, :], 0.0).then_inc(zeroed, 1)

                def body(i, first):
                    for h in range(2):
                        n = 2 * i + h
                        if not first:
                            pool.wait_ge(turned, n - 1)
                        nc.gpsimd.tensor_copy(stage[:, h, :], group(agg, n)).then_inc(staged, 1)
                peel_first(pool, GSTEPS, body)

            @block.tensor
            def _(pe):
                pe.wait_ge(w_in, 16 * 12)

                def body(i, first):
                    for h in range(2):
                        n = 2 * i + h
                        pe.wait_ge(staged, n + 1)
                        for q in range(GB // 2):
                            last = nc.tensor.transpose(ps_t[:, q, :], stage[:, h, q * P:(q + 1) * P],
                                                       ident[:, :])
                        last.then_inc(turned, 1)
                        pe.wait_ge(copied, n + 1)
                        if not first or h:
                            pe.wait_ge(biased, n)
                        nc.tensor.matmul(ps_1[:, 0:512], lhsT=wbd[0][:, :], rhs=aT[:, 0:512], start=True,
                                         stop=True)
                        nc.tensor.matmul(ps_1[:, 512:GC], lhsT=wbd[0][:, :], rhs=aT[:, 512:GC], start=True,
                                         stop=True).then_inc(mixed, 1)
                peel_first(pe, GSTEPS, body)
                for k in range(2):
                    pe.wait_ge(folded, k + 1)
                    nc.tensor.matmul(ps_f[:, k:k + 1], lhsT=fold[:, :], rhs=tmp[:, k:k + 1], start=True,
                                     stop=True).then_inc(mixed, 1)

            @block.scalar
            def _(act):
                act.wait_ge(w_in, 16 * 12)

                def body(i, first):
                    for h in range(2):
                        n = 2 * i + h
                        act.wait_ge(turned, n + 1)
                        if not first or h:
                            act.wait_ge(mixed, n)
                        nc.scalar.activation(aT[:, 0:512], ps_t[:, 0:4, :].rearrange("p q n -> p (q n)"), ACT.Copy)
                        nc.scalar.activation(aT[:, 512:GC], ps_t[:, 4:7, :].rearrange("p q n -> p (q n)"),
                                             ACT.Copy).then_inc(copied, 1)
                        act.wait_ge(mixed, n + 1)
                        to = group(agg, n)
                        nc.scalar.activation(to, ps_1[:, 0:GC], ACT.Identity,
                                             bias=cols[:, 0:1]).then_inc(biased, 1)
                peel_first(act, GSTEPS, body)
                act.wait_ge(folded, 3)
                nc.scalar.activation(tmp[:, 4:5], tmp[:, 3:4], ACT.Sqrt, bias=eps_col[:, 0:1]).then_inc(rooted, 1)

            @block.vector
            def _(dve):
                def body(i, first):
                    for h in range(2):
                        n = 2 * i + h
                        dve.wait_ge(biased, n + 1)
                        if isinstance(n, int) and n == 2 * GSTEPS - 1:
                            nc.vector.memset(agg[:, C0 + REST:C0 + P], 0.0).then_inc(padz, 1)
                            nc.vector.memset(agg[D:P, C0:C0 + REST], 0.0).then_inc(padz, 1)
                            dve.wait_ge(padz, 2)
                        for s in range(2):
                            nc.vector.bn_stats(stats[:, bass.ds(2 * n + s, 1), :].rearrange("p a s -> p (a s)"),
                                               agg[:, bass.ds(n * GC + s * (GC // 2), GC // 2)])
                body(0, True)
                with dve.Fori(1, GSTEPS - 1) as i:
                    body(i, False)
                body(GSTEPS - 1, False)
                c = Links(dve, chain, 0)
                c.step(0)
                for a in range(2):
                    last = nc.vector.tensor_tensor(fold[:, a * D:(a + 1) * D], ident[:, 0:D], ident[:, D:P],
                                                   ALU.add)
                c.link(last)
                c.link(nc.vector.bn_aggr(mv[:, :], stats[:, :, :].rearrange("p a s -> p (a s)")))
                nc.vector.tensor_copy(tmp[:, 0:1], mv[:, 0:1]).then_inc(folded, 1)
                dve.wait_ge(mixed, 2 * GSTEPS + 1)
                c.link(nc.vector.tensor_scalar(tmp[:, 2:3], ps_f[:, 0:1], 0.5, None, ALU.mult))
                c.link(nc.vector.tensor_tensor(tmp[:, 5:6], mv[:, 0:1], tmp[:, 2:3], ALU.subtract))
                c.link(nc.vector.tensor_tensor(tmp[:, 6:7], tmp[:, 5:6], tmp[:, 5:6], ALU.mult))
                nc.vector.tensor_tensor(tmp[:, 1:2], tmp[:, 6:7], mv[:, 1:2], ALU.add).then_inc(folded, 1)
                dve.wait_ge(mixed, 2 * GSTEPS + 2)
                c.link(nc.vector.tensor_scalar(tmp[:, 7:8], tmp[:, 2:3], NP / N, None, ALU.mult))
                c.link(nc.vector.tensor_tensor(tmp[:, 5:6], tmp[:, 7:8], tmp[:, 7:8], ALU.mult))
                c.link(nc.vector.tensor_scalar(tmp[:, 6:7], ps_f[:, 1:2], 0.5 * NP / N, None, ALU.mult))
                nc.vector.scalar_tensor_tensor(out=tmp[:, 3:4], in0=tmp[:, 5:6], scalar=-pads / NP,
                                               in1=tmp[:, 6:7], op0=ALU.mult, op1=ALU.add).then_inc(folded, 1)
                dve.wait_ge(rooted, 1)
                c.link(nc.vector.reciprocal(tmp[:, 4:5], tmp[:, 4:5]))
                c.link(nc.vector.tensor_tensor(scale[:, :], tmp[:, 4:5], cols[:, 1:2], ALU.mult))
                c.link(nc.vector.tensor_tensor(tmp[:, 5:6], tmp[:, 7:8], scale[:, :], ALU.mult))
                c.link(nc.vector.tensor_tensor(shift[:, :], cols[:, 2:3], tmp[:, 5:6], ALU.subtract))

        with ExitStack() as ctx:
            ctx.enter_context(nc.cleanup_on_exit())
            p = Pass(nc, ctx, "m2")
            y = p.sb("y", [P, 2, GC])
            xh = p.sb("xh", [P, 2, GC])
            x1 = p.sb("x1", [P, 2, GC])
            hb = p.sb("hb", [P, 2, GC])
            st = p.sb("st", [P, GB, 6])
            small = p.sb("small", [P, 5, GB])
            ps_2 = p.ps("ps_2", [P, 8, P])
            std_ready, roots, shifts, chain, y_ready, mixed, x1_ready, h_ready, summed = p.sems(
                "std_ready roots shifts chain y_ready mixed x1_ready h_ready summed")
            xh_in, h_out = ([p.sem(f"{s}{h}") for h in range(2)] for s in ("xh_in", "h_out"))
            block = ctx.enter_context(nc.Block())

            @block.sync
            def _(sp):
                load_store(sp, GSTEPS,
                           lambda i, h: sp.dma_start(rows_of(xh[:, h, :]), tiles_of(xh_tab, (2 * i + h) * GB, GB))
                           .then_inc(xh_in[h], 16),
                           lambda i, h: (sp.wait_ge(h_ready, 2 * i + h + 1),
                                         store_group(sp, h_tab, 2 * i + h, hb[:, h, :]).then_inc(h_out[h], 16)))
                for h in range(2):
                    sp.wait_ge(h_out[h], 16 * GSTEPS)

            @block.scalar
            def _(act):
                def activate(n, h):
                    nc.scalar.activation(y[:, h, :], group(agg, n), ACT.Relu, bias=shift[:, 0:1],
                                         scale=scale[:, 0:1]).then_inc(y_ready, 1)

                def body(i, first, last=False):
                    for h in range(2):
                        n = 2 * i + h
                        if not (last and h):
                            if not first or h:
                                act.wait_ge(mixed, n)
                            activate(n + 1, 1 - h)
                        if not first:
                            act.wait_ge(h_out[h], 16 * i)
                            act.wait_ge(summed, n - 1)
                        norm_apply(nc, act, lambda k: x1[:, h, k * D:(k + 1) * D], small, eps_col,
                                   lambda k: hb[:, h, k * D:(k + 1) * D], std_ready, roots, shifts,
                                   n).then_inc(h_ready, 1)
                activate(0, 0)
                body(0, True)
                with act.Fori(1, GSTEPS - 1) as i:
                    body(i, False)
                body(GSTEPS - 1, False, True)

            @block.tensor
            def _(pe):
                def body(i, first):
                    for h in range(2):
                        n = 2 * i + h
                        pe.wait_ge(y_ready, n + 1)
                        if not first or h:
                            pe.wait_ge(x1_ready, n)
                        for q in range(GB // 2):
                            nc.tensor.matmul(ps_2[:, q, :], lhsT=y[:, h, q * P:(q + 1) * P], rhs=wbd[1][:, :],
                                             start=True, stop=False)
                            last = nc.tensor.matmul(ps_2[:, q, :], lhsT=ones[0:1, :], rhs=b2row[:, :],
                                                    start=False, stop=True)
                        last.then_inc(mixed, 1)
                peel_first(pe, GSTEPS, body)

            @block.vector
            def _(dve):
                c = Links(dve, chain, 8)

                def body(i, first):
                    c.step(i)
                    for h in range(2):
                        n = 2 * i + h
                        dve.wait_ge(mixed, n + 1)
                        dve.wait_ge(xh_in[h], 16 * (i + 1))
                        if not first:
                            dve.wait_ge(summed, n - 1)
                        nc.vector.tensor_tensor(x1[:, h, :], ps_2[:, 0:7, :].rearrange("p q n -> p (q n)"),
                                                xh[:, h, :], ALU.add).then_inc(x1_ready, 1)
                        dve.wait_ge(x1_ready, n + 1)
                        if not first or h:
                            dve.wait_ge(h_ready, n)
                        norm_stats(nc, c, lambda k: x1[:, h, k * D:(k + 1) * D], st, small, eps_col,
                                   std_ready, roots, n).then_inc(shifts, 1)
                peel_first(dve, GSTEPS, body)

            @block.gpsimd
            def _(pool):
                def body(i, first):
                    for h in range(2):
                        n = 2 * i + h
                        pool.wait_ge(h_ready, n + 1)
                        nc.gpsimd.tensor_tensor(group(agg, n), x1[:, h, :], hb[:, h, :], ALU.add)\
                            .then_inc(summed, 1)
                peel_first(pool, GSTEPS, body)


def load_store(sp, steps, load, store, before_load=None):
    load(0, 0)
    load(0, 1)
    with sp.Fori(0, steps - 1) as i:
        for h in range(2):
            store(i, h)
            load(i + 1, h)
    for h in range(2):
        store(steps - 1, h)


def gated_edges(nc, h_tab, ea10_s, Wf, bf, Ws, bs, agg, deg, src_idx, dst_idx, dst_rel, win, win_m, win_b,
                iota_b, ident, ones, ones_b):
    K1 = EB + 1
    K = SB * K1
    with ExitStack() as ctx:
        ctx.enter_context(nc.cleanup_on_exit())
        p = Pass(nc, ctx, "e1")
        ring = p.sb("ring", [P, 2, SB, 2 * D])
        idx_small = p.sb("idx", [P, 2, 2, SB], I32)
        ea = p.sb("ea", [P, 2, SB, K1])
        eaT = p.sb("eaT", [K, P])
        hT = p.sb("hT", [P, SB, P])
        wcat = p.sb("wcat", [P, P])
        wea = p.sb("wea", [K, SB, P])
        small_e = p.sb("small_e", [P, SB, P])
        log_e = p.sb("log_e", [P, SB, P])
        soft = p.sb("soft", [P, SB, P])
        gate = p.sb("gate", [P, SB, D])
        ps_t = p.ps("ps_t", [P, 8, P])
        ps_m = p.ps("ps_m", [P, 8, P])
        landed, ea_in = ([p.sem(f"{s}{h}") for h in range(2)] for s in ("landed", "ea_in"))
        idx_ready, turned, copied, mixed, act_chain, logs_ready, soft_ready, gated, cleared, w_in, zeroed, negated = p.sems(
            "idx_ready turned copied mixed act_chain logs_ready soft_ready gated cleared w_in zeroed negated")
        sums = Sums(nc, ctx, p.tag, agg, dst_rel, win, win_m, iota_b, True, deg, win_b, ones_b)
        block = ctx.enter_context(nc.Block())

        @block.gpsimd
        def _(pool):
            nc.gpsimd.memset(wea[:, :, :], 0.0).then_inc(zeroed, 1)
            nc.gpsimd.memset(ea[:, :, :, EB:K1], 1.0).then_inc(cleared, 1)
            gather_pass(nc, pool, p.tag, [(h_tab, src_idx, 0), (h_tab, dst_idx, 1)], idx_small,
                        lambda h, j, s: ring[:, h, j, s * D:(s + 1) * D],
                        lambda i, h: pool.wait_ge(turned, 2 * i + h - 1), landed, idx_ready)

        @block.sync
        def _(sp):
            sp.wait_ge(zeroed, 1)
            for a, (wd, bd) in enumerate(((Wf, bf), (Ws, bs))):
                half = slice(a * D, (a + 1) * D)
                sp.dma_start(wcat[:, half], wd[0:P, :]).then_inc(w_in, 16)
                for j in range(SB):
                    sp.dma_start(wea[j * K1:j * K1 + EB, j, half], wd[P:P + EB, :]).then_inc(w_in, 16)
                    sp.dma_start(wea[j * K1 + EB:(j + 1) * K1, j, half],
                                 bd.rearrange("(o f) -> o f", o=1)).then_inc(w_in, 16)

            def body(i, first):
                for h in range(2):
                    n = 2 * i + h
                    if not first:
                        sp.wait_ge(turned, n - 1)
                    sp.dma_start(ea[:, h, :, 0:EB], tiles_of(ea10_s, n * SB, SB)).then_inc(ea_in[h], 16)
            peel_first(sp, STEPS, body)

        @block.tensor
        def _(pe):
            sums.start(pe, "pe")
            pe.wait_ge(negated, 2)
            pe.wait_ge(cleared, 1)

            def mix(i, h):
                n = 2 * i + h
                pe.wait_ge(ea_in[h], 16 * (i + 1))
                pe.wait_ge(landed[h], 16 * 2 * SB * (i + 1))
                nc.tensor.transpose(ps_t[0:K, SB, :], ea[:, h, :, :].rearrange("p k f -> p (k f)"), ident[:, :])
                for j in range(SB):
                    last = nc.tensor.transpose(ps_t[:, j, :], ring[:, h, j, :], ident[:, :])
                last.then_inc(turned, 1)
                pe.wait_ge(copied, n + 1)
                if behind(n, 1):
                    pe.wait_ge(soft_ready, n)
                for j in range(SB):
                    nc.tensor.matmul(ps_m[:, j, :], lhsT=hT[:, j, :], rhs=wcat[:, :], start=True, stop=False)
                    last = nc.tensor.matmul(ps_m[:, j, :], lhsT=eaT[:, :], rhs=wea[:, j, :], start=False,
                                            stop=True)
                last.then_inc(mixed, 1)
            staged(pe, [mix, lambda i, h: sums.tensor_sum_parts(pe, 2 * i + h, h)])

        @block.scalar
        def _(act):
            c = Links(act, act_chain, 4)
            act.wait_ge(w_in, 16 * 2 * (1 + 2 * SB))
            nc.scalar.activation(wcat[:, 0:D], wcat[:, 0:D], ACT.Copy, scale=-1.0).then_inc(negated, 1)
            nc.scalar.activation(wea[:, :, 0:D], wea[:, :, 0:D], ACT.Copy, scale=-1.0).then_inc(negated, 1)

            def gates(i, h):
                n = 2 * i + h
                if h == 0:
                    c.step(i)
                act.wait_ge(turned, n + 1)
                nc.scalar.activation(eaT[:, :], ps_t[0:K, SB, :], ACT.Copy)
                nc.scalar.activation(hT[:, 0:BANK, :], ps_t[:, 0:BANK, :], ACT.Copy)
                nc.scalar.activation(hT[:, BANK:SB, :], ps_t[:, BANK:SB, :], ACT.Copy).then_inc(copied, 1)
                act.wait_ge(mixed, n + 1)
                c.link(nc.scalar.activation(small_e[:, :, :], ps_m[:, 0:SB, :], ACT.Abs))
                c.link(nc.scalar.activation(small_e[:, :, :], small_e[:, :, :], ACT.Exp, scale=-1.0))
                nc.scalar.activation(log_e[:, :, :], small_e[:, :, :], ACT.Ln,
                                     bias=ones[:, 0:1]).then_inc(logs_ready, 1)
                act.wait_ge(soft_ready, n + 1)
                nc.scalar.activation(gate[:, :, :], soft[:, :, 0:D], ACT.Exp, scale=-1.0).then_inc(gated, 1)
                sums.scalar_high(act, n, h)
                if h == 1:
                    c.done()
            staged(act, [gates])

        @block.vector
        def _(dve):
            for name in ("dve", "link", "place"):
                sums.start(dve, name)

            def message(i, h):
                n = 2 * i + h
                dve.wait_ge(logs_ready, n + 1)
                nc.vector.scalar_tensor_tensor(out=soft[:, :, :], in0=ps_m[:, 0:SB, :], scalar=0.0,
                                               in1=log_e[:, :, :], op0=ALU.max, op1=ALU.add)\
                    .then_inc(soft_ready, 1)
                sums.vector_members(dve, n, h)
                dve.wait_ge(gated, n + 1)
                nc.vector.tensor_tensor(sums.msg[:, h, :, :], gate[:, :, :], soft[:, :, D:P],
                                        ALU.mult).then_inc(sums.msg_ready, 1)
                sums.vector_split(dve, n, h)
            staged(dve, [message, lambda i, h: sums.vector_add(dve, 2 * i + h)])


def norm_nodes(nc, agg, h_tab, eps_col):
    with ExitStack() as ctx:
        ctx.enter_context(nc.cleanup_on_exit())
        p = Pass(nc, ctx, "n2")
        hb = p.sb("hb", [P, 2, GC])
        st = p.sb("st", [P, GB, 6])
        small = p.sb("small", [P, 5, GB])
        std_ready, roots, shifts, chain, h_ready = p.sems("std_ready roots shifts chain h_ready")
        h_out = [p.sem(f"h_out{h}") for h in range(2)]
        block = ctx.enter_context(nc.Block())

        @block.sync
        def _(sp):
            with sp.Fori(0, GSTEPS) as i:
                for h in range(2):
                    sp.wait_ge(h_ready, 2 * i + h + 1)
                    store_group(sp, h_tab, 2 * i + h, hb[:, h, :]).then_inc(h_out[h], 16)
            for h in range(2):
                sp.wait_ge(h_out[h], 16 * GSTEPS)

        @block.vector
        def _(dve):
            c = Links(dve, chain, 8)

            def body(i, first):
                c.step(i)
                for h in range(2):
                    n = 2 * i + h
                    if not first or h:
                        dve.wait_ge(h_ready, n)
                    norm_stats(nc, c, lambda k: agg[:, bass.ds(n * GC + k * D, D)], st, small, eps_col,
                               std_ready, roots, n).then_inc(shifts, 1)
                c.done()
            peel_first(dve, GSTEPS, body)

        @block.scalar
        def _(act):
            def body(i, first):
                for h in range(2):
                    n = 2 * i + h
                    if not first:
                        act.wait_ge(h_out[h], 16 * i)
                    norm_apply(nc, act, lambda k: agg[:, bass.ds(n * GC + k * D, D)], small, eps_col,
                               lambda k: hb[:, h, k * D:(k + 1) * D], std_ready, roots, shifts,
                               n).then_inc(h_ready, 1)
            peel_first(act, GSTEPS, body)


def rel_edges(nc, h_tab, pair_s, W_rel, agg, src_idx, dst_rel, win, win_m, iota_b, ident, odd, even):
    QUADS = RELS // 4
    parts = ((0, BANK), (BANK, SB))
    with ExitStack() as ctx:
        ctx.enter_context(nc.cleanup_on_exit())
        p = Pass(nc, ctx, "e2")
        ring = p.sb("ring", [P, 2, SB, 2 * D])
        idx_small = p.sb("idx", [P, 1, 2, SB], I32)
        pairs = p.sb("pairs", [P, 2, SB * P], I32)
        hT = p.sb("hT", [P, SB * P])
        kept = p.sb("kept", [P, 2, QUADS, SB * P])
        w = p.sb("w", [P, QUADS, 2 * D])
        pair = p.sb("pair", [P, QUADS])
        own = p.sb("own", [P, 2, SB, D])
        ps_t = p.ps("ps_t", [P, 8, P])
        ps_m = p.ps("ps_m", [P, 8, P])
        landed, t_in = ([p.sem(f"{s}{h}") for h in range(2)] for s in ("landed", "t_in"))
        idx_ready, turned, copied, kept_ready, mixed, picked, w_in, pair_ready, doubled = p.sems(
            "idx_ready turned copied kept_ready mixed picked w_in pair_ready doubled")
        sums = Sums(nc, ctx, p.tag, agg, dst_rel, win, win_m, iota_b, parts=True)
        block = ctx.enter_context(nc.Block())

        @block.gpsimd
        def _(pool):
            for a in range(2):
                nc.gpsimd.iota(pair[a * D:(a + 1) * D, :], [[2, QUADS]], base=a, channel_multiplier=0,
                               allow_small_or_imprecise_dtypes=True).then_inc(pair_ready, 1)
                pool.wait_ge(pair_ready, a + 1)
            gather_pass(nc, pool, p.tag, [(h_tab, src_idx, 0)], idx_small, lambda h, j, s: ring[:, h, j, 0:D],
                        lambda i, h: pool.wait_ge(turned, 2 * i + h - 1), landed, idx_ready)

        @block.sync
        def _(sp):
            for a in range(2):
                for k in range(QUADS):
                    sp.dma_start(w[a * D:(a + 1) * D, k, :].rearrange("i (b o) -> i b o", b=2),
                                 W_rel[4 * k + 2 * a:4 * k + 2 * a + 2, :, :].rearrange("b i o -> i b o"))\
                        .then_inc(w_in, 16)

            def body(i, first):
                for h in range(2):
                    n = 2 * i + h
                    if not first:
                        sp.wait_ge(kept_ready, 2 * (n - 1))
                    sp.dma_start(pairs[:, h, :],
                                 pair_s[0:1, bass.ds(n * SB * P, SB * P)].to_broadcast([P, SB * P]))\
                        .then_inc(t_in[h], 16)
            peel_first(sp, STEPS, body)

        @block.tensor
        def _(pe):
            sums.start(pe, "pe")
            pe.wait_ge(w_in, 16 * 2 * QUADS)

            def turn(i, h):
                n = 2 * i + h
                pe.wait_ge(landed[h], 16 * SB * (i + 1))
                pe.wait_ge(doubled, n + 1)
                if behind(n, 1):
                    pe.wait_ge(copied, n)
                for j in range(SB):
                    last = nc.tensor.transpose(ps_t[:, j, :], ring[:, h, j, :], ident[:, :])
                last.then_inc(turned, 1)

            def mix(i, h):
                n = 2 * i + h
                if behind(n, 1):
                    pe.wait_ge(picked, 2 * n)
                for q, (t0, t1) in enumerate(parts):
                    pe.wait_ge(kept_ready, 2 * n + q + 1)
                    for j in range(t0, t1):
                        for k in range(QUADS):
                            last = nc.tensor.matmul(ps_m[:, j, :], lhsT=kept[:, h, k, j * P:(j + 1) * P],
                                                    rhs=w[:, k, :], start=(k == 0), stop=(k == QUADS - 1))
                last.then_inc(mixed, 1)
            staged(pe, [turn, mix, lambda i, h: sums.tensor_sum_parts(pe, 2 * i + h, h)])

        @block.scalar
        def _(act):
            def copy(i, h):
                n = 2 * i + h
                act.wait_ge(landed[h], 16 * SB * (i + 1))
                nc.scalar.activation(ring[:, h, :, D:2 * D], ring[:, h, :, 0:D], ACT.Copy).then_inc(doubled, 1)
                act.wait_ge(turned, n + 1)
                if behind(n, 1):
                    act.wait_ge(kept_ready, 2 * n)
                nc.scalar.activation(hT[:, 0:BANK * P], ps_t[:, 0:BANK, :].rearrange("p q n -> p (q n)"), ACT.Copy)
                nc.scalar.activation(hT[:, BANK * P:SB * P],
                                     ps_t[:, BANK:SB, :].rearrange("p q n -> p (q n)"),
                                     ACT.Copy).then_inc(copied, 1)
            staged(act, [copy, lambda i, h: sums.scalar_high(act, 2 * i + h, h)])

        @block.vector
        def _(dve):
            for name in ("dve", "link", "place"):
                sums.start(dve, name)
            dve.wait_ge(pair_ready, 2)

            def keep(i, h):
                n = 2 * i + h
                dve.wait_ge(t_in[h], 16 * (i + 1))
                dve.wait_ge(copied, n + 1)
                if behind(n, 2):
                    dve.wait_ge(mixed, n - 1)
                for t0, t1 in parts:
                    at = slice(t0 * P, t1 * P)
                    for k in range(QUADS):
                        last = nc.vector.scalar_tensor_tensor(
                            out=kept[:, h, k, at], in0=pairs[:, h, at], scalar=pair[:, k:k + 1],
                            in1=hT[:, at], op0=ALU.is_equal, op1=ALU.mult)
                    last.then_inc(kept_ready, 1)

            def message(i, h):
                n = 2 * i + h
                sums.vector_members(dve, n, h)
                dve.wait_ge(mixed, n + 1)
                for b, mask in enumerate((even, odd)):
                    nc.vector.tensor_tensor(own[:, b, :, :], ps_m[:, 0:SB, b * D:(b + 1) * D],
                                            mask[:, bass.ds(n * SB, SB)].unsqueeze(2).to_broadcast([P, SB, D]),
                                            ALU.mult).then_inc(picked, 1)
                dve.wait_ge(picked, 2 * n + 2)
                nc.vector.tensor_tensor(sums.msg[:, h, :, :], own[:, 0, :, :], own[:, 1, :, :],
                                        ALU.add).then_inc(sums.msg_ready, 1)
                sums.vector_split(dve, n, h)
            staged(dve, [keep, message, lambda i, h: sums.vector_add(dve, 2 * i + h)])


def gcn_start(nc, agg, deg, dinv, h_tab, z_tab, xh_tab, eps_col):
    with ExitStack() as ctx:
        ctx.enter_context(nc.cleanup_on_exit())
        p = Pass(nc, ctx, "n3")
        hb = p.sb("hb", [P, 2, GC])
        st = p.sb("st", [P, GB, 6])
        small = p.sb("small", [P, 5, GB])
        std_ready, roots, shifts, chain, h_ready, scaled, dinv_ready, deg_root = p.sems(
            "std_ready roots shifts chain h_ready scaled dinv_ready deg_root")
        x_out, z_out, u_out = ([p.sem(f"{s}{h}") for h in range(2)] for s in ("x_out", "z_out", "u_out"))
        block = ctx.enter_context(nc.Block())

        @block.sync
        def _(sp):
            with sp.Fori(0, GSTEPS) as i:
                for h in range(2):
                    n = 2 * i + h
                    store_group(sp, xh_tab, n, group(agg, n)).then_inc(x_out[h], 16)
                for h in range(2):
                    n = 2 * i + h
                    sp.wait_ge(h_ready, n + 1)
                    store_group(sp, z_tab, n, hb[:, h, :]).then_inc(z_out[h], 16)
                    sp.wait_ge(scaled, n + 1)
                    store_group(sp, h_tab, n, group(agg, n)).then_inc(u_out[h], 16)
            for h in range(2):
                for s in (x_out, z_out, u_out):
                    sp.wait_ge(s[h], 16 * GSTEPS)

        @block.vector
        def _(dve):
            c = Links(dve, chain, 8)
            dve.wait_ge(deg_root, 1)
            nc.vector.reciprocal(dinv[:, :], dinv[:, :]).then_inc(dinv_ready, 1)

            def body(i, first):
                c.step(i)
                for h in range(2):
                    n = 2 * i + h
                    if not first or h:
                        dve.wait_ge(h_ready, n)
                    norm_stats(nc, c, lambda k: agg[:, bass.ds(n * GC + k * D, D)], st, small, eps_col,
                               std_ready, roots, n).then_inc(shifts, 1)
                c.done()
            peel_first(dve, GSTEPS, body)

        @block.scalar
        def _(act):
            nc.scalar.activation(dinv[:, :], deg[:, :], ACT.Sqrt, bias=1.0).then_inc(deg_root, 1)

            def body(i, first):
                for h in range(2):
                    n = 2 * i + h
                    if not first:
                        act.wait_ge(z_out[h], 16 * i)
                        act.wait_ge(scaled, n - 1)
                    norm_apply(nc, act, lambda k: agg[:, bass.ds(n * GC + k * D, D)], small, eps_col,
                               lambda k: hb[:, h, k * D:(k + 1) * D], std_ready, roots, shifts,
                               n).then_inc(h_ready, 1)
            peel_first(act, GSTEPS, body)

        @block.gpsimd
        def _(pool):
            pool.wait_ge(dinv_ready, 1)

            def body(i, first):
                for h in range(2):
                    n = 2 * i + h
                    pool.wait_ge(h_ready, n + 1)
                    pool.wait_ge(x_out[h], 16 * (i + 1))
                    nc.gpsimd.tensor_tensor(rows_of(group(agg, n)), rows_of(hb[:, h, :]), per_row(dinv, n),
                                            ALU.mult).then_inc(scaled, 1)
            peel_first(pool, GSTEPS, body)


def per_row(dinv, n):
    return dinv[:, bass.ds(n * GB, GB)].unsqueeze(2).to_broadcast([P, GB, D])


def gcn_nodes(nc, layer, agg, dinv, h_tab, z_tab, xh_tab, W_gcn, b_gcn, ident, ones, out, end=False):
    with ExitStack() as ctx:
        ctx.enter_context(nc.cleanup_on_exit())
        p = Pass(nc, ctx, "n5" if end else "n4")
        v = p.sb("v", [P, GC])
        vT = p.sb("vT", [P, 2, GB // 2, P])
        w = p.sb("w", [P, 2, P])
        brow = p.sb("brow", [3, 2, P])
        bpart = p.sb("bpart", [3, 3, 2, P], BF16)
        brest = p.sb("brest", [3, 3, 2, P])
        bias = p.sb("bias", [3, 2, P], BF16)
        ones3 = p.sb("ones3", [3, P], BF16)
        ex = p.sb("ex", [P, GB, D])
        ax = p.sb("ax", [P, GB, D])
        zi = p.sb("zi", [P, 2, GC])
        zo = p.sb("zo", [P, 2, GC])
        xi = p.sb("xi", [P, 2, GC])
        ps_t = p.ps("ps_t", [P, 8, P])
        ps_g = p.ps("ps_g", [P, 16, P])
        zeroed, w_in, v_ready, turned, copied, mixed, gate_ready, taken, z_ready, scaled, bias_chain = p.sems(
            "zeroed w_in v_ready turned copied mixed gate_ready taken z_ready scaled bias_chain")
        z_in, x_in, z_out, u_out = ([p.sem(f"{s}{h}") for h in range(2)] for s in ("z_in", "x_in", "z_out", "u_out"))
        block = ctx.enter_context(nc.Block())

        @block.sync
        def _(sp):
            sp.wait_ge(zeroed, 1)
            for a in range(2):
                sp.dma_start(w[a * D:(a + 1) * D, a, :], W_gcn[bass.ds(layer, 1), :, :].rearrange("o k f -> (o k) f")).then_inc(w_in, 16)
                sp.dma_start(brow[:, a, :], b_gcn[bass.ds(layer, 1), :].to_broadcast([3, P])).then_inc(w_in, 16)

            def load(i, h):
                n = 2 * i + h
                sp.dma_start(rows_of(zi[:, h, :]), tiles_of(z_tab, n * GB, GB)).then_inc(z_in[h], 16)
                if end:
                    sp.dma_start(rows_of(xi[:, h, :]), tiles_of(xh_tab, n * GB, GB)).then_inc(x_in[h], 16)

            def store(i, h):
                n = 2 * i + h
                sp.wait_ge(scaled, n + 1)
                if not end:
                    store_group(sp, z_tab, n, zo[:, h, :]).then_inc(z_out[h], 16)
                    store_group(sp, h_tab, n, group(agg, n)).then_inc(u_out[h], 16)
                elif isinstance(n, int) and n == 2 * GSTEPS - 1:
                    left = FULL - n * GB
                    rows = rows_of(zo[:, h, :])
                    sp.dma_start(tiles_of(out, n * GB, left), rows[:, 0:left, :]).then_inc(z_out[h], 16)
                    sp.dma_start(out[FULL * P:N, :], rows[0:REST, left, :]).then_inc(u_out[h], 16)
                else:
                    store_group(sp, out, n, zo[:, h, :]).then_inc(z_out[h], 16)
            load_store(sp, GSTEPS, load, store)
            for h in range(2):
                sp.wait_ge(z_out[h], 16 * GSTEPS)
                if not end:
                    sp.wait_ge(u_out[h], 16 * GSTEPS)
            if end:
                sp.wait_ge(u_out[1], 16)

        @block.vector
        def _(dve):
            def scale(i, h):
                n = 2 * i + h
                if behind(n, 1):
                    dve.wait_ge(turned, n)
                nc.vector.tensor_tensor(rows_of(v[:, :]), rows_of(group(agg, n)), per_row(dinv, n),
                                        ALU.mult).then_inc(v_ready, 1)

            def state(i, h):
                n = 2 * i + h
                dve.wait_ge(gate_ready, n + 1)
                if behind(n, 1):
                    dve.wait_ge(z_ready, n)
                nc.vector.tensor_tensor(ax[:, :, :], ps_g[:, 0:GB, 0:D], ex[:, :, :],
                                        ALU.mult).then_inc(taken, 1)
                dve.wait_ge(taken, n + 1)
                dve.wait_ge(z_in[h], 16 * (i + 1))
                if behind(n, 2):
                    dve.wait_ge(z_out[h], 16 * i)
                    dve.wait_ge(scaled, n - 1)
                nc.vector.tensor_tensor(rows_of(zo[:, h, :]), ax[:, :, :], rows_of(zi[:, h, :]),
                                        ALU.add).then_inc(z_ready, 1)

            nc.vector.memset(ones3[:, :], 1.0)
            c = Links(dve, bias_chain, 8)
            c.step(0)
            dve.wait_ge(w_in, 64)
            c.link(nc.vector.tensor_copy(bpart[:, 0, :, :], brow[:, :, :]))
            c.link(nc.vector.tensor_tensor(brest[:, 0, :, :], brow[:, :, :], bpart[:, 0, :, :], ALU.subtract))
            c.link(nc.vector.tensor_copy(bpart[:, 1, :, :], brest[:, 0, :, :]))
            c.link(nc.vector.tensor_tensor(bpart[:, 2, :, :], brest[:, 0, :, :], bpart[:, 1, :, :], ALU.subtract))
            c.link(nc.vector.tensor_scalar(brest[:, 1, :, :], bpart[:, 0, :, :], ident[0:3, 0:1], None, ALU.mult))
            c.link(nc.vector.scalar_tensor_tensor(out=brest[:, 2, :, :], in0=bpart[:, 1, :, :],
                                                  scalar=ident[0:3, 1:2], in1=brest[:, 1, :, :],
                                                  op0=ALU.mult, op1=ALU.add))
            c.link(nc.vector.scalar_tensor_tensor(out=bias[:, :, :], in0=bpart[:, 2, :, :],
                                                  scalar=ident[0:3, 2:3], in1=brest[:, 2, :, :],
                                                  op0=ALU.mult, op1=ALU.add))
            staged(dve, [scale, lambda i, h: None, state], GSTEPS)

        @block.tensor
        def _(pe):
            def turn(i, h):
                n = 2 * i + h
                pe.wait_ge(v_ready, n + 1)
                if behind(n, 1):
                    pe.wait_ge(copied, n)
                for q in range(GB // 2):
                    last = nc.tensor.transpose(ps_t[:, q, :], v[:, q * P:(q + 1) * P], ident[:, :])
                last.then_inc(turned, 1)

            def mix(i, h):
                n = 2 * i + h
                pe.wait_ge(copied, n + 1)
                if behind(n, 1):
                    pe.wait_ge(taken, n)
                else:
                    pe.wait_ge(bias_chain, 7)
                for q in range(GB // 2):
                    to = ps_g[:, 2 * q:2 * q + 2, :]
                    nc.tensor.matmul(to, lhsT=vT[:, h, q, :], rhs=w[:, :, :], start=True, stop=False)
                    last = nc.tensor.matmul(to, lhsT=ones3[:, :], rhs=bias[:, :, :], start=False, stop=True)
                last.then_inc(mixed, 1)
            pe.wait_ge(w_in, 64)
            staged(pe, [turn, mix], GSTEPS)

        @block.scalar
        def _(act):
            def copy(i, h):
                n = 2 * i + h
                act.wait_ge(turned, n + 1)
                if behind(n, 2):
                    act.wait_ge(mixed, n - 1)
                nc.scalar.activation(vT[:, h, 0:BANK, :], ps_t[:, 0:BANK, :], ACT.Copy)
                nc.scalar.activation(vT[:, h, BANK:GB // 2, :], ps_t[:, BANK:GB // 2, :],
                                     ACT.Copy).then_inc(copied, 1)

            def gates(i, h):
                n = 2 * i + h
                act.wait_ge(mixed, n + 1)
                if behind(n, 1):
                    act.wait_ge(taken, n)
                nc.scalar.activation(ex[:, :, :], ps_g[:, 0:GB, D:P], ACT.Sigmoid).then_inc(gate_ready, 1)
            staged(act, [copy, gates], GSTEPS)

        @block.gpsimd
        def _(pool):
            nc.gpsimd.memset(w[:, :, :], 0.0).then_inc(zeroed, 1)

            def body(i, first):
                for h in range(2):
                    n = 2 * i + h
                    pool.wait_ge(z_ready, n + 1)
                    if end:
                        pool.wait_ge(x_in[h], 16 * (i + 1))
                        nc.gpsimd.tensor_tensor(zo[:, h, :], zo[:, h, :], xi[:, h, :], ALU.add)\
                            .then_inc(scaled, 1)
                    else:
                        nc.gpsimd.tensor_tensor(rows_of(group(agg, n)), rows_of(zo[:, h, :]), per_row(dinv, n),
                                                ALU.mult).then_inc(scaled, 1)
            peel_first(pool, GSTEPS, body)


_INS = ["x", "src", "dst", "edge_attr_10", "edge_attr_32", "edge_type_16", "L0_gnn_W_edge", "L0_gnn_b_edge",
        "L0_gnn_W1", "L0_gnn_b1", "L0_gnn_gamma", "L0_gnn_beta", "L0_gnn_W2", "L0_gnn_b2", "L1_gnn_Wf",
        "L1_gnn_bf", "L1_gnn_Ws", "L1_gnn_bs", "L2_gnn_weight", "L3_gnn_Ws", "L3_gnn_bs"]


def kernel(**inputs):
    import numpy as _np
    import concourse.bacc as _bacc
    from concourse import mybir as _mybir
    from concourse.bass_utils import run_bass_kernel_spmd as _run

    nc = _bacc.Bacc("TRN2", target_bir_lowering=False, num_devices=1)
    arrays, args = {}, []
    for name in _INS:
        a = _np.ascontiguousarray(inputs[name])
        arrays[f"in_{name}"] = a
        args.append(nc.dram_tensor(f"in_{name}", a.shape, _mybir.dt.from_np(a.dtype),
                                   kind="ExternalInput").ap())
    out = nc.dram_tensor("out", (N, D), F32, kind="ExternalOutput").ap()
    build(nc, *args, out)
    r = _run(nc, [arrays], core_ids=[0])
    return r.results[0]["out"]
```

```python
from contextlib import ExitStack

import concourse.bass as bass
from concourse import mybir

F32 = mybir.dt.float32
BF16 = mybir.dt.bfloat16
I32 = mybir.dt.int32
ALU = mybir.AluOpType
ACT = mybir.ActivationFunctionType
AX = mybir.AxisListType

P = 128
D = 64
N = 50000
E = 50000
SB = 7
STEPS = 28
T = SB * 2 * STEPS
NP = T * P
FULL = N // P
REST = N - FULL * P
BANK = 4
W = 2 * P
GB = 14
DEEP = 4
GSTEPS = T // (2 * GB)
GC = GB * D
LN_EPS = 1e-5
BN_EPS = 1e-5
RELS = 16
EA = 32
EB = 10
LAYERS = 3
WHY = "the table is clamped to the node blocks where it is made"


class Links:

    def __init__(self, eng, sem, per_step):
        self.eng, self.sem, self.per_step, self.at = eng, sem, per_step, 0

    def step(self, i):
        self.i, self.at = i, 0

    def link(self, ins):
        self.at += 1
        ins.then_inc(self.sem, 1)
        self.eng.wait_ge(self.sem, self.i * self.per_step + self.at)

    def done(self):
        assert self.at == self.per_step, (self.at, self.per_step)


def peel_first(eng, n, body):
    body(0, True)
    with eng.Fori(1, n) as i:
        body(i, False)


def staged(eng, stages, steps=STEPS, halves=2):
    lead = max(lag for lag, _ in stages)

    def turn(i, h):
        for lag, stage in stages:
            ahead = h + lead - lag
            at = i + ahead // halves
            if not (isinstance(at, int) and at >= steps):
                stage(at, ahead % halves)
    for m in range(lead):
        for lag, stage in stages:
            if lag <= m:
                stage((m - lag) // halves, (m - lag) % halves)
    for h in range(halves):
        turn(0, h)
    with eng.Fori(1, steps - 1) as i:
        for h in range(halves):
            turn(i, h)
    for h in range(halves):
        turn(steps - 1, h)


def behind(n, k):
    return not (isinstance(n, int) and n < k)


def tiles_of(dram, first, count):
    return dram[bass.ds(first * P, count * P), :].rearrange("(k p) f -> p k f", p=P)


def load_regs(nc, eng_type, ap, top):
    _, values = nc.values_load_multi_w_load_instructions(
        ap, engines=[eng_type], min_val=0, max_val=top, skip_runtime_bounds_check_because=WHY)
    return values


def build(nc, x, src, dst, ea10, ea32, et, W_edge, b_edge, W1, b1, gamma, beta, W2, b2,
          Wf, bf, Ws, bs, W_rel, W_gcn, b_gcn, out):
    with ExitStack() as whole:
        def scratch(name, shape, dt=F32):
            return nc.dram_tensor(name, shape, dt, kind="Internal").ap()

        h_tab = scratch("h_tab", (NP, D))
        xh_tab = scratch("xh_tab", (NP, D))
        ea10_s = scratch("ea10_s", (NP, EB))
        ea32_s = scratch("ea32_s", (NP, EA))
        pair_s = scratch("pair_s", (1, NP), I32)

        def keep(name, shape, dt=F32):
            return whole.enter_context(nc.sbuf_tensor(name, shape, dt))

        agg = keep("agg", [P, T * D])
        src_idx = keep("src_idx", [P, T], I32)
        dst_idx = keep("dst_idx", [P, T], I32)
        dst_rel = keep("dst_rel", [P, T])
        win = keep("win", [1, 2 * STEPS * 8], I32)
        win_b = keep("win_b", [1, 2 * STEPS * 8], I32)
        win_m = keep("win_m", [1, 2 * STEPS * 8], I32)
        iota_w = keep("iota_w", [P, W])
        iota_b = keep("iota_b", [P, W], BF16)
        odd = keep("odd", [P, T])
        even = keep("even", [P, T])
        ident = keep("ident", [P, P])
        ones = keep("ones", [P, P])
        ones_b = keep("ones_b", [P, 1], BF16)
        deg = keep("deg", [P, T])
        root = keep("root", [P, T])
        dinv = keep("dinv", [P, T])
        eps_col = keep("eps_col", [P, 1])

        prologue(nc, src, dst, et, ea10, ea32, ea10_s, ea32_s, pair_s, src_idx, dst_idx, dst_rel, win,
                 win_m, win_b, iota_w, iota_b, ident, ones, ones_b, odd, even, deg, eps_col)
        first_norm(nc, x, agg, h_tab, xh_tab, eps_col)
        gin_edges(nc, h_tab, ea32_s, W_edge, b_edge, agg, src_idx, dst_rel, win, win_m, iota_b, ident)
        gin_nodes(nc, agg, xh_tab, h_tab, W1, b1, gamma, beta, W2, b2, ident, ones, eps_col)
        gated_edges(nc, h_tab, ea10_s, Wf, bf, Ws, bs, agg, deg, src_idx, dst_idx, dst_rel, win, win_m, win_b,
                    iota_b, ident, ones, ones_b)
        norm_nodes(nc, agg, h_tab, eps_col)
        rel_edges(nc, h_tab, pair_s, W_rel, agg, src_idx, dst_rel, win, win_m, iota_b, ident, odd, even)
        gcn_start(nc, agg, deg, root, dinv, h_tab, xh_tab, eps_col)
        with nc.Fori(0, LAYERS - 1) as layer:
            gcn_edges(nc, h_tab, agg, src_idx, dst_rel, win, win_m, iota_w)
            gcn_nodes(nc, layer, agg, root, dinv, h_tab, xh_tab, W_gcn, b_gcn, ident, ones, out)
        gcn_edges(nc, h_tab, agg, src_idx, dst_rel, win, win_m, iota_w, end=True)
        gcn_nodes(nc, LAYERS - 1, agg, root, dinv, h_tab, xh_tab, W_gcn, b_gcn, ident, ones, out, end=True)


def prologue(nc, src, dst, et, ea10, ea32, ea10_s, ea32_s, pair_s, src_idx, dst_idx, dst_rel, win,
             win_m, win_b, iota_w, iota_b, ident, ones, ones_b, odd, even, deg, eps_col):
    C = -(-T // P)
    lasts = T - (C - 1) * P
    with ExitStack() as ctx:
        ctx.enter_context(nc.cleanup_on_exit())
        def sb(name, shape, dt=F32):
            return ctx.enter_context(nc.sbuf_tensor(name, shape, dt))

        def sem(name):
            return nc.alloc_semaphore(name)

        srow = sb("p_srow", [P, C, P], I32)
        drow = sb("p_drow", [P, C, P], I32)
        trow = sb("p_trow", [P, C, P], I32)
        pairs = sb("p_pairs", [P, C, P], I32)
        trowf = sb("p_trowf", [P, C, P])
        srowf = sb("p_srowf", [P, C, P])
        drowf = sb("p_drowf", [P, C, P])
        drelf = sb("p_drelf", [P, C, P])
        lo_i = sb("p_lo_i", [P, C, 2], I32)
        lo_f = sb("p_lo_f", [P, C, 2])
        cols = sb("p_cols", [P, C, 3])
        base = sb("p_base", [P, C])
        rows = sb("p_rows", [1, 3, C * P])
        zero = sb("p_zero", [P, EA * 2])
        ps = [ctx.enter_context(nc.psum_tensor(f"p_ps{k}", [P, C, P], F32)) for k in range(4)]
        ps_r = [ctx.enter_context(nc.psum_tensor(f"p_psr{k}", [P, C, P], F32)) for k in range(3)]
        padded, loaded, consts, made, turned, copied, chain, zeroed, pooled, paired = (
            sem("p_" + s) for s in ("padded", "loaded", "consts", "made", "turned", "copied", "chain",
                                    "zeroed", "pooled", "paired"))
        block = ctx.enter_context(nc.Block())
        pad_rows = NP - E

        @block.sync
        def _(sp):
            sp.dma_start(ea32_s[0:E, :].rearrange("(a b) f -> a (b f)", a=400),
                         ea32.rearrange("(a b) f -> a (b f)", a=400)).then_inc(copied, 16)
            sp.dma_start(ea10_s[0:E, :].rearrange("(a b) f -> a (b f)", a=400),
                         ea10.rearrange("(a b) f -> a (b f)", a=400)).then_inc(copied, 16)
            sp.wait_ge(zeroed, 1)
            sp.dma_start(ea32_s[E:NP, :].rearrange("(a b) f -> a (b f)", b=2),
                         zero[0:pad_rows // 2, 0:2 * EA]).then_inc(copied, 16)
            sp.dma_start(ea10_s[E:NP, :].rearrange("(a b) f -> a (b f)", b=2),
                         zero[0:pad_rows // 2, 0:2 * EB]).then_inc(copied, 16)
            sp.wait_ge(paired, 1)
            for k in range(C):
                many = min(P, T - k * P)
                sp.dma_start(pair_s[0:1, k * P * P:(k * P + many) * P].rearrange("o (t p) -> (o t) p", p=P),
                             pairs[0:many, k, :]).then_inc(copied, 16)
            sp.wait_ge(copied, 16 * (4 + C))

        @block.scalar
        def _(act):
            act.wait_ge(padded, 3)
            for row, dram in ((srow, src), (drow, dst), (trow, et)):
                full = (C - 1) * P
                act.dma_start(row[:, 0:C - 1, :],
                              dram[0:full * P].rearrange("(c t p) -> t c p", t=P, p=P)).then_inc(loaded, 16)
                act.dma_start(row[0:FULL - full, C - 1, :],
                              dram[full * P:FULL * P].rearrange("(t p) -> t p", p=P)).then_inc(loaded, 16)
                act.dma_start(row[FULL - full:FULL - full + 1, C - 1, 0:REST],
                              dram[FULL * P:E].rearrange("(o p) -> o p", o=1)).then_inc(loaded, 16)

        @block.gpsimd
        def _(pool):
            nc.gpsimd.memset(ident[:, :], 0.0).then_inc(pooled, 1)
            nc.gpsimd.iota(iota_w[:, :], [[1, W]], base=0, channel_multiplier=0,
                           allow_small_or_imprecise_dtypes=True).then_inc(pooled, 1)
            pool.wait_ge(pooled, 2)
            nc.gpsimd.affine_select(out=ident[:, :], in_=ident[:, :], compare_op=ALU.not_equal, fill=1.0,
                                    base=0, pattern=[[-1, P]], channel_multiplier=1).then_inc(consts, 1)
            nc.gpsimd.memset(ones[:, :], 1.0)
            nc.gpsimd.memset(deg[:, :], 0.0)
            nc.gpsimd.memset(eps_col[:, :], LN_EPS).then_inc(pooled, 1)
            pool.wait_ge(pooled, 3)

        @block.vector
        def _(dve):
            c = Links(dve, chain, 0)
            c.step(0)
            nc.vector.memset(srow[:, :, :], 0).then_inc(padded, 1)
            nc.vector.memset(drow[:, :, :], -1).then_inc(padded, 1)
            nc.vector.memset(trow[:, :, :], 0).then_inc(padded, 1)
            nc.vector.memset(zero[:, :], 0.0).then_inc(zeroed, 1)
            dve.wait_ge(loaded, 16 * 9)
            dve.wait_ge(pooled, 2)
            nc.vector.tensor_scalar(pairs[:, :, :], trow[:, :, :], 1, None,
                                    ALU.arith_shift_right).then_inc(paired, 1)
            c.link(nc.vector.tensor_scalar(trow[:, :, :], trow[:, :, :], 1, None, ALU.bitwise_and))
            nc.vector.tensor_copy(trowf[:, :, :], trow[:, :, :]).then_inc(made, 1)
            nc.vector.tensor_copy(iota_b[:, :], iota_w[:, :])
            nc.vector.memset(ones_b[:, :], 1.0)
            nc.vector.tensor_copy(srowf[:, :, :], srow[:, :, :]).then_inc(made, 1)
            c.link(nc.vector.tensor_copy(drowf[:, :, :], drow[:, :, :]))
            c.link(nc.vector.tensor_scalar(drelf[:, :, :], drowf[:, :, :], 0.0, float(NP), ALU.is_lt, ALU.mult))
            c.link(nc.vector.tensor_tensor(drelf[:, :, :], drelf[:, :, :], drowf[:, :, :], ALU.add))
            c.link(nc.vector.tensor_reduce(lo_i[:, :, 0], drelf[:, :, :], AX.X, ALU.min))
            c.link(nc.vector.tensor_reduce(lo_i[:, :, 1], drowf[:, :, :], AX.X, ALU.max))
            c.link(nc.vector.tensor_scalar(lo_i[:, :, :], lo_i[:, :, :], 7, None, ALU.arith_shift_right))
            c.link(nc.vector.tensor_copy(lo_f[:, :, :], lo_i[:, :, :]))
            c.link(nc.vector.tensor_scalar(cols[:, :, 2], lo_f[:, :, 0], 0.0, float(T - 2), ALU.max, ALU.min))
            c.link(nc.vector.tensor_scalar(cols[:, :, 0], cols[:, :, 2], float(D), None, ALU.mult))
            c.link(nc.vector.tensor_scalar(base[:, :], cols[:, :, 2], float(P), None, ALU.mult))
            c.link(nc.vector.tensor_tensor(cols[:, :, 1], lo_f[:, :, 1], cols[:, :, 2], ALU.subtract))
            c.link(nc.vector.tensor_scalar(cols[:, :, 1], cols[:, :, 1], -1.0, 0.0, ALU.add, ALU.max))
            for k in range(C):
                last = nc.vector.tensor_scalar(drelf[:, k, :], drowf[:, k, :], base[:, k:k + 1], None,
                                               ALU.subtract)
            last.then_inc(made, 1)
            dve.wait_ge(turned, 1)
            nc.vector.tensor_copy(src_idx[:, :], ps[0][:, :, :].rearrange("p c t -> p (c t)")[:, 0:T])
            nc.vector.tensor_scalar(dst_idx[:, :], ps[1][:, :, :].rearrange("p c t -> p (c t)")[:, 0:T],
                                    0.0, None, ALU.max)
            nc.vector.tensor_copy(dst_rel[:, :], ps[2][:, :, :].rearrange("p c t -> p (c t)")[:, 0:T])
            by_tile = ps[3][:, :, :].rearrange("p c t -> p (c t)")[:, 0:T]
            nc.vector.tensor_copy(odd[:, :], by_tile)
            nc.vector.tensor_scalar(even[:, :], by_tile, -1.0, 1.0, ALU.mult, ALU.add)
            for k in range(3):
                last = nc.vector.tensor_copy(rows[:, k, :], ps_r[k][0:1, :, :].rearrange("p c t -> p (c t)"))
            c.link(last)
            halves = [rows[:, k, 0:T].rearrange("p (n j) -> p n j", j=SB) for k in range(3)]
            w8 = win[:, :].rearrange("p (n j) -> p n j", j=8)
            wb8 = win_b[:, :].rearrange("p (n j) -> p n j", j=8)
            wm8 = win_m[:, :].rearrange("p (n j) -> p n j", j=8)
            nc.vector.tensor_copy(wm8[:, :, 0:SB], halves[1])
            nc.vector.tensor_copy(w8[:, :, 0:SB], halves[0])
            c.link(nc.vector.tensor_reduce(w8[:, :, SB], halves[1], AX.X, ALU.max))
            nc.vector.tensor_copy(wb8[:, :, 0:SB], halves[2])
            c.link(nc.vector.tensor_copy(wb8[:, :, SB], w8[:, :, SB]))

        @block.tensor
        def _(pe):
            pe.wait_ge(consts, 1)
            pe.wait_ge(made, 3)
            pe.wait_ge(chain, 13)
            for k in range(C):
                for to, frm in zip(ps, (srowf, drowf, drelf, trowf)):
                    nc.tensor.transpose(to[:, k, :], frm[:, k, :], ident[:, :])
                for q in range(3):
                    last = nc.tensor.transpose(ps_r[q][0:1, k, :], cols[:, k, q:q + 1], ident[:, :])
            last.then_inc(turned, 1)


def gather_pass(nc, pool, tag, tables, idx_small, ring, wait_used, landed, idx_ready, steps=STEPS, halves=2):
    count = pool.alloc_register(f"{tag}_halves")
    pool.reg_mov(count, 1)

    def body(i, first):
        for h in range(halves):
            n = halves * i + h
            if not first:
                wait_used(i, h)
            for s, (_, index, _) in enumerate(tables):
                last = nc.gpsimd.tensor_copy(idx_small[:, s, h, :], index[:, bass.ds(n * SB, SB)])
            last.then_inc(idx_ready, 1)
            pool.wait_ge(idx_ready, pool.snap(count))
            pool.reg_add(count, count, 1)
            for j in range(SB):
                for s, (dram, _, slot) in enumerate(tables):
                    pool.indirect_dma_start(
                        out=ring(h, j, slot), out_offset=None, in_=dram[:, :],
                        in_offset=bass.IndirectOffsetOnAxis(ap=idx_small[:, s, h, j:j + 1], axis=0),
                    ).then_inc(landed[h], 16)
    peel_first(pool, steps, body)


class Sums:

    def __init__(self, nc, ctx, tag, agg, dst_rel, win, win_m, iota, parts, deg=None, win_b=None, ones=None,
                 scalar_members=False):
        def sem(name):
            return nc.alloc_semaphore(f"{tag}_{name}")

        def sb(name, shape, dt=F32):
            return ctx.enter_context(nc.sbuf_tensor(f"{tag}_{name}", shape, dt))
        self.nc, self.tag, self.agg, self.dst_rel, self.iota = nc, tag, agg, dst_rel, iota
        self.win, self.win_m = win, win_m
        self.deg, self.win_b, self.ones = deg, win_b, ones
        dt = BF16 if parts else F32
        self.S = sb("S", [P, 2, SB, W], dt)
        self.Sx = sb("Sx", [P, P], dt)
        self.relx = sb("relx", [P, SB])
        if scalar_members:
            self.away = sb("away", [P, 2, SB, W], dt)
            self.distances = sem("distances")
        if parts:
            self.msg = sb("msg", [P, 2, SB, D])
            self.rest = sb("rest", [P, SB, D])
            self.parts = sb("parts", [P, 2, 3, SB, D], BF16)
            self.msg_ready, self.high, self.split, self.parts_ready = (
                sem(x) for x in ("msg_ready", "high", "split", "parts_ready"))
        self.ps = ctx.enter_context(nc.psum_tensor(f"{tag}_ps_sum", [P, 8, 2, D], F32))
        self.ps_x = ctx.enter_context(nc.psum_tensor(f"{tag}_ps_x", [P, 512], F32))
        self.count = {}
        self.member_ready, self.summed, self.added, self.x_ready, self.x_summed, self.x_chain, self.counted, \
            self.deg_summed, self.half_done = (
                sem(x) for x in ("member_ready", "summed", "added", "x_ready", "x_summed", "x_chain",
                                 "counted", "deg_summed", "half_done"))
        self.tick = sb("tick", [1, 1])

    def start(self, eng, name):
        self.count[name] = eng.alloc_register(f"{self.tag}_{name}")
        eng.reg_mov(self.count[name], 1)

    def wait_next(self, eng, sem, name):
        r = self.count[name]
        eng.wait_ge(sem, eng.snap(r))
        eng.reg_add(r, r, 1)

    def within(self, dve, at, top):
        r = self.count["place"]
        dve.reg_alu(r, at, top, op=ALU.min)
        return dve.snap(r, min_val=0, max_val=top)

    def vector_members(self, dve, n, h):
        for j in range(SB):
            self.nc.vector.tensor_scalar(self.S[:, h % 2, j, :], self.iota[:, :],
                                         self.dst_rel[:, bass.ds(n * SB + j, 1)], None,
                                         ALU.is_equal).then_inc(self.member_ready, 1)

    def scalar_members(self, act, n, h):
        nc = self.nc
        if behind(n, 2):
            act.wait_ge(self.half_done, n - 1)
        for j in range(SB):
            last = nc.scalar.activation(self.away[:, h, j, :], self.iota[:, :], ACT.Abs, scale=-1.0,
                                        bias=self.dst_rel[:, bass.ds(n * SB + j, 1)])
        last.then_inc(self.distances, 1)
        act.wait_ge(self.distances, n + 1)
        nc.scalar.activation(self.S[:, h, :, :], self.away[:, h, :, :], ACT.Relu, scale=-1.0, bias=1.0)\
            .then_inc(self.member_ready, SB)

    def scalar_high(self, act, n, h):
        act.wait_ge(self.msg_ready, n + 1)
        if behind(n, 2):
            act.wait_ge(self.half_done, n - 1)
        self.nc.scalar.activation(self.parts[:, h, 0, :, :], self.msg[:, h, :, :], ACT.Copy)\
            .then_inc(self.high, 1)

    def vector_split(self, dve, n, h):
        high, mid, low = (self.parts[:, h, q, :, :] for q in range(3))
        dve.wait_ge(self.high, n + 1)
        self.nc.vector.tensor_tensor(self.rest[:, :, :], self.msg[:, h, :, :], high, ALU.subtract)\
            .then_inc(self.split, 1)
        dve.wait_ge(self.split, 2 * n + 1)
        self.nc.vector.tensor_copy(mid, self.rest[:, :, :]).then_inc(self.split, 1)
        dve.wait_ge(self.split, 2 * n + 2)
        self.nc.vector.tensor_tensor(low, self.rest[:, :, :], mid, ALU.subtract).then_inc(self.parts_ready, 1)

    def tensor_sum(self, pe, n, h, msgs):
        nc = self.nc
        S = self.S[:, h % 2, :, :]
        for j in range(SB):
            pe.wait_ge(self.member_ready, n * SB + j + 1)
            if j in (0, BANK) and behind(n, 1):
                pe.wait_ge(self.added, (n - 1) * SB + min(j + BANK, SB))
            rhs = msgs(j)
            for w in range(2):
                for q, part in enumerate(rhs):
                    last = nc.tensor.matmul(self.ps[:, j, w, :], lhsT=S[:, j, w * P:(w + 1) * P],
                                            rhs=part, start=q == 0, stop=q == len(rhs) - 1)
            last.then_inc(self.summed, 1)
        if self.deg is not None:
            if behind(n, 1):
                pe.wait_ge(self.half_done, n)
            for j in range(SB):
                for w in range(2):
                    at = 128 + 2 * j + w
                    last = nc.tensor.matmul(self.ps_x[:, at:at + 1], lhsT=S[:, j, w * P:(w + 1) * P],
                                            rhs=self.ones[:, 0:1], start=True, stop=True)
            last.then_inc(self.deg_summed, 1)
        (more,) = load_regs(nc, mybir.EngineType.PE, self.win[0:1, bass.ds(n * 8 + SB, 1)], T)
        with pe.If(more > 0):
            further = load_regs(nc, mybir.EngineType.PE, self.win_m[0:1, bass.ds(n * 8, SB)], T)
            for j in range(SB):
                with pe.If(further[j] > 0):
                    with pe.Fori(0, further[j]) as _:
                        self.wait_next(pe, self.x_ready, "pe")
                        rhs = msgs(j)
                        for q, part in enumerate(rhs):
                            last = nc.tensor.matmul(self.ps_x[:, 0:D], lhsT=self.Sx[:, :], rhs=part,
                                                    start=q == 0, stop=q == len(rhs) - 1)
                        if self.deg is not None:
                            last = nc.tensor.matmul(self.ps_x[:, 64:65], lhsT=self.Sx[:, :],
                                                    rhs=self.ones[:, 0:1], start=True, stop=True)
                        last.then_inc(self.x_summed, 1)

    def tensor_sum_parts(self, pe, n, h):
        pe.wait_ge(self.parts_ready, n + 1)
        self.tensor_sum(pe, n, h, lambda j: [self.parts[:, h, q, j, :] for q in range(3)])

    def vector_add(self, dve, n):
        nc = self.nc
        DVE = mybir.EngineType.DVE
        regs = load_regs(nc, DVE, self.win[0:1, bass.ds(n * 8, 8)], (T - 2) * D)
        if self.deg is not None:
            blocks = load_regs(nc, DVE, self.win_b[0:1, bass.ds(n * 8, 8)], T - 2)
        for j in range(SB):
            if j in (0, BANK):
                dve.wait_ge(self.summed, n * SB + min(j + BANK, SB))
            if not (isinstance(n, int) and n * SB + j == 0):
                dve.wait_ge(self.added, n * SB + j)
            part = self.agg[:, bass.ds(regs[j], 2 * D)]
            nc.vector.tensor_tensor(part, self.ps[:, j, :, :].rearrange("p w f -> p (w f)"), part,
                                    ALU.add).then_inc(self.added, 1)
        if self.deg is not None:
            dve.wait_ge(self.deg_summed, n + 1)
            for j in range(SB):
                if not (isinstance(n, int) and n * SB + j == 0):
                    dve.wait_ge(self.counted, n * SB + j)
                part = self.deg[:, bass.ds(blocks[j], 2)]
                nc.vector.tensor_tensor(part, self.ps_x[:, 128 + 2 * j:130 + 2 * j], part,
                                        ALU.add).then_inc(self.counted, 1)
        more = regs[SB]
        with dve.If(more > 0):
            dve.wait_ge(self.added, n * SB + SB)
            if self.deg is not None:
                dve.wait_ge(self.counted, n * SB + SB)

            def link(ins):
                ins.then_inc(self.x_chain, 1)
                self.wait_next(dve, self.x_chain, "link")
            link(nc.vector.tensor_scalar(self.relx[:, :], self.dst_rel[:, bass.ds(n * SB, SB)], -float(P),
                                         None, ALU.add))
            further = load_regs(nc, DVE, self.win_m[0:1, bass.ds(n * 8, SB)], T)
            for j in range(SB):
                with dve.If(further[j] > 0):
                    with dve.Fori(0, further[j]) as w:
                        rel = self.relx[:, j:j + 1]
                        link(nc.vector.tensor_scalar(rel, rel, -float(P), None, ALU.add))
                        nc.vector.tensor_scalar(self.Sx[:, :], self.iota[:, 0:P], rel, None,
                                                ALU.is_equal).then_inc(self.x_ready, 1)
                        self.wait_next(dve, self.x_summed, "dve")
                        part = self.agg[:, bass.ds(self.within(dve, regs[j] + w * D + 2 * D, (T - 1) * D), D)]
                        link(nc.vector.tensor_tensor(part, self.ps_x[:, 0:D], part, ALU.add))
                        if self.deg is not None:
                            part = self.deg[:, bass.ds(self.within(dve, blocks[j] + w + 2, T - 1), 1)]
                            link(nc.vector.tensor_tensor(part, self.ps_x[:, 64:65], part, ALU.add))
        nc.vector.memset(self.tick[:, :], 0.0).then_inc(self.half_done, 1)


class Pass:

    def __init__(self, nc, ctx, tag):
        self.nc, self.ctx, self.tag = nc, ctx, tag

    def sb(self, name, shape, dt=F32):
        return self.ctx.enter_context(self.nc.sbuf_tensor(f"{self.tag}_{name}", shape, dt))

    def ps(self, name, shape):
        return self.ctx.enter_context(self.nc.psum_tensor(f"{self.tag}_{name}", shape, F32))

    def sem(self, name):
        return self.nc.alloc_semaphore(f"{self.tag}_{name}")

    def sems(self, names):
        return [self.sem(n) for n in names.split()]


class Norm:
    LINKS = 5
    SHARE = 3

    def __init__(self, p, eps_col):
        self.nc, self.eps_col = p.nc, eps_col
        self.st = p.sb("st", [P, 2, GB, 6])
        self.small = p.sb("small", [P, 2, 5, GB])
        self.std_ready, self.roots, self.shifts, self.chain, self.h_ready, self.share_ready = p.sems(
            "std_ready roots shifts chain h_ready share_ready")

    def vector(self, dve, n, h, x_in, to, wait_free=None):
        nc = self.nc
        st = self.st[:, h, :, :]
        mean2, m2, rstd, shift, dif = (self.small[:, h, s, :] for s in range(5))
        at = [self.LINKS * n]

        def link(ins):
            ins.then_inc(self.chain, 1)
            at[0] = at[0] + 1
            dve.wait_ge(self.chain, at[0])
        if behind(n, 2):
            dve.wait_ge(self.h_ready, n - 1)
        for k in range(GB):
            last = nc.vector.bn_stats(st[:, k, :], x_in(k))
        link(last)
        nc.vector.tensor_tensor(mean2, st[:, :, 1], st[:, :, 4], ALU.add)
        nc.vector.tensor_tensor(dif, st[:, :, 1], st[:, :, 4], ALU.subtract)
        link(nc.vector.tensor_tensor(m2, st[:, :, 2], st[:, :, 5], ALU.add))
        link(nc.vector.tensor_tensor(dif, dif, dif, ALU.mult))
        nc.vector.scalar_tensor_tensor(out=m2, in0=dif, scalar=D / 4.0, in1=m2, op0=ALU.mult,
                                       op1=ALU.add).then_inc(self.std_ready, 1)
        dve.wait_ge(self.roots, n + 1)
        link(nc.vector.reciprocal(rstd, rstd))
        nc.vector.scalar_tensor_tensor(out=shift, in0=mean2, scalar=-0.5, in1=rstd, op0=ALU.mult,
                                       op1=ALU.mult).then_inc(self.shifts, 1)
        dve.wait_ge(self.shifts, n + 1)
        if wait_free:
            wait_free()
        for k in range(GB - self.SHARE, GB):
            last = nc.vector.tensor_scalar(to(k, k + 1), x_in(k), rstd[:, k:k + 1], shift[:, k:k + 1],
                                           ALU.mult, ALU.add)
        link(last)
        share = to(GB - self.SHARE, GB)
        nc.vector.tensor_scalar(share, share, 0.0, None, ALU.max).then_inc(self.share_ready, 1)

    def scalar_root(self, act, n, h):
        act.wait_ge(self.std_ready, n + 1)
        self.nc.scalar.activation(self.small[:, h, 2, :], self.small[:, h, 1, :], ACT.Sqrt,
                                  bias=self.eps_col[:, 0:1], scale=1.0 / D).then_inc(self.roots, 1)

    def scalar_apply(self, act, n, h, x_in, to):
        act.wait_ge(self.shifts, n + 1)
        for k in range(GB - self.SHARE):
            if k == GB - self.SHARE - 1:
                act.wait_ge(self.share_ready, n + 1)
            last = self.nc.scalar.activation(to(k, k + 1), x_in(k), ACT.Relu, bias=self.small[:, h, 3, k:k + 1],
                                             scale=self.small[:, h, 2, k:k + 1])
        last.then_inc(self.h_ready, 1)


def group(agg, n):
    return agg[:, bass.ds(n * GC, GC)]


def rows_of(buf):
    return buf.rearrange("p (k f) -> p k f", f=D)


def store_group(sp, tab, n, buf):
    return sp.dma_start(tiles_of(tab, n * GB, GB), rows_of(buf))


def first_norm(nc, x, agg, h_tab, xh_tab, eps_col):
    steps = GSTEPS // 2
    with ExitStack() as ctx:
        ctx.enter_context(nc.cleanup_on_exit())
        p = Pass(nc, ctx, "n0")
        xb = p.sb("x", [P, DEEP, GC])
        xh = p.sb("xh", [P, 2, GC])
        norm = Norm(p, eps_col)
        h_ready = norm.h_ready
        xh_ready = p.sem("xh_ready")
        x_in, xh_out, h_out = ([p.sem(f"{s}{h}") for h in range(DEEP)] for s in ("x_in", "xh_out", "h_out"))
        block = ctx.enter_context(nc.Block())
        full_groups = FULL // GB
        left = FULL - full_groups * GB
        assert full_groups == 2 * GSTEPS - 1

        @block.sync
        def _(sp):
            def load(i, h, first):
                n = DEEP * i + h
                if not first:
                    sp.wait_ge(xh_ready, n - DEEP + 1)
                if isinstance(n, int) and n == full_groups:
                    part = rows_of(xb[:, h, :])
                    sp.dma_start(part[:, 0:left, :], tiles_of(x, n * GB, left)).then_inc(x_in[h], 16)
                    sp.dma_start(part[0:REST, left, :], x[FULL * P:N, :]).then_inc(x_in[h], 16)
                else:
                    sp.dma_start(rows_of(xb[:, h, :]), tiles_of(x, n * GB, GB)).then_inc(x_in[h], 16)

            def store(i, h):
                n = DEEP * i + h
                sp.wait_ge(h_ready, n + 1)
                store_group(sp, h_tab, n, group(agg, n)).then_inc(h_out[h], 16)
                sp.wait_ge(xh_ready, n + 1)
                store_group(sp, xh_tab, n, xh[:, h % 2, :]).then_inc(xh_out[h], 16)

            for h in range(DEEP):
                load(0, h, True)
            with sp.Fori(0, steps - 2) as i:
                for h in range(DEEP):
                    store(i, h)
                    load(i + 1, h, False)
            for i in range(steps - 2, steps):
                for h in range(DEEP):
                    store(i, h)
                    if i + 1 < steps:
                        load(i + 1, h, False)
            for h in range(DEEP):
                sp.wait_ge(h_out[h], 16 * steps)
                sp.wait_ge(xh_out[h], 16 * steps)

        def x_landed(eng, i, h):
            eng.wait_ge(x_in[h], 16 * (i + 1) + (16 if isinstance(i, int) and i == steps - 1 and h == DEEP - 1 else 0))

        def to(n):
            return lambda k0, k1: agg[:, bass.ds(n * GC + k0 * D, (k1 - k0) * D)]

        def peel_last(eng, body):
            body(0, True)
            with eng.Fori(1, steps - 1) as i:
                body(i, False)
            body(steps - 1, False)

        @block.vector
        def _(dve):
            def body(i, first):
                for h in range(DEEP):
                    x_landed(dve, i, h)
                    norm.vector(dve, DEEP * i + h, h % 2, lambda k: xb[:, h, k * D:(k + 1) * D], to(DEEP * i + h))
            peel_last(dve, body)

        @block.scalar
        def _(act):
            staged(act, [(0, lambda i, h: norm.scalar_root(act, DEEP * i + h, h % 2)),
                         (0, lambda i, h: norm.scalar_apply(
                             act, DEEP * i + h, h % 2, lambda k: xb[:, h, k * D:(k + 1) * D],
                             to(DEEP * i + h)))], steps, DEEP)

        @block.gpsimd
        def _(pool):
            def body(i, first):
                for h in range(DEEP):
                    n = DEEP * i + h
                    pool.wait_ge(h_ready, n + 1)
                    if behind(n, 2):
                        pool.wait_ge(xh_out[(h + 2) % DEEP], 16 * (i + (h - 2) // DEEP + 1))
                    nc.gpsimd.tensor_tensor(xh[:, h % 2, :], xb[:, h, :], group(agg, n), ALU.add)\
                        .then_inc(xh_ready, 1)
            peel_last(pool, body)


def gcn_edges(nc, h_tab, agg, src_idx, dst_rel, win, win_m, iota_w, end=False):
    HALVES = 4
    steps = 2 * STEPS // HALVES
    with ExitStack() as ctx:
        ctx.enter_context(nc.cleanup_on_exit())
        p = Pass(nc, ctx, "e4" if end else "e3")
        ring = p.sb("ring", [P, HALVES, SB, D])
        idx_small = p.sb("idx", [P, 1, HALVES, SB], I32)
        landed = [p.sem(f"landed{h}") for h in range(HALVES)]
        idx_ready = p.sem("idx_ready")
        sums = Sums(nc, ctx, p.tag, agg, dst_rel, win, win_m, iota_w, parts=False)
        block = ctx.enter_context(nc.Block())

        @block.gpsimd
        def _(pool):
            gather_pass(nc, pool, p.tag, [(h_tab, src_idx, 0)], idx_small, lambda h, j, s: ring[:, h, j, :],
                        lambda i, h: pool.wait_ge(sums.half_done, HALVES * (i - 1) + h + 1), landed, idx_ready,
                        steps, HALVES)

        @block.vector
        def _(dve):
            for name in ("dve", "link", "place"):
                sums.start(dve, name)
            staged(dve, [(0, lambda i, h: sums.vector_members(dve, HALVES * i + h, h)),
                         (1, lambda i, h: sums.vector_add(dve, HALVES * i + h))], steps, HALVES)

        @block.tensor
        def _(pe):
            sums.start(pe, "pe")

            def add_up(i, h):
                pe.wait_ge(landed[h], 16 * SB * (i + 1))
                sums.tensor_sum(pe, HALVES * i + h, h, lambda j: [ring[:, h, j, :]])
            staged(pe, [(0, add_up)], steps, HALVES)


def gin_edges(nc, h_tab, ea32_s, W_edge, b_edge, agg, src_idx, dst_rel, win, win_m, iota_b, ident):
    K1 = EA + 1
    PACK = 3
    packs = [(q * PACK, min(PACK, SB - q * PACK)) for q in range(-(-SB // PACK))]
    steps = 2 * STEPS // DEEP
    with ExitStack() as ctx:
        ctx.enter_context(nc.cleanup_on_exit())
        p = Pass(nc, ctx, "e0")
        ring = p.sb("ring", [P, DEEP, SB, D])
        idx_small = p.sb("idx", [P, 1, DEEP, SB], I32)
        ea = p.sb("ea", [P, DEEP, SB, K1])
        eaT = p.sb("eaT", [P, 2, len(packs), P])
        w = p.sb("w", [P, PACK, D])
        raw = p.sb("raw", [P, 2, SB, D])
        ps_t = p.ps("ps_t", [P, 4, P])
        ps_e = p.ps("ps_e", [P, 8, D])
        landed, ea_in = ([p.sem(f"{s}{h}") for h in range(DEEP)] for s in ("landed", "ea_in"))
        idx_ready, turned, copied, mixed, raw_ready, cleared, w_in, zeroed = p.sems(
            "idx_ready turned copied mixed raw_ready cleared w_in zeroed")
        sums = Sums(nc, ctx, p.tag, agg, dst_rel, win, win_m, iota_b, parts=True)
        block = ctx.enter_context(nc.Block())

        @block.gpsimd
        def _(pool):
            nc.gpsimd.memset(w[:, :, :], 0.0).then_inc(zeroed, 1)
            nc.gpsimd.memset(ea[:, :, :, EA:K1], 1.0).then_inc(cleared, 1)
            gather_pass(nc, pool, p.tag, [(h_tab, src_idx, 0)], idx_small, lambda h, j, s: ring[:, h, j, :],
                        lambda i, h: pool.wait_ge(raw_ready, DEEP * (i - 1) + h + 1), landed, idx_ready,
                        steps, DEEP)

        @block.sync
        def _(sp):
            sp.wait_ge(zeroed, 1)
            for q in range(PACK):
                sp.dma_start(w[q * K1:q * K1 + EA, q, :], W_edge[:, :]).then_inc(w_in, 16)
                sp.dma_start(w[q * K1 + EA:(q + 1) * K1, q, :],
                             b_edge.rearrange("(o f) -> o f", o=1)).then_inc(w_in, 16)

            def body(i, first):
                for h in range(DEEP):
                    n = DEEP * i + h
                    if not first:
                        sp.wait_ge(turned, n - DEEP + 1)
                    sp.dma_start(ea[:, h, :, 0:EA], tiles_of(ea32_s, n * SB, SB)).then_inc(ea_in[h], 16)
            peel_first(sp, steps, body)

        @block.scalar
        def _(act):
            def copy(i, h):
                n = DEEP * i + h
                act.wait_ge(turned, n + 1)
                if behind(n, 2):
                    act.wait_ge(mixed, n - 1)
                for q, (_, many) in enumerate(packs):
                    last = nc.scalar.activation(eaT[0:many * K1, h % 2, q, :], ps_t[0:many * K1, q, :], ACT.Copy)
                last.then_inc(copied, 1)

            def relu(i, h):
                n = DEEP * i + h
                act.wait_ge(raw_ready, n + 1)
                nc.scalar.activation(sums.msg[:, h % 2, :, :], raw[:, h % 2, :, :], ACT.Relu).then_inc(sums.msg_ready, 1)
                sums.scalar_high(act, n, h % 2)
            staged(act, [(0, copy), (1, relu)], steps, DEEP)

        @block.tensor
        def _(pe):
            sums.start(pe, "pe")
            pe.wait_ge(w_in, 16 * 2 * PACK)
            pe.wait_ge(cleared, 1)

            def turn(i, h):
                n = DEEP * i + h
                pe.wait_ge(ea_in[h], 16 * (i + 1))
                if behind(n, 1):
                    pe.wait_ge(copied, n)
                for q, (t0, many) in enumerate(packs):
                    last = nc.tensor.transpose(
                        ps_t[0:many * K1, q, :],
                        ea[:, h, t0:t0 + many, :].rearrange("p k f -> p (k f)"), ident[:, :])
                last.then_inc(turned, 1)

            def mix(i, h):
                n = DEEP * i + h
                pe.wait_ge(copied, n + 1)
                if behind(n, 1):
                    pe.wait_ge(raw_ready, n)
                for j in range(SB):
                    q = j // PACK
                    k = packs[q][1] * K1
                    last = nc.tensor.matmul(ps_e[:, j, :], lhsT=eaT[0:k, h % 2, q, :], rhs=w[0:k, j % PACK, :],
                                            start=True, stop=True)
                last.then_inc(mixed, 1)
            staged(pe, [(0, turn), (1, mix),
                        (2, lambda i, h: sums.tensor_sum_parts(pe, DEEP * i + h, h % 2))], steps, DEEP)

        @block.vector
        def _(dve):
            for name in ("dve", "link", "place"):
                sums.start(dve, name)

            def message(i, h):
                n = DEEP * i + h
                dve.wait_ge(landed[h], 16 * SB * (i + 1))
                dve.wait_ge(mixed, n + 1)
                nc.vector.tensor_tensor(raw[:, h % 2, :, :], ps_e[:, 0:SB, :], ring[:, h, :, :],
                                        ALU.add).then_inc(raw_ready, 1)
                sums.vector_members(dve, n, h)
            staged(dve, [(0, message), (1, lambda i, h: sums.vector_add(dve, DEEP * i + h)),
                         (0, lambda i, h: sums.vector_split(dve, DEEP * i + h, h % 2))], steps, DEEP)


def gin_nodes(nc, agg, xh_tab, h_tab, W1, b1, gamma, beta, W2, b2, ident, ones, eps_col):
    pads = NP - N
    C0 = (FULL // 2) * P
    assert FULL % 2 == 0 and T - FULL == 2
    with ExitStack() as both:
        p = Pass(nc, both, "m")
        wbd = [p.sb(f"wbd{k}", [P, P]) for k in range(2)]
        cols = p.sb("cols", [P, 3])
        b2row = p.sb("b2row", [1, P])
        scale, shift = p.sb("scale", [P, 1]), p.sb("shift", [P, 1])
        with ExitStack() as ctx:
            ctx.enter_context(nc.cleanup_on_exit())
            p = Pass(nc, ctx, "m1")
            stage = p.sb("stage", [P, 2, GC])
            aT = p.sb("aT", [P, 2, GC])
            stats = p.sb("stats", [P, 4 * GSTEPS, 6])
            mv = p.sb("mv", [P, 2])
            fold = p.sb("fold", [P, P])
            tmp = p.sb("tmp", [P, 8])
            ps_t = p.ps("ps_t", [P, 8, P])
            ps_1 = p.ps("ps_1", [P, 1024])
            ps_f = p.ps("ps_f", [P, 2])
            zeroed, w_in, stage_in, turned, copied, mixed, biased, chain, folded, rooted, padz = p.sems(
                "zeroed w_in stage_in turned copied mixed biased chain folded rooted padz")
            block = ctx.enter_context(nc.Block())

            @block.sync
            def _(sp):
                sp.wait_ge(zeroed, 2)
                for a in range(2):
                    half = slice(a * D, (a + 1) * D)
                    for wb, wd in zip(wbd, (W1, W2)):
                        sp.dma_start(wb[half, half], wd[:, :]).then_inc(w_in, 16)
                    for k, vec in enumerate((b1, gamma, beta)):
                        sp.dma_start(cols[half, k:k + 1], vec.rearrange("(f o) -> f o", o=1)).then_inc(w_in, 16)
                    sp.dma_start(b2row[:, half], b2.rearrange("(o f) -> o f", o=1)).then_inc(w_in, 16)
                sp.wait_ge(w_in, 16 * 12)

            @block.gpsimd
            def _(pool):
                nc.gpsimd.memset(wbd[0][:, :], 0.0).then_inc(zeroed, 1)
                nc.gpsimd.memset(wbd[1][:, :], 0.0).then_inc(zeroed, 1)

            @block.tensor
            def _(pe):
                pe.wait_ge(w_in, 16 * 12)

                def turn(i, h):
                    n = 2 * i + h
                    pe.wait_ge(stage_in, n + 1)
                    if behind(n, 1):
                        pe.wait_ge(copied, n)
                    for q in range(GB // 2):
                        last = nc.tensor.transpose(ps_t[:, q, :], stage[:, h, q * P:(q + 1) * P], ident[:, :])
                    last.then_inc(turned, 1)

                def mix(i, h):
                    n = 2 * i + h
                    pe.wait_ge(copied, n + 1)
                    if behind(n, 1):
                        pe.wait_ge(biased, n)
                    nc.tensor.matmul(ps_1[:, 0:512], lhsT=wbd[0][:, :], rhs=aT[:, h, 0:512], start=True,
                                     stop=True)
                    nc.tensor.matmul(ps_1[:, 512:GC], lhsT=wbd[0][:, :], rhs=aT[:, h, 512:GC], start=True,
                                     stop=True).then_inc(mixed, 1)
                staged(pe, [(0, turn), (1, mix)], GSTEPS)
                for k in range(2):
                    pe.wait_ge(folded, k + 1)
                    nc.tensor.matmul(ps_f[:, k:k + 1], lhsT=fold[:, :], rhs=tmp[:, k:k + 1], start=True,
                                     stop=True).then_inc(mixed, 1)

            @block.scalar
            def _(act):
                act.wait_ge(w_in, 16 * 12)

                def copy(i, h):
                    n = 2 * i + h
                    act.wait_ge(turned, n + 1)
                    if behind(n, 2):
                        act.wait_ge(mixed, n - 1)
                    nc.scalar.activation(aT[:, h, 0:512], ps_t[:, 0:4, :].rearrange("p q n -> p (q n)"), ACT.Copy)
                    nc.scalar.activation(aT[:, h, 512:GC], ps_t[:, 4:7, :].rearrange("p q n -> p (q n)"),
                                         ACT.Copy).then_inc(copied, 1)

                def bias(i, h):
                    n = 2 * i + h
                    act.wait_ge(mixed, n + 1)
                    nc.scalar.activation(group(agg, n), ps_1[:, 0:GC], ACT.Identity,
                                         bias=cols[:, 0:1]).then_inc(biased, 1)
                staged(act, [(0, copy), (1, bias)], GSTEPS)
                act.wait_ge(folded, 3)
                nc.scalar.activation(tmp[:, 4:5], tmp[:, 3:4], ACT.Sqrt, bias=eps_col[:, 0:1]).then_inc(rooted, 1)

            @block.vector
            def _(dve):
                def bring(i, h):
                    n = 2 * i + h
                    if behind(n, 2):
                        dve.wait_ge(turned, n - 1)
                    nc.vector.tensor_copy(stage[:, h, :], group(agg, n)).then_inc(stage_in, 1)

                def take(i, h):
                    n = 2 * i + h
                    dve.wait_ge(biased, n + 1)
                    if isinstance(n, int) and n == 2 * GSTEPS - 1:
                        nc.vector.memset(agg[:, C0 + REST:C0 + P], 0.0).then_inc(padz, 1)
                        nc.vector.memset(agg[D:P, C0:C0 + REST], 0.0).then_inc(padz, 1)
                        dve.wait_ge(padz, 2)
                    for s in range(2):
                        nc.vector.bn_stats(stats[:, bass.ds(2 * n + s, 1), :].rearrange("p a s -> p (a s)"),
                                           agg[:, bass.ds(n * GC + s * (GC // 2), GC // 2)])
                staged(dve, [(0, bring), (2, take)], GSTEPS)
                c = Links(dve, chain, 0)
                c.step(0)
                for a in range(2):
                    last = nc.vector.tensor_tensor(fold[:, a * D:(a + 1) * D], ident[:, 0:D], ident[:, D:P],
                                                   ALU.add)
                c.link(last)
                c.link(nc.vector.bn_aggr(mv[:, :], stats[:, :, :].rearrange("p a s -> p (a s)")))
                nc.vector.tensor_copy(tmp[:, 0:1], mv[:, 0:1]).then_inc(folded, 1)
                dve.wait_ge(mixed, 2 * GSTEPS + 1)
                c.link(nc.vector.tensor_scalar(tmp[:, 2:3], ps_f[:, 0:1], 0.5, None, ALU.mult))
                c.link(nc.vector.tensor_tensor(tmp[:, 5:6], mv[:, 0:1], tmp[:, 2:3], ALU.subtract))
                c.link(nc.vector.tensor_tensor(tmp[:, 6:7], tmp[:, 5:6], tmp[:, 5:6], ALU.mult))
                nc.vector.tensor_tensor(tmp[:, 1:2], tmp[:, 6:7], mv[:, 1:2], ALU.add).then_inc(folded, 1)
                dve.wait_ge(mixed, 2 * GSTEPS + 2)
                c.link(nc.vector.tensor_scalar(tmp[:, 7:8], tmp[:, 2:3], NP / N, None, ALU.mult))
                c.link(nc.vector.tensor_tensor(tmp[:, 5:6], tmp[:, 7:8], tmp[:, 7:8], ALU.mult))
                c.link(nc.vector.tensor_scalar(tmp[:, 6:7], ps_f[:, 1:2], 0.5 * NP / N, None, ALU.mult))
                nc.vector.scalar_tensor_tensor(out=tmp[:, 3:4], in0=tmp[:, 5:6], scalar=-pads / NP,
                                               in1=tmp[:, 6:7], op0=ALU.mult, op1=ALU.add).then_inc(folded, 1)
                dve.wait_ge(rooted, 1)
                c.link(nc.vector.reciprocal(tmp[:, 4:5], tmp[:, 4:5]))
                c.link(nc.vector.tensor_tensor(scale[:, :], tmp[:, 4:5], cols[:, 1:2], ALU.mult))
                c.link(nc.vector.tensor_tensor(tmp[:, 5:6], tmp[:, 7:8], scale[:, :], ALU.mult))
                c.link(nc.vector.tensor_tensor(shift[:, :], cols[:, 2:3], tmp[:, 5:6], ALU.subtract))

        with ExitStack() as ctx:
            ctx.enter_context(nc.cleanup_on_exit())
            p = Pass(nc, ctx, "m2")
            y = p.sb("y", [P, 2, GC])
            xh = p.sb("xh", [P, DEEP, GC])
            x1 = p.sb("x1", [P, 2, GC])
            hb = p.sb("hb", [P, 2, GC])
            norm = Norm(p, eps_col)
            h_ready = norm.h_ready
            ps_2 = p.ps("ps_2", [P, 2, 8, P])
            y_ready, mixed, x1_ready, summed = p.sems("y_ready mixed x1_ready summed")
            xh_in, h_out = ([p.sem(f"{s}{h}") for h in range(DEEP)] for s in ("xh_in", "h_out"))
            steps = GSTEPS // 2
            block = ctx.enter_context(nc.Block())

            @block.sync
            def _(sp):
                load_store(sp, steps,
                           lambda i, h: sp.dma_start(rows_of(xh[:, h, :]), tiles_of(xh_tab, (DEEP * i + h) * GB, GB))
                           .then_inc(xh_in[h], 16),
                           lambda i, h: (sp.wait_ge(h_ready, DEEP * i + h + 1),
                                         store_group(sp, h_tab, DEEP * i + h, hb[:, h % 2, :])
                                         .then_inc(h_out[h], 16)), DEEP)
                for h in range(DEEP):
                    sp.wait_ge(h_out[h], 16 * steps)

            def to(h):
                return lambda k0, k1: hb[:, h % 2, k0 * D:k1 * D]

            def wait_free(eng, i, h):
                n = DEEP * i + h
                if behind(n, 2):
                    eng.wait_ge(h_out[(h + 2) % DEEP], 16 * (i + (h - 2) // DEEP + 1))
                    eng.wait_ge(summed, n - 1)

            @block.scalar
            def _(act):
                def activate(i, h):
                    n = DEEP * i + h
                    if behind(n, 2):
                        act.wait_ge(mixed, n - 1)
                    nc.scalar.activation(y[:, h % 2, :], group(agg, n), ACT.Relu, bias=shift[:, 0:1],
                                         scale=scale[:, 0:1]).then_inc(y_ready, 1)

                def apply(i, h):
                    wait_free(act, i, h)
                    norm.scalar_apply(act, DEEP * i + h, h % 2, lambda k: x1[:, h % 2, k * D:(k + 1) * D], to(h))
                staged(act, [(2, lambda i, h: norm.scalar_root(act, DEEP * i + h, h % 2)), (2, apply),
                             (0, activate)], steps, DEEP)

            @block.tensor
            def _(pe):
                def body(i, first):
                    for h in range(DEEP):
                        n = DEEP * i + h
                        pe.wait_ge(y_ready, n + 1)
                        if behind(n, 2):
                            pe.wait_ge(x1_ready, n - 1)
                        for q in range(GB // 2):
                            nc.tensor.matmul(ps_2[:, h % 2, q, :], lhsT=y[:, h % 2, q * P:(q + 1) * P], rhs=wbd[1][:, :],
                                             start=True, stop=False)
                            last = nc.tensor.matmul(ps_2[:, h % 2, q, :], lhsT=ones[0:1, :], rhs=b2row[:, :],
                                                    start=False, stop=True)
                        last.then_inc(mixed, 1)
                peel_first(pe, steps, body)

            @block.vector
            def _(dve):
                def rows(i, h):
                    n = DEEP * i + h
                    dve.wait_ge(mixed, n + 1)
                    dve.wait_ge(xh_in[h], 16 * (i + 1))
                    if behind(n, 2):
                        dve.wait_ge(summed, n - 1)
                    nc.vector.tensor_tensor(x1[:, h % 2, :], ps_2[:, h % 2, 0:7, :].rearrange("p q n -> p (q n)"),
                                            xh[:, h, :], ALU.add).then_inc(x1_ready, 1)
                    dve.wait_ge(x1_ready, n + 1)
                    norm.vector(dve, n, h % 2, lambda k: x1[:, h % 2, k * D:(k + 1) * D], to(h),
                                lambda: wait_free(dve, i, h))
                staged(dve, [(0, rows)], steps, DEEP)

            @block.gpsimd
            def _(pool):
                def body(i, first):
                    for h in range(DEEP):
                        n = DEEP * i + h
                        pool.wait_ge(h_ready, n + 1)
                        nc.gpsimd.tensor_tensor(group(agg, n), x1[:, h % 2, :], hb[:, h % 2, :], ALU.add)\
                            .then_inc(summed, 1)
                peel_first(pool, steps, body)


def load_store(sp, steps, load, store, halves=2):
    for h in range(halves):
        load(0, h)
    with sp.Fori(0, steps - 1) as i:
        for h in range(halves):
            store(i, h)
            load(i + 1, h)
    for h in range(halves):
        store(steps - 1, h)


def gated_edges(nc, h_tab, ea10_s, Wf, bf, Ws, bs, agg, deg, src_idx, dst_idx, dst_rel, win, win_m, win_b,
                iota_b, ident, ones, ones_b):
    K1 = EB + 1
    K = SB * K1
    steps = 2 * STEPS // DEEP
    with ExitStack() as ctx:
        ctx.enter_context(nc.cleanup_on_exit())
        p = Pass(nc, ctx, "e1")
        ring = p.sb("ring", [P, DEEP, SB, 2 * D])
        idx_small = p.sb("idx", [P, 2, DEEP, SB], I32)
        ea = p.sb("ea", [P, DEEP, SB, K1])
        eaT = p.sb("eaT", [K, P])
        hT = p.sb("hT", [P, SB, P])
        wcat = p.sb("wcat", [P, P])
        wea = p.sb("wea", [K, SB, P])
        small_e = p.sb("small_e", [P, SB, P])
        log_e = p.sb("log_e", [P, SB, P])
        soft = p.sb("soft", [P, SB, P])
        gate = p.sb("gate", [P, SB, D])
        ps_t = p.ps("ps_t", [P, 8, P])
        ps_m = p.ps("ps_m", [P, 8, P])
        landed, ea_in = ([p.sem(f"{s}{h}") for h in range(DEEP)] for s in ("landed", "ea_in"))
        idx_ready, turned, copied, mixed, act_chain, logs_ready, soft_ready, gated, cleared, w_in, zeroed, negated = p.sems(
            "idx_ready turned copied mixed act_chain logs_ready soft_ready gated cleared w_in zeroed negated")
        sums = Sums(nc, ctx, p.tag, agg, dst_rel, win, win_m, iota_b, True, deg, win_b, ones_b)
        block = ctx.enter_context(nc.Block())

        @block.gpsimd
        def _(pool):
            nc.gpsimd.memset(wea[:, :, :], 0.0).then_inc(zeroed, 1)
            nc.gpsimd.memset(ea[:, :, :, EB:K1], 1.0).then_inc(cleared, 1)
            gather_pass(nc, pool, p.tag, [(h_tab, src_idx, 0), (h_tab, dst_idx, 1)], idx_small,
                        lambda h, j, s: ring[:, h, j, s * D:(s + 1) * D],
                        lambda i, h: pool.wait_ge(turned, DEEP * (i - 1) + h + 1), landed, idx_ready,
                        steps, DEEP)

        @block.sync
        def _(sp):
            sp.wait_ge(zeroed, 1)
            for a, (wd, bd) in enumerate(((Wf, bf), (Ws, bs))):
                half = slice(a * D, (a + 1) * D)
                sp.dma_start(wcat[:, half], wd[0:P, :]).then_inc(w_in, 16)
                for j in range(SB):
                    sp.dma_start(wea[j * K1:j * K1 + EB, j, half], wd[P:P + EB, :]).then_inc(w_in, 16)
                    sp.dma_start(wea[j * K1 + EB:(j + 1) * K1, j, half],
                                 bd.rearrange("(o f) -> o f", o=1)).then_inc(w_in, 16)

            def body(i, first):
                for h in range(DEEP):
                    n = DEEP * i + h
                    if not first:
                        sp.wait_ge(turned, n - DEEP + 1)
                    sp.dma_start(ea[:, h, :, 0:EB], tiles_of(ea10_s, n * SB, SB)).then_inc(ea_in[h], 16)
            peel_first(sp, steps, body)

        @block.tensor
        def _(pe):
            sums.start(pe, "pe")
            pe.wait_ge(negated, 2)
            pe.wait_ge(cleared, 1)

            def mix(i, h):
                n = DEEP * i + h
                pe.wait_ge(ea_in[h], 16 * (i + 1))
                pe.wait_ge(landed[h], 16 * 2 * SB * (i + 1))
                nc.tensor.transpose(ps_t[0:K, SB, :], ea[:, h, :, :].rearrange("p k f -> p (k f)"), ident[:, :])
                for j in range(SB):
                    last = nc.tensor.transpose(ps_t[:, j, :], ring[:, h, j, :], ident[:, :])
                last.then_inc(turned, 1)
                pe.wait_ge(copied, n + 1)
                if behind(n, 1):
                    pe.wait_ge(soft_ready, n)
                for j in range(SB):
                    nc.tensor.matmul(ps_m[:, j, :], lhsT=hT[:, j, :], rhs=wcat[:, :], start=True, stop=False)
                    last = nc.tensor.matmul(ps_m[:, j, :], lhsT=eaT[:, :], rhs=wea[:, j, :], start=False,
                                            stop=True)
                last.then_inc(mixed, 1)
            staged(pe, [(0, mix), (1, lambda i, h: sums.tensor_sum_parts(pe, DEEP * i + h, h % 2))], steps, DEEP)

        @block.scalar
        def _(act):
            c = Links(act, act_chain, 2 * DEEP)
            nc.scalar.preload_act_table_set("natural_log_exp_and_others")
            act.wait_ge(w_in, 16 * 2 * (1 + 2 * SB))
            nc.scalar.activation(wcat[:, 0:D], wcat[:, 0:D], ACT.Copy, scale=-1.0).then_inc(negated, 1)
            nc.scalar.activation(wea[:, :, 0:D], wea[:, :, 0:D], ACT.Copy, scale=-1.0).then_inc(negated, 1)

            def gates(i, h):
                n = DEEP * i + h
                if h == 0:
                    c.step(i)
                act.wait_ge(turned, n + 1)
                nc.scalar.activation(eaT[:, :], ps_t[0:K, SB, :], ACT.Copy)
                nc.scalar.activation(hT[:, 0:BANK, :], ps_t[:, 0:BANK, :], ACT.Copy)
                nc.scalar.activation(hT[:, BANK:SB, :], ps_t[:, BANK:SB, :], ACT.Copy).then_inc(copied, 1)
                act.wait_ge(mixed, n + 1)
                c.link(nc.scalar.activation(small_e[:, :, :], ps_m[:, 0:SB, :], ACT.Abs))
                c.link(nc.scalar.activation(small_e[:, :, :], small_e[:, :, :], ACT.Exp, scale=-1.0))
                nc.scalar.activation(log_e[:, :, :], small_e[:, :, :], ACT.Ln,
                                     bias=ones[:, 0:1]).then_inc(logs_ready, 1)
                act.wait_ge(soft_ready, n + 1)
                nc.scalar.activation(gate[:, :, :], soft[:, :, 0:D], ACT.Exp, scale=-1.0).then_inc(gated, 1)
                sums.scalar_high(act, n, h % 2)
                if h == DEEP - 1:
                    c.done()
            staged(act, [(0, gates)], steps, DEEP)

        @block.vector
        def _(dve):
            for name in ("dve", "link", "place"):
                sums.start(dve, name)

            def soften(i, h):
                n = DEEP * i + h
                dve.wait_ge(logs_ready, n + 1)
                nc.vector.scalar_tensor_tensor(out=soft[:, :, :], in0=ps_m[:, 0:SB, :], scalar=0.0,
                                               in1=log_e[:, :, :], op0=ALU.max, op1=ALU.add)\
                    .then_inc(soft_ready, 1)
                sums.vector_members(dve, n, h)

            def message(i, h):
                n = DEEP * i + h
                dve.wait_ge(gated, n + 1)
                nc.vector.tensor_tensor(sums.msg[:, h % 2, :, :], gate[:, :, :], soft[:, :, D:P],
                                        ALU.mult).then_inc(sums.msg_ready, 1)
            staged(dve, [(0, soften), (0, message), (1, lambda i, h: sums.vector_add(dve, DEEP * i + h)),
                         (0, lambda i, h: sums.vector_split(dve, DEEP * i + h, h % 2))], steps, DEEP)


def norm_nodes(nc, agg, h_tab, eps_col):
    with ExitStack() as ctx:
        ctx.enter_context(nc.cleanup_on_exit())
        p = Pass(nc, ctx, "n2")
        hb = p.sb("hb", [P, 2, GC])
        norm = Norm(p, eps_col)
        h_ready = norm.h_ready
        h_out = [p.sem(f"h_out{h}") for h in range(2)]
        block = ctx.enter_context(nc.Block())

        @block.sync
        def _(sp):
            with sp.Fori(0, GSTEPS) as i:
                for h in range(2):
                    sp.wait_ge(h_ready, 2 * i + h + 1)
                    store_group(sp, h_tab, 2 * i + h, hb[:, h, :]).then_inc(h_out[h], 16)
            for h in range(2):
                sp.wait_ge(h_out[h], 16 * GSTEPS)

        def x_in(n):
            return lambda k: agg[:, bass.ds(n * GC + k * D, D)]

        def to(h):
            return lambda k0, k1: hb[:, h, k0 * D:k1 * D]

        def wait_free(eng, i, h):
            if behind(2 * i + h, 2):
                eng.wait_ge(h_out[h], 16 * i)

        @block.vector
        def _(dve):
            staged(dve, [(0, lambda i, h: norm.vector(dve, 2 * i + h, h, x_in(2 * i + h), to(h),
                                                      lambda: wait_free(dve, i, h)))], GSTEPS)

        @block.scalar
        def _(act):
            def apply(i, h):
                wait_free(act, i, h)
                norm.scalar_apply(act, 2 * i + h, h, x_in(2 * i + h), to(h))
            staged(act, [(0, lambda i, h: norm.scalar_root(act, 2 * i + h, h)), (0, apply)], GSTEPS)


def rel_edges(nc, h_tab, pair_s, W_rel, agg, src_idx, dst_rel, win, win_m, iota_b, ident, odd, even):
    QUADS = RELS // 4
    parts = ((0, BANK), (BANK, SB))
    with ExitStack() as ctx:
        ctx.enter_context(nc.cleanup_on_exit())
        p = Pass(nc, ctx, "e2")
        ring = p.sb("ring", [P, 2, SB, 2 * D])
        idx_small = p.sb("idx", [P, 1, 2, SB], I32)
        pairs = p.sb("pairs", [P, 2, SB * P], I32)
        hT = p.sb("hT", [P, SB * P])
        kept = p.sb("kept", [P, 2, QUADS, SB * P])
        w = p.sb("w", [P, QUADS, 2 * D])
        pair = p.sb("pair", [P, QUADS])
        own = p.sb("own", [P, 2, SB, D])
        ps_t = p.ps("ps_t", [P, 8, P])
        ps_m = p.ps("ps_m", [P, 8, P])
        landed, t_in = ([p.sem(f"{s}{h}") for h in range(2)] for s in ("landed", "t_in"))
        idx_ready, turned, copied, kept_ready, mixed, picked, w_in, pair_ready, doubled = p.sems(
            "idx_ready turned copied kept_ready mixed picked w_in pair_ready doubled")
        sums = Sums(nc, ctx, p.tag, agg, dst_rel, win, win_m, iota_b, parts=True, scalar_members=True)
        block = ctx.enter_context(nc.Block())

        @block.gpsimd
        def _(pool):
            for a in range(2):
                nc.gpsimd.iota(pair[a * D:(a + 1) * D, :], [[2, QUADS]], base=a, channel_multiplier=0,
                               allow_small_or_imprecise_dtypes=True).then_inc(pair_ready, 1)
                pool.wait_ge(pair_ready, a + 1)
            gather_pass(nc, pool, p.tag, [(h_tab, src_idx, 0)], idx_small, lambda h, j, s: ring[:, h, j, 0:D],
                        lambda i, h: pool.wait_ge(turned, 2 * i + h - 1), landed, idx_ready)

        @block.sync
        def _(sp):
            for a in range(2):
                for k in range(QUADS):
                    sp.dma_start(w[a * D:(a + 1) * D, k, :].rearrange("i (b o) -> i b o", b=2),
                                 W_rel[4 * k + 2 * a:4 * k + 2 * a + 2, :, :].rearrange("b i o -> i b o"))\
                        .then_inc(w_in, 16)

            def body(i, first):
                for h in range(2):
                    n = 2 * i + h
                    if not first:
                        sp.wait_ge(kept_ready, 2 * (n - 1))
                    sp.dma_start(pairs[:, h, :],
                                 pair_s[0:1, bass.ds(n * SB * P, SB * P)].to_broadcast([P, SB * P]))\
                        .then_inc(t_in[h], 16)
            peel_first(sp, STEPS, body)

        @block.tensor
        def _(pe):
            sums.start(pe, "pe")
            pe.wait_ge(w_in, 16 * 2 * QUADS)

            def turn(i, h):
                n = 2 * i + h
                pe.wait_ge(landed[h], 16 * SB * (i + 1))
                pe.wait_ge(doubled, n + 1)
                if behind(n, 1):
                    pe.wait_ge(copied, n)
                for j in range(SB):
                    last = nc.tensor.transpose(ps_t[:, j, :], ring[:, h, j, :], ident[:, :])
                last.then_inc(turned, 1)

            def mix(i, h):
                n = 2 * i + h
                if behind(n, 1):
                    pe.wait_ge(picked, 2 * n)
                for q, (t0, t1) in enumerate(parts):
                    pe.wait_ge(kept_ready, 2 * n + q + 1)
                    for j in range(t0, t1):
                        for k in range(QUADS):
                            last = nc.tensor.matmul(ps_m[:, j, :], lhsT=kept[:, h, k, j * P:(j + 1) * P],
                                                    rhs=w[:, k, :], start=(k == 0), stop=(k == QUADS - 1))
                last.then_inc(mixed, 1)
            staged(pe, [(0, turn), (1, mix), (2, lambda i, h: sums.tensor_sum_parts(pe, 2 * i + h, h))])

        @block.scalar
        def _(act):
            def copy(i, h):
                n = 2 * i + h
                act.wait_ge(landed[h], 16 * SB * (i + 1))
                nc.scalar.activation(ring[:, h, :, D:2 * D], ring[:, h, :, 0:D], ACT.Copy).then_inc(doubled, 1)
                act.wait_ge(turned, n + 1)
                if behind(n, 1):
                    act.wait_ge(kept_ready, 2 * n)
                nc.scalar.activation(hT[:, 0:BANK * P], ps_t[:, 0:BANK, :].rearrange("p q n -> p (q n)"), ACT.Copy)
                nc.scalar.activation(hT[:, BANK * P:SB * P],
                                     ps_t[:, BANK:SB, :].rearrange("p q n -> p (q n)"),
                                     ACT.Copy).then_inc(copied, 1)
            staged(act, [(0, copy), (1, lambda i, h: sums.scalar_members(act, 2 * i + h, h)),
                         (1, lambda i, h: sums.scalar_high(act, 2 * i + h, h))])

        @block.vector
        def _(dve):
            for name in ("dve", "link", "place"):
                sums.start(dve, name)
            dve.wait_ge(pair_ready, 2)

            def keep(i, h):
                n = 2 * i + h
                dve.wait_ge(t_in[h], 16 * (i + 1))
                dve.wait_ge(copied, n + 1)
                if behind(n, 2):
                    dve.wait_ge(mixed, n - 1)
                for t0, t1 in parts:
                    at = slice(t0 * P, t1 * P)
                    for k in range(QUADS):
                        last = nc.vector.scalar_tensor_tensor(
                            out=kept[:, h, k, at], in0=pairs[:, h, at], scalar=pair[:, k:k + 1],
                            in1=hT[:, at], op0=ALU.is_equal, op1=ALU.mult)
                    last.then_inc(kept_ready, 1)

            def message(i, h):
                n = 2 * i + h
                dve.wait_ge(mixed, n + 1)
                for b, mask in enumerate((even, odd)):
                    nc.vector.tensor_tensor(own[:, b, :, :], ps_m[:, 0:SB, b * D:(b + 1) * D],
                                            mask[:, bass.ds(n * SB, SB)].unsqueeze(2).to_broadcast([P, SB, D]),
                                            ALU.mult).then_inc(picked, 1)
                dve.wait_ge(picked, 2 * n + 2)
                nc.vector.tensor_tensor(sums.msg[:, h, :, :], own[:, 0, :, :], own[:, 1, :, :],
                                        ALU.add).then_inc(sums.msg_ready, 1)
            staged(dve, [(0, keep), (1, message), (2, lambda i, h: sums.vector_add(dve, 2 * i + h)),
                         (1, lambda i, h: sums.vector_split(dve, 2 * i + h, h))])


def gcn_start(nc, agg, deg, root, dinv, h_tab, xh_tab, eps_col):
    with ExitStack() as ctx:
        ctx.enter_context(nc.cleanup_on_exit())
        p = Pass(nc, ctx, "n3")
        hb = p.sb("hb", [P, 2, GC])
        norm = Norm(p, eps_col)
        h_ready = norm.h_ready
        scaled, dinv_ready, deg_root = p.sems("scaled dinv_ready deg_root")
        x_out, u_out = ([p.sem(f"{s}{h}") for h in range(2)] for s in ("x_out", "u_out"))
        block = ctx.enter_context(nc.Block())

        @block.sync
        def _(sp):
            with sp.Fori(0, GSTEPS) as i:
                for h in range(2):
                    n = 2 * i + h
                    store_group(sp, xh_tab, n, group(agg, n)).then_inc(x_out[h], 16)
                for h in range(2):
                    n = 2 * i + h
                    sp.wait_ge(scaled, n + 1)
                    store_group(sp, h_tab, n, group(agg, n)).then_inc(u_out[h], 16)
            for h in range(2):
                for s in (x_out, u_out):
                    sp.wait_ge(s[h], 16 * GSTEPS)

        def x_in(n):
            return lambda k: agg[:, bass.ds(n * GC + k * D, D)]

        def to(h):
            return lambda k0, k1: hb[:, h, k0 * D:k1 * D]

        def wait_free(eng, i, h):
            if behind(2 * i + h, 2):
                eng.wait_ge(scaled, 2 * i + h - 1)

        @block.vector
        def _(dve):
            dve.wait_ge(deg_root, 1)
            nc.vector.reciprocal(dinv[:, :], root[:, :]).then_inc(dinv_ready, 1)
            staged(dve, [(0, lambda i, h: norm.vector(dve, 2 * i + h, h, x_in(2 * i + h), to(h),
                                                      lambda: wait_free(dve, i, h)))], GSTEPS)

        @block.scalar
        def _(act):
            nc.scalar.activation(root[:, :], deg[:, :], ACT.Sqrt, bias=1.0).then_inc(deg_root, 1)

            def apply(i, h):
                wait_free(act, i, h)
                norm.scalar_apply(act, 2 * i + h, h, x_in(2 * i + h), to(h))
            staged(act, [(0, lambda i, h: norm.scalar_root(act, 2 * i + h, h)), (0, apply)], GSTEPS)

        @block.gpsimd
        def _(pool):
            pool.wait_ge(dinv_ready, 1)

            def body(i, first):
                for h in range(2):
                    n = 2 * i + h
                    pool.wait_ge(h_ready, n + 1)
                    pool.wait_ge(x_out[h], 16 * (i + 1))
                    nc.gpsimd.tensor_tensor(rows_of(group(agg, n)), rows_of(hb[:, h, :]), per_row(dinv, n),
                                            ALU.mult).then_inc(scaled, 1)
            peel_first(pool, GSTEPS, body)


def per_row(dinv, n):
    return dinv[:, bass.ds(n * GB, GB)].unsqueeze(2).to_broadcast([P, GB, D])


def gcn_nodes(nc, layer, agg, root, dinv, h_tab, xh_tab, W_gcn, b_gcn, ident, ones, out, end=False):
    steps = GSTEPS // 2
    parts = ((0, BANK), (BANK, GB // 2))
    with ExitStack() as ctx:
        ctx.enter_context(nc.cleanup_on_exit())
        p = Pass(nc, ctx, "n5" if end else "n4")
        v = p.sb("v", [P, GC])
        vT = p.sb("vT", [P, 2, GB // 2, P])
        w = p.sb("w", [P, 2, P])
        brow = p.sb("brow", [3, 2, P])
        bpart = p.sb("bpart", [3, 3, 2, P], BF16)
        brest = p.sb("brest", [3, 3, 2, P])
        bias = p.sb("bias", [3, 2, P], BF16)
        ones3 = p.sb("ones3", [3, P], BF16)
        ex = p.sb("ex", [P, GB, D])
        ax = p.sb("ax", [P, GB, D])
        zi = p.sb("zi", [P, DEEP, GC])
        zo = p.sb("zo", [P, 2, GC])
        xi = p.sb("xi", [P, DEEP, GC])
        ps_t = p.ps("ps_t", [P, 8, P])
        ps_g = p.ps("ps_g", [P, 16, P])
        zeroed, w_in, v_ready, turned, copied, mixed, gate_ready, taken, z_ready, scaled, bias_chain, z_back = p.sems(
            "zeroed w_in v_ready turned copied mixed gate_ready taken z_ready scaled bias_chain z_back")
        z_in, x_in, z_out, u_out = ([p.sem(f"{s}{h}") for h in range(DEEP)] for s in ("z_in", "x_in", "z_out", "u_out"))
        block = ctx.enter_context(nc.Block())

        @block.sync
        def _(sp):
            sp.wait_ge(zeroed, 1)
            for a in range(2):
                sp.dma_start(w[a * D:(a + 1) * D, a, :],
                             W_gcn[bass.ds(layer, 1), :, :].rearrange("o k f -> (o k) f")).then_inc(w_in, 16)
                sp.dma_start(brow[:, a, :], b_gcn[bass.ds(layer, 1), :].to_broadcast([3, P])).then_inc(w_in, 16)

            def load(i, h):
                n = DEEP * i + h
                sp.dma_start(rows_of(zi[:, h, :]), tiles_of(h_tab, n * GB, GB)).then_inc(z_in[h], 16)
                if end:
                    sp.dma_start(rows_of(xi[:, h, :]), tiles_of(xh_tab, n * GB, GB)).then_inc(x_in[h], 16)

            def store(i, h):
                n = DEEP * i + h
                sp.wait_ge(scaled, n + 1)
                if not end:
                    store_group(sp, h_tab, n, group(agg, n)).then_inc(u_out[h], 16)
                elif isinstance(n, int) and n == 2 * GSTEPS - 1:
                    left = FULL - n * GB
                    rows = rows_of(zo[:, h % 2, :])
                    sp.dma_start(tiles_of(out, n * GB, left), rows[:, 0:left, :]).then_inc(z_out[h], 16)
                    sp.dma_start(out[FULL * P:N, :], rows[0:REST, left, :]).then_inc(u_out[h], 16)
                else:
                    store_group(sp, out, n, zo[:, h % 2, :]).then_inc(z_out[h], 16)
            load_store(sp, steps, load, store, DEEP)
            for h in range(DEEP):
                sp.wait_ge((z_out if end else u_out)[h], 16 * steps)
            if end:
                sp.wait_ge(u_out[DEEP - 1], 16)

        @block.vector
        def _(dve):
            def scale(i, h):
                n = DEEP * i + h
                if behind(n, 1):
                    dve.wait_ge(turned, n)
                nc.vector.tensor_tensor(rows_of(v[:, :]), rows_of(group(agg, n)), per_row(dinv, n),
                                        ALU.mult).then_inc(v_ready, 1)

            def state(i, h):
                n = DEEP * i + h
                if behind(n, 1):
                    dve.wait_ge(z_ready, n)
                for q, (q0, q1) in enumerate(parts):
                    dve.wait_ge(gate_ready, 2 * n + q + 1)
                    at = slice(2 * q0, 2 * q1)
                    nc.vector.tensor_tensor(ax[:, at, :], ps_g[:, at, 0:D], ex[:, at, :],
                                            ALU.mult).then_inc(taken, 1)
                dve.wait_ge(taken, 2 * n + 2)
                dve.wait_ge(z_back, n + 1)
                if behind(n, 2):
                    if end:
                        dve.wait_ge(z_out[(h + 2) % DEEP], 16 * (i + (h - 2) // DEEP + 1))
                    dve.wait_ge(scaled, n - 1)
                nc.vector.tensor_tensor(rows_of(zo[:, h % 2, :]), ax[:, :, :], rows_of(zi[:, h, :]),
                                        ALU.add).then_inc(z_ready, 1)

            nc.vector.memset(ones3[:, :], 1.0)
            c = Links(dve, bias_chain, 8)
            c.step(0)
            dve.wait_ge(w_in, 64)
            c.link(nc.vector.tensor_copy(bpart[:, 0, :, :], brow[:, :, :]))
            c.link(nc.vector.tensor_tensor(brest[:, 0, :, :], brow[:, :, :], bpart[:, 0, :, :], ALU.subtract))
            c.link(nc.vector.tensor_copy(bpart[:, 1, :, :], brest[:, 0, :, :]))
            c.link(nc.vector.tensor_tensor(bpart[:, 2, :, :], brest[:, 0, :, :], bpart[:, 1, :, :], ALU.subtract))
            c.link(nc.vector.tensor_scalar(brest[:, 1, :, :], bpart[:, 0, :, :], ident[0:3, 0:1], None, ALU.mult))
            c.link(nc.vector.scalar_tensor_tensor(out=brest[:, 2, :, :], in0=bpart[:, 1, :, :],
                                                  scalar=ident[0:3, 1:2], in1=brest[:, 1, :, :],
                                                  op0=ALU.mult, op1=ALU.add))
            c.link(nc.vector.scalar_tensor_tensor(out=bias[:, :, :], in0=bpart[:, 2, :, :],
                                                  scalar=ident[0:3, 2:3], in1=brest[:, 2, :, :],
                                                  op0=ALU.mult, op1=ALU.add))
            staged(dve, [(0, scale), (2, state)], steps, DEEP)

        @block.tensor
        def _(pe):
            def turn(i, h):
                n = DEEP * i + h
                pe.wait_ge(v_ready, n + 1)
                if behind(n, 1):
                    pe.wait_ge(copied, n)
                for q in range(GB // 2):
                    last = nc.tensor.transpose(ps_t[:, q, :], v[:, q * P:(q + 1) * P], ident[:, :])
                last.then_inc(turned, 1)

            def mix(i, h):
                n = DEEP * i + h
                pe.wait_ge(copied, n + 1)
                if not behind(n, 1):
                    pe.wait_ge(bias_chain, 7)
                for part, (q0, q1) in enumerate(parts):
                    if behind(n, 1):
                        pe.wait_ge(taken, 2 * n + part - 1)
                    for q in range(q0, q1):
                        to = ps_g[:, 2 * q:2 * q + 2, :]
                        nc.tensor.matmul(to, lhsT=vT[:, h % 2, q, :], rhs=w[:, :, :], start=True, stop=False)
                        last = nc.tensor.matmul(to, lhsT=ones3[:, :], rhs=bias[:, :, :], start=False, stop=True)
                    last.then_inc(mixed, 1)
            pe.wait_ge(w_in, 64)
            staged(pe, [(0, turn), (1, mix)], steps, DEEP)

        @block.scalar
        def _(act):
            def copy(i, h):
                n = DEEP * i + h
                act.wait_ge(turned, n + 1)
                if behind(n, 2):
                    act.wait_ge(mixed, 2 * n - 2)
                nc.scalar.activation(vT[:, h % 2, 0:BANK, :], ps_t[:, 0:BANK, :], ACT.Copy)
                nc.scalar.activation(vT[:, h % 2, BANK:GB // 2, :], ps_t[:, BANK:GB // 2, :],
                                     ACT.Copy).then_inc(copied, 1)

            def gates(i, h):
                n = DEEP * i + h
                for q, (q0, q1) in enumerate(parts):
                    act.wait_ge(mixed, 2 * n + q + 1)
                    if behind(n, 1):
                        act.wait_ge(taken, 2 * n + q - 1)
                    at = slice(2 * q0, 2 * q1)
                    nc.scalar.activation(ex[:, at, :], ps_g[:, at, D:P], ACT.Sigmoid).then_inc(gate_ready, 1)
            staged(act, [(0, copy), (1, gates)], steps, DEEP)

        @block.gpsimd
        def _(pool):
            nc.gpsimd.memset(w[:, :, :], 0.0).then_inc(zeroed, 1)

            def back(i, h):
                pool.wait_ge(z_in[h], 16 * (i + 1))
                nc.gpsimd.tensor_tensor(rows_of(zi[:, h, :]), rows_of(zi[:, h, :]), per_row(root, DEEP * i + h),
                                        ALU.mult).then_inc(z_back, 1)

            def finish(i, h):
                n = DEEP * i + h
                pool.wait_ge(z_ready, n + 1)
                if end:
                    pool.wait_ge(x_in[h], 16 * (i + 1))
                    nc.gpsimd.tensor_tensor(zo[:, h % 2, :], zo[:, h % 2, :], xi[:, h, :], ALU.add).then_inc(scaled, 1)
                else:
                    nc.gpsimd.tensor_tensor(rows_of(group(agg, n)), rows_of(zo[:, h % 2, :]), per_row(dinv, n),
                                            ALU.mult).then_inc(scaled, 1)
            staged(pool, [(1, finish), (0, back)], steps, DEEP)


_INS = ["x", "src", "dst", "edge_attr_10", "edge_attr_32", "edge_type_16", "L0_gnn_W_edge", "L0_gnn_b_edge",
        "L0_gnn_W1", "L0_gnn_b1", "L0_gnn_gamma", "L0_gnn_beta", "L0_gnn_W2", "L0_gnn_b2", "L1_gnn_Wf",
        "L1_gnn_bf", "L1_gnn_Ws", "L1_gnn_bs", "L2_gnn_weight", "L3_gnn_Ws", "L3_gnn_bs"]


def kernel(**inputs):
    import numpy as _np
    import concourse.bacc as _bacc
    from concourse import mybir as _mybir
    from concourse.bass_utils import run_bass_kernel_spmd as _run

    nc = _bacc.Bacc("TRN2", target_bir_lowering=False, num_devices=1)
    arrays, args = {}, []
    for name in _INS:
        a = _np.ascontiguousarray(inputs[name])
        arrays[f"in_{name}"] = a
        args.append(nc.dram_tensor(f"in_{name}", a.shape, _mybir.dt.from_np(a.dtype),
                                   kind="ExternalInput").ap())
    out = nc.dram_tensor("out", (N, D), F32, kind="ExternalOutput").ap()
    build(nc, *args, out)
    r = _run(nc, [arrays], core_ids=[0])
    return r.results[0]["out"]
```
